# Optimizing a Trainium2 kernel written in Bass

```python
import numpy as np
import jax
import jax.numpy as jnp

def _softmax(x, axis=-1):
    return jax.nn.softmax(x, axis=axis)

def _gelu(x):
    return jax.nn.gelu(x, approximate=True)

def _silu(x):
    return jax.nn.silu(x)

def _sigmoid(x):
    return jax.nn.sigmoid(x)

def _layernorm(x, axis=-1, eps=1e-05):
    m = jnp.mean(x, axis=axis, keepdims=True)
    v = jnp.var(x, axis=axis, keepdims=True)
    return (x - m) / jnp.sqrt(v + eps)

def _scatter_add(tgt, idx, src, axis=0):
    return tgt.at[idx].add(src)

def _segment_sum(src, seg, n):
    return jax.ops.segment_sum(src, seg, n)
kernel_name = 'mk_macaron_d2_jaxref_r8_732c5c'

def setup_inputs(seed: int=0):
    np.random.seed(seed)
    _w = jnp.asarray

    def _L0_attn_setup():
        import jax, jax.numpy as jnp
        import numpy as np
        B, L, E, H = (4, 128, 128, 16)
        D = E // H
        SPARSITY = 0.4
        NEG_INF = jnp.float32(-1e+30)
        key = jax.random.key(seed)
        ks = jax.random.split(key, 8)
        s = 0.02
        return {'hidden_states': jax.random.normal(ks[0], (B, L, E), jnp.float32), 'qkv_w': jax.random.normal(ks[1], (3 * E, E), jnp.float32) * s, 'qkv_b': jax.random.normal(ks[2], (3 * E,), jnp.float32) * s, 'r_w1': jax.random.normal(ks[3], (E // 4, E), jnp.float32) * s, 'r_b1': jax.random.normal(ks[4], (E // 4,), jnp.float32) * s, 'r_w2': jax.random.normal(ks[5], (H, E // 4), jnp.float32) * s, 'r_b2': jax.random.normal(ks[6], (H,), jnp.float32) * s}
    _L0_attn_in = _L0_attn_setup()

    def _L0_ffn_setup():
        import jax, jax.numpy as jnp
        import numpy as np
        key = jax.random.key(seed)
        k1, k2, k3, k4, k5 = jax.random.split(key, 5)
        d_in, d_out, r = (128, 128, 32)
        x = jax.random.normal(k1, (8, 1024, d_in), dtype=jnp.float32)
        W = jax.random.normal(k2, (d_out, d_in), dtype=jnp.float32) * (1.0 / np.sqrt(d_in))
        b = jax.random.normal(k3, (d_out,), dtype=jnp.float32) * 0.01
        V_r = jax.random.normal(k4, (d_in, r), dtype=jnp.float32) * (1.0 / np.sqrt(d_in))
        C = jax.random.normal(k5, (d_out, r), dtype=jnp.float32) * (1.0 / np.sqrt(r))
        return {'x': x, 'W': W, 'b': b, 'V_r': V_r, 'C': C}
    _L0_ffn_in = _L0_ffn_setup()

    def _L1_attn_setup():
        import jax, jax.numpy as jnp
        import numpy as np
        DIM = 128
        HEADS = 16
        HEAD_DIM = DIM // HEADS
        RANK = 16
        LORA_ALPHA = 1
        SCALING = LORA_ALPHA / RANK
        SCALE = HEAD_DIM ** (-0.5)
        B, N = (8, 128)

        def _lora_linear(x, W, A, Blo, bias=None):
            y = x @ W.T + x @ A.T @ Blo.T * SCALING
            if bias is not None:
                y = y + bias
            return y

        def _split_heads(t, b, n):
            return t.reshape(b, n, HEADS, HEAD_DIM).transpose(0, 2, 1, 3)
        key = jax.random.key(seed)
        ks = jax.random.split(key, 15)
        s = 1.0 / np.sqrt(DIM)
        inp = {'x': jax.random.normal(ks[0], (B, N, DIM), jnp.float32), 'Wq': jax.random.normal(ks[1], (DIM, DIM), jnp.float32) * s, 'Wk': jax.random.normal(ks[2], (DIM, DIM), jnp.float32) * s, 'Wv': jax.random.normal(ks[3], (DIM, DIM), jnp.float32) * s, 'Wo': jax.random.normal(ks[4], (DIM, DIM), jnp.float32) * s, 'bo': jnp.zeros((DIM,), jnp.float32), 'Aq': jax.random.normal(ks[5], (RANK, DIM), jnp.float32) * s, 'Bq': jax.random.normal(ks[6], (DIM, RANK), jnp.float32) * s, 'Ak': jax.random.normal(ks[7], (RANK, DIM), jnp.float32) * s, 'Bk': jax.random.normal(ks[8], (DIM, RANK), jnp.float32) * s, 'Av': jax.random.normal(ks[9], (RANK, DIM), jnp.float32) * s, 'Bv': jax.random.normal(ks[10], (DIM, RANK), jnp.float32) * s, 'Ao': jax.random.normal(ks[11], (RANK, DIM), jnp.float32) * s, 'Bo': jax.random.normal(ks[12], (DIM, RANK), jnp.float32) * s}
        return inp
    _L1_attn_in = _L1_attn_setup()

    def _L1_ffn_setup():
        import jax, jax.numpy as jnp
        import numpy as np
        H, I, E, K = (128, 64, 32, 8)
        B, S = (4, 128)

        def silu(x):
            return x * jax.nn.sigmoid(x)
        key = jax.random.key(seed)
        ks = jax.random.split(key, 14)

        def w(k, shape, fan_in):
            return jax.random.normal(k, shape, jnp.float32) / np.float32(np.sqrt(fan_in))
        return {'hidden_states': jax.random.normal(ks[0], (B, S, H), jnp.float32), 'Wr': w(ks[1], (H, E), H), 'br': jnp.zeros((E,), jnp.float32), 'Wg_s': w(ks[2], (H, I), H), 'bg_s': jnp.zeros((I,), jnp.float32), 'Wu_s': w(ks[3], (H, I), H), 'bu_s': jnp.zeros((I,), jnp.float32), 'Wd_s': w(ks[4], (I, H), I), 'bd_s': jnp.zeros((H,), jnp.float32), 'Wg': w(ks[5], (E, H, I), H), 'bg': jnp.zeros((E, I), jnp.float32), 'Wu': w(ks[6], (E, H, I), H), 'bu': jnp.zeros((E, I), jnp.float32), 'Wd': w(ks[7], (E, I, H), I), 'bd': jnp.zeros((E, H), jnp.float32)}
    _L1_ffn_in = _L1_ffn_setup()
    _d = {'L0_attn_hidden_states': _L0_attn_in['hidden_states'], 'L0_attn_qkv_w': _L0_attn_in['qkv_w'], 'L0_attn_qkv_b': _L0_attn_in['qkv_b'], 'L0_attn_r_w1': _L0_attn_in['r_w1'], 'L0_attn_r_b1': _L0_attn_in['r_b1'], 'L0_attn_r_w2': _L0_attn_in['r_w2'], 'L0_attn_r_b2': _L0_attn_in['r_b2'], 'L0_ffn_W': _L0_ffn_in['W'], 'L0_ffn_b': _L0_ffn_in['b'], 'L0_ffn_V_r': _L0_ffn_in['V_r'], 'L0_ffn_C': _L0_ffn_in['C'], 'L1_attn_Wq': _L1_attn_in['Wq'], 'L1_attn_Wk': _L1_attn_in['Wk'], 'L1_attn_Wv': _L1_attn_in['Wv'], 'L1_attn_Wo': _L1_attn_in['Wo'], 'L1_attn_bo': _L1_attn_in['bo'], 'L1_attn_Aq': _L1_attn_in['Aq'], 'L1_attn_Bq': _L1_attn_in['Bq'], 'L1_attn_Ak': _L1_attn_in['Ak'], 'L1_attn_Bk': _L1_attn_in['Bk'], 'L1_attn_Av': _L1_attn_in['Av'], 'L1_attn_Bv': _L1_attn_in['Bv'], 'L1_attn_Ao': _L1_attn_in['Ao'], 'L1_attn_Bo': _L1_attn_in['Bo'], 'L1_ffn_Wr': _L1_ffn_in['Wr'], 'L1_ffn_br': _L1_ffn_in['br'], 'L1_ffn_Wg_s': _L1_ffn_in['Wg_s'], 'L1_ffn_bg_s': _L1_ffn_in['bg_s'], 'L1_ffn_Wu_s': _L1_ffn_in['Wu_s'], 'L1_ffn_bu_s': _L1_ffn_in['bu_s'], 'L1_ffn_Wd_s': _L1_ffn_in['Wd_s'], 'L1_ffn_bd_s': _L1_ffn_in['bd_s'], 'L1_ffn_Wg': _L1_ffn_in['Wg'], 'L1_ffn_bg': _L1_ffn_in['bg'], 'L1_ffn_Wu': _L1_ffn_in['Wu'], 'L1_ffn_bu': _L1_ffn_in['bu'], 'L1_ffn_Wd': _L1_ffn_in['Wd'], 'L1_ffn_bd': _L1_ffn_in['bd']}
    _x0 = _d['L0_attn_hidden_states']
    _d['L0_attn_hidden_states'] = jax.random.normal(jax.random.fold_in(jax.random.key(seed), 1), (16, 256, 128), dtype=_x0.dtype)
    del _x0
    return _d

def reference(L0_attn_hidden_states, L0_attn_qkv_w, L0_attn_qkv_b, L0_attn_r_w1, L0_attn_r_b1, L0_attn_r_w2, L0_attn_r_b2, L0_ffn_W, L0_ffn_b, L0_ffn_V_r, L0_ffn_C, L1_attn_Wq, L1_attn_Wk, L1_attn_Wv, L1_attn_Wo, L1_attn_bo, L1_attn_Aq, L1_attn_Bq, L1_attn_Ak, L1_attn_Bk, L1_attn_Av, L1_attn_Bv, L1_attn_Ao, L1_attn_Bo, L1_ffn_Wr, L1_ffn_br, L1_ffn_Wg_s, L1_ffn_bg_s, L1_ffn_Wu_s, L1_ffn_bu_s, L1_ffn_Wd_s, L1_ffn_bd_s, L1_ffn_Wg, L1_ffn_bg, L1_ffn_Wu, L1_ffn_bu, L1_ffn_Wd, L1_ffn_bd):

    def _L0_attn_ref(hidden_states, qkv_w, qkv_b, r_w1, r_b1, r_w2, r_b2):
        import jax, jax.numpy as jnp
        import numpy as np
        B, L, E, H = (4, 128, 128, 16)
        D = E // H
        SPARSITY = 0.4
        NEG_INF = jnp.float32(-1e+30)
        bsz, tgt_len, embed_dim = hidden_states.shape
        qkv = (hidden_states @ qkv_w.T + qkv_b).reshape(bsz, tgt_len, 3, H, D)
        qkv = jnp.transpose(qkv, (2, 0, 3, 1, 4))
        q, k, v = (qkv[0], qkv[1], qkv[2])
        h1 = jax.nn.relu(hidden_states @ r_w1.T + r_b1)
        routing_logits = jax.nn.sigmoid(h1 @ r_w2.T + r_b2)
        routing_scores = jax.nn.sigmoid(routing_logits)
        attn = jnp.einsum('bhqd,bhkd->bhqk', q, k) / jnp.sqrt(jnp.float32(D))
        k_keep = max(1, int(tgt_len * SPARSITY))
        rs_t = jnp.transpose(routing_scores, (0, 2, 1))
        _, top_idx = jax.lax.top_k(rs_t, k_keep)
        keep = jnp.zeros((bsz, H, tgt_len), dtype=bool)
        keep = keep.at[jnp.arange(bsz)[:, None, None], jnp.arange(H)[None, :, None], top_idx].set(True)
        sparse = jnp.where(keep[:, :, None, :], attn, NEG_INF)
        w = jax.nn.softmax(sparse.astype(jnp.float32), axis=-1).astype(q.dtype)
        out = jnp.einsum('bhqk,bhkd->bhqd', w, v)
        out = jnp.transpose(out, (0, 2, 1, 3)).reshape(bsz, tgt_len, embed_dim)
        return out

    def _L0_ffn_ref(x, W, b, V_r, C):
        import jax, jax.numpy as jnp
        import numpy as np
        base = jnp.einsum('bsd,od->bso', x, W) + b
        correction = jnp.einsum('bsr,or->bso', jnp.einsum('bsd,dr->bsr', x, V_r), C)
        return base + correction

    def _L1_attn_ref(x, Wq, Wk, Wv, Wo, bo, Aq, Bq, Ak, Bk, Av, Bv, Ao, Bo):
        import jax, jax.numpy as jnp
        import numpy as np
        DIM = 128
        HEADS = 16
        HEAD_DIM = DIM // HEADS
        RANK = 16
        LORA_ALPHA = 1
        SCALING = LORA_ALPHA / RANK
        SCALE = HEAD_DIM ** (-0.5)
        B, N = (8, 128)

        def _lora_linear(x, W, A, Blo, bias=None):
            y = x @ W.T + x @ A.T @ Blo.T * SCALING
            if bias is not None:
                y = y + bias
            return y

        def _split_heads(t, b, n):
            return t.reshape(b, n, HEADS, HEAD_DIM).transpose(0, 2, 1, 3)
        b, n, c = x.shape
        q = _split_heads(_lora_linear(x, Wq, Aq, Bq), b, n)
        k = _split_heads(_lora_linear(x, Wk, Ak, Bk), b, n)
        v = _split_heads(_lora_linear(x, Wv, Av, Bv), b, n)
        attn = jnp.einsum('bhnd,bhmd->bhnm', q, k) * SCALE
        attn = jax.nn.softmax(attn, axis=-1)
        out = jnp.einsum('bhnm,bhmd->bhnd', attn, v)
        out = out.transpose(0, 2, 1, 3).reshape(b, n, c)
        return _lora_linear(out, Wo, Ao, Bo, bias=bo)

    def _L1_ffn_ref(hidden_states, Wr, br, Wg_s, bg_s, Wu_s, bu_s, Wd_s, bd_s, Wg, bg, Wu, bu, Wd, bd):
        import jax, jax.numpy as jnp
        import numpy as np
        H, I, E, K = (128, 64, 32, 8)
        B, S = (4, 128)

        def silu(x):
            return x * jax.nn.sigmoid(x)
        b, s, h = hidden_states.shape
        T = b * s
        x = hidden_states.reshape(T, h)
        logits = jnp.dot(x.astype(jnp.float32), Wr) + br
        aff = jax.nn.sigmoid(logits)
        top_v, top_i = jax.lax.top_k(aff, K)
        top_w = top_v / (jnp.sum(top_v, axis=-1, keepdims=True) + 1e-09)
        top_w = top_w.astype(hidden_states.dtype)
        e_total = Wr.shape[1]
        w_full = jnp.zeros((T, e_total), hidden_states.dtype)
        w_full = w_full.at[jnp.arange(T)[:, None], top_i].set(top_w)
        shared = jnp.dot(silu(jnp.dot(x, Wg_s) + bg_s) * (jnp.dot(x, Wu_s) + bu_s), Wd_s) + bd_s
        gate = silu(jnp.einsum('th,ehi->eti', x, Wg) + bg[:, None, :])
        up = jnp.einsum('th,ehi->eti', x, Wu) + bu[:, None, :]
        down = jnp.einsum('eti,eih->eth', gate * up, Wd) + bd[:, None, :]
        routed = jnp.einsum('te,eth->th', w_full, down)
        return (shared + routed).reshape(b, s, h)
    x = L0_attn_hidden_states
    x = x + 0.5 * _L0_ffn_ref(_layernorm(x, axis=-1), L0_ffn_W, L0_ffn_b, L0_ffn_V_r, L0_ffn_C)
    x = x + _L0_attn_ref(_layernorm(x, axis=-1), L0_attn_qkv_w, L0_attn_qkv_b, L0_attn_r_w1, L0_attn_r_b1, L0_attn_r_w2, L0_attn_r_b2)
    x = x + 0.5 * _L0_ffn_ref(_layernorm(x, axis=-1), L0_ffn_W, L0_ffn_b, L0_ffn_V_r, L0_ffn_C)
    x = x + 0.5 * _L1_ffn_ref(_layernorm(x, axis=-1), L1_ffn_Wr, L1_ffn_br, L1_ffn_Wg_s, L1_ffn_bg_s, L1_ffn_Wu_s, L1_ffn_bu_s, L1_ffn_Wd_s, L1_ffn_bd_s, L1_ffn_Wg, L1_ffn_bg, L1_ffn_Wu, L1_ffn_bu, L1_ffn_Wd, L1_ffn_bd)
    x = x + _L1_attn_ref(_layernorm(x, axis=-1), L1_attn_Wq, L1_attn_Wk, L1_attn_Wv, L1_attn_Wo, L1_attn_bo, L1_attn_Aq, L1_attn_Bq, L1_attn_Ak, L1_attn_Bk, L1_attn_Av, L1_attn_Bv, L1_attn_Ao, L1_attn_Bo)
    x = x + 0.5 * _L1_ffn_ref(_layernorm(x, axis=-1), L1_ffn_Wr, L1_ffn_br, L1_ffn_Wg_s, L1_ffn_bg_s, L1_ffn_Wu_s, L1_ffn_bu_s, L1_ffn_Wd_s, L1_ffn_bd_s, L1_ffn_Wg, L1_ffn_bg, L1_ffn_Wu, L1_ffn_bu, L1_ffn_Wd, L1_ffn_bd)
    return x

_drawn_inputs = setup_inputs


def setup_inputs(seed=0):
    import zlib

    import numpy as np

    out = dict(_drawn_inputs(seed))
    spreads = {'L1_attn_bo': (0.0, 0.1),
     'L1_ffn_br': (0.0, 0.318),
     'L1_ffn_bg_s': (0.0, 0.1),
     'L1_ffn_bu_s': (0.0, 0.1),
     'L1_ffn_bd_s': (0.0, 0.1),
     'L1_ffn_bg': (0.0, 0.615),
     'L1_ffn_bu': (0.0, 0.641),
     'L1_ffn_bd': (0.0, 0.379)}
    factors = {'L0_attn_r_b1': 8.0,
     'L0_attn_r_b2': 8.0,
     'L0_ffn_b': 5.686,
     'L1_attn_Aq': 8.0,
     'L1_attn_Bq': 8.0,
     'L1_attn_Ak': 8.0,
     'L1_attn_Bk': 8.0,
     'L1_attn_Av': 8.0,
     'L1_attn_Bv': 8.0,
     'L1_attn_Ao': 8.0,
     'L1_attn_Bo': 8.0}
    for name, (base, spread) in spreads.items():
        noise = np.random.default_rng([zlib.crc32(name.encode()), seed]).standard_normal(out[name].shape)
        drawn = base * np.exp(spread * noise) if base else spread * noise
        out[name] = jnp.asarray(drawn.astype(out[name].dtype))
    for name, factor in factors.items():
        out[name] = (out[name] * factor).astype(out[name].dtype)
    return out
```

```python
import concourse.bass as bass
from concourse import mybir
from contextlib import ExitStack

F32 = mybir.dt.float32
F16 = mybir.dt.float16
ALU = mybir.AluOpType
ACT = mybir.ActivationFunctionType
AX = mybir.AxisListType

P = 128
BATCH, SEQ, DIM = 16, 256, 128
TILES = BATCH * SEQ // P
TPB = SEQ // P
HEADS, HD = 16, 8
LANES = 4
GROUPS = HEADS // LANES
KEEP = int(SEQ * 0.4)
RRANK = 32
LORA = 16
EXPERTS, TOPK, INTER = 32, 8, 64
PAIRS = EXPERTS // 2
EPS = 1e-5
NEG = -3.0e38
MASKED = 60000.0
SCORE_SCALE = HD ** -0.5
WS = 32.0
ROW_MASK, ROW_MAX = 24, 25
UNITS = PAIRS + 1
TPS = 4
WIDE = TPS * P
SUPERS = TILES // TPS
RING = 4
LAG = 3
NBATCH_R = P // HEADS


def wait(eng, sem, n):
    if isinstance(n, int) and n <= 0:
        return
    eng.wait_ge(sem, n)


def program(nc, io, stages=99):
    ctx = ExitStack()
    with ctx:
        def sb(name, shape, dt=F32):
            return ctx.enter_context(nc.sbuf_tensor(name, shape, dt))

        def sem(name):
            return ctx.enter_context(nc.semaphore(name))

        X = sb("X", [P, TILES, DIM])
        mean = sb("mean", [P, TILES])
        var_eps = sb("var_eps", [P, TILES])
        rstd = sb("rstd", [P, TILES])
        minus_half = sb("minus_half", [P, TILES])
        bnst = sb("bnst", [P, 4, 6])
        bnmv = sb("bnmv", [P, 4, 2])
        ident = sb("ident", [P, P])
        ones_row = sb("ones_row", [1, P])
        PS = ctx.enter_context(nc.psum_tensor("PS", [P, 8, 512], F32))

        ffn0_wT = sb("ffn0_wT", [P, DIM])
        ffn0_vT = sb("ffn0_vT", [RRANK, DIM])
        ffn0_cT = sb("ffn0_cT", [RRANK, DIM])
        ffn0_b = sb("ffn0_b", [1, DIM])
        ffn0_eff = sb("ffn0_eff", [P, DIM])

        xn = sb("xn", [P, 2, 4, DIM])
        xT = sb("xT", [P, 2, SEQ])

        r_w1T = sb("r_w1T", [P, RRANK])
        r_b1 = sb("r_b1", [RRANK, 1])
        r_w2pad = sb("r_w2pad", [RRANK, 2 * P - HEADS])
        r_b2 = sb("r_b2", [P, 1])
        h1 = sb("h1", [RRANK, 2, SEQ])
        z = sb("z", [P, 2, SEQ])
        top8 = sb("top8", [P, 2, 8])
        dropped = sb("dropped", [P, 2, SEQ], F16)
        dropped_dram = nc.dram_tensor("dropped_scratch", (BATCH * HEADS, SEQ), F16, kind="Internal").ap()

        a_wqT = sb("a_wqT", [P, 2, DIM])
        a_wkT = sb("a_wkT", [P, 2, DIM])
        a_wvT = sb("a_wvT", [P, 2, DIM])
        a_woT = sb("a_woT", [P, DIM])
        a_qk_bias = sb("a_qk_bias", [P, 2, 2])
        a_v_bias = sb("a_v_bias", [1, DIM])
        a_bo = sb("a_bo", [1, DIM])
        lora_raw = sb("lora_raw", [P, 4, DIM])
        lora_a = sb("lora_a", [LORA, 4, DIM])
        lora_bT = sb("lora_bT", [LORA, 4, DIM])
        sel = sb("sel", [P, 4, GROUPS, P], F16)
        sel_drop = sb("sel_drop", [HEADS, GROUPS, P], F16)
        lane_bias = sb("lane_bias", [P, 2])
        ident16 = sb("ident16", [P, P], F16)
        qk_nat = sb("qk_nat", [P, 2, 2, SEQ], F16)
        stacks = sb("stacks", [P, 4 * GROUPS * SEQ], F16)
        qs, ks = (stacks[:, i * 2 * GROUPS * SEQ:(i + 1) * 2 * GROUPS * SEQ].rearrange(
            "p (b v q) -> p b v q", b=2, v=GROUPS) for i in range(2))
        drop_row = sb("drop_row", [HEADS, 2, SEQ], F16)
        mz = sb("mz", [P, TPB, GROUPS, P], F16)
        vp = sb("vp", [P, 2, TPB, HEADS, 32])
        probs = sb("probs", [P, 2 * LANES, TPB, SEQ])
        o_sb = sb("o_sb", [P, 2, SEQ])
        rec = sb("rec", [P, 2, TPB, LANES])
        att = sb("att", [P, 2, TPB, DIM])
        attT = sb("attT", [P, SEQ])

        wg_hi = sb("wg_hi", [P, UNITS, P], F16)
        wg_lo = sb("wg_lo", [P, UNITS, P], F16)
        wu_hi = sb("wu_hi", [P, UNITS, P], F16)
        wu_lo = sb("wu_lo", [P, UNITS, P], F16)
        wd_hi = sb("wd_hi", [P, UNITS, P], F16)
        wd_lo = sb("wd_lo", [P, UNITS, P], F16)
        wr_raw = sb("wr_raw", [P, EXPERTS])
        wr = sb("wr", [P, 2, EXPERTS], F16)
        m_bg = sb("m_bg", [P, UNITS])
        m_bu = sb("m_bu", [P, UNITS])
        m_bd = sb("m_bd", [EXPERTS + 1, DIM])
        m_br = sb("m_br", [P, EXPERTS])
        x_hi = sb("x_hi", [P, 2, WIDE], F16)
        x_lo = sb("x_lo", [P, 2, WIDE], F16)
        logits = sb("logits", [P, TPS, EXPERTS])
        ranked = sb("ranked", [P, TPS, EXPERTS])
        aff = sb("aff", [P, TPS, EXPERTS])
        best = sb("best", [P, TPS, TOPK])
        wsum = sb("wsum", [P, TPS])
        w_tok = sb("w_tok", [P, TPS, EXPERTS])
        wT = sb("wT", [EXPERTS + 1, 2, WIDE])
        w_wide = sb("w_wide", [P, 2, PAIRS, WIDE])
        w_dram = nc.dram_tensor("w_scratch", (SUPERS, EXPERTS, WIDE), F32, kind="Internal").ap()
        gate_pair = probs[:].rearrange("p (i r) t q -> p i r (t q)", i=2)
        gate = gate_pair[:, 0, :, :]
        gw = gate_pair[:, 1, :, :]
        gate_shared = lora_raw[0:INTER].rearrange("p i c -> p (i c)")
        hid = sb("hid", [P, RING + 1, WIDE])
        hid_hi = sb("hid_hi", [P, RING + 1, WIDE], F16)
        hid_lo = stacks[:, 0:(RING + 1) * WIDE].rearrange("p (r q) -> p r q", r=RING + 1)
        downT = z[:].rearrange("p h k -> p (h k)")

        x_dram = io["x"].rearrange("b (t p) h -> p (b t) h", p=P)
        out_dram = io["out"].rearrange("b (t p) h -> p (b t) h", p=P)

        s_load = sem("s_load")
        s_late = sem("s_late")
        s_x = sem("s_x")
        s_out = sem("s_out")
        s_vzero = sem("s_vzero")
        s_const = sem("s_const")
        s_stat = sem("s_stat")
        s_rstd = sem("s_rstd")
        s_xn = sem("s_xn")
        s_xnT_ps = sem("s_xnT_ps")
        s_xT = sem("s_xT")
        s_ffn = sem("s_ffn")
        s_xup = sem("s_xup")
        s_eff_ps = sem("s_eff_ps")
        s_eff = sem("s_eff")
        s_h1_ps = sem("s_h1_ps")
        s_h1 = sem("s_h1")
        s_z_ps = sem("s_z_ps")
        s_z = sem("s_z")
        s_top = [sem("s_top0"), sem("s_top1")]
        s_taken = [sem("s_taken0"), sem("s_taken1")]
        s_drop = sem("s_drop")
        s_drop_out = sem("s_drop_out")
        s_drop_in = [sem("s_drop_in0"), sem("s_drop_in1")]
        s_lora_ps = sem("s_lora_ps")
        s_lora = sem("s_lora")
        s_qk_ps = sem("s_qk_ps")
        s_hi = sem("s_hi")
        s_lo = sem("s_lo")
        s_v_ps = sem("s_v_ps")
        s_v = sem("s_v")
        s_stack_ps = sem("s_stack_ps")
        s_stack = sem("s_stack")
        s_s1 = sem("s_s1")
        s_max = sem("s_max")
        s_mT = sem("s_mT")
        s_madd = sem("s_madd")
        s_s2 = sem("s_s2")
        s_exp = sem("s_exp")
        s_av = sem("s_av")
        s_o = sem("s_o")
        s_oT = sem("s_oT")
        s_rec = sem("s_rec")
        s_norm = sem("s_norm")
        s_att0 = sem("s_att0")
        s_aT_ps = sem("s_aT_ps")
        s_aT = sem("s_aT")
        s_proj = sem("s_proj")
        s_att1 = sem("s_att1")
        s_split = sem("s_split")
        s_split_lo = sem("s_split_lo")
        s_wl = sem("s_wl")
        s_xps = sem("s_xps")
        s_xap = sem("s_xap")
        s_xhi = sem("s_xhi")
        s_xlo = sem("s_xlo")
        s_lg_ps = sem("s_lg_ps")
        s_lg = sem("s_lg")
        s_th = sem("s_th")
        s_aff = sem("s_aff")
        s_rank = sem("s_rank")
        s_wv = sem("s_wv")
        s_ws = sem("s_ws")
        s_w = sem("s_w")
        s_wT_ps = sem("s_wT_ps")
        s_wT = sem("s_wT")
        s_wst = [sem("s_wst0"), sem("s_wst1")]
        s_wide = [[sem(f"s_wide{i}{q}") for q in range(4)] for i in range(2)]
        s_g = sem("s_g")
        s_u = sem("s_u")
        s_silu = sem("s_silu")
        s_gw = sem("s_gw")
        s_hid = sem("s_hid")
        s_hhi = sem("s_hhi")
        s_hlo = sem("s_hlo")
        s_down = sem("s_down")
        s_dsum = sem("s_dsum")
        s_dT = sem("s_dT")
        s_dT_ps = sem("s_dT_ps")
        s_mup = sem("s_mup")

        def stats(dve, tile0, n):
            dve.drain()
            for t in range(n):
                nc.vector.bn_stats(bnst[:, t, :], X[:, tile0 + t, :])
            dve.drain()
            for t in range(n):
                nc.vector.bn_aggr(bnmv[:, t, :], bnst[:, t, :])
            dve.drain()
            nc.vector.tensor_copy(mean[:, bass.ds(tile0, n)], bnmv[:, 0:n, 0])
            nc.vector.tensor_scalar(var_eps[:, bass.ds(tile0, n)], bnmv[:, 0:n, 1], EPS, None,
                                    ALU.add).then_inc(s_stat, 1)

        def rstds(pool, tile0, n, g):
            pool.wait_ge(s_stat, g + 1)
            nc.gpsimd.tensor_tensor(rstd[:, bass.ds(tile0, n)], var_eps[:, bass.ds(tile0, n)],
                                    minus_half[:, 0:n], ALU.pow).then_inc(s_rstd, 1)

        with nc.Block() as block:
            table = [(ident, io["ident"]), (ffn0_wT, io["ffn0_wT"]), (ffn0_vT, io["ffn0_vT"]),
                     (ffn0_cT, io["ffn0_cT"]), (ffn0_b, io["ffn0_b"])]
            late = [(r_w1T, io["r_w1T"]), (r_b1, io["r_b1"]), (r_b2, io["r_b2"]),
                    (r_w2pad[:, P - HEADS:P], io["r_w2T"]),
                    (a_wqT[:, 0, :], io["qkv_wT"][:, 0:DIM]), (a_wkT[:, 0, :], io["qkv_wT"][:, DIM:2 * DIM]),
                    (a_wvT[:, 0, :], io["qkv_wT"][:, 2 * DIM:3 * DIM]), (a_qk_bias[:, 0, :], io["qk_bias"]),
                    (a_v_bias, io["v_bias"]), (a_bo, io["bo"]), (lora_raw, io["lora_w"]),
                    (lora_a, io["lora_a"]), (lora_bT, io["lora_bT"]), (sel, io["sel"]),
                    (sel_drop, io["sel_drop"]), (lane_bias, io["lane_bias"]), (ident16, io["ident16"])]

            @block.sync
            def _(sp):
                sp.dma_start(X[:, :, :], x_dram).then_inc(s_x, 16)
                for dst, src in table:
                    sp.dma_start(dst[:], src).then_inc(s_load, 16)
                sp.wait_ge(s_const, 3)
                for dst, src in late:
                    sp.dma_start(dst[:] if dst.shape == src.shape else dst[:], src).then_inc(s_late, 16)

            @block.gpsimd
            def _(pool):
                nc.gpsimd.memset(minus_half[:], -0.5).then_inc(s_const, 1)
                nc.gpsimd.memset(vp[:], 0.0).then_inc(s_vzero, 1)
                nc.gpsimd.memset(mz[:], 0.0).then_inc(s_vzero, 1)
                nc.gpsimd.memset(a_qk_bias[:, 1, :], 0.0).then_inc(s_vzero, 1)
                pool.wait_ge(s_vzero, 1)
                nc.gpsimd.memset(vp[:, :, :, :, HD:HD + 1], 1.0).then_inc(s_vzero, 1)
                for s in (s_att0, s_aT_ps, s_dT, s_dT_ps):
                    pool.sem_inc(s, 1)
                pool.wait_ge(s_const, 1)
                with pool.Fori(0, BATCH) as b:
                    rstds(pool, b * TPB, TPB, b)

            @block.vector
            def _(dve):
                nc.vector.memset(ones_row[:], 1.0).then_inc(s_const, 1)
                nc.vector.memset(r_w2pad[:], 0.0).then_inc(s_const, 1)
                dve.wait_ge(s_x, 16)
                with dve.Fori(0, BATCH) as b:
                    stats(dve, b * TPB, TPB)
                dve.wait_ge(s_eff_ps, 1)
                nc.vector.tensor_copy(ffn0_eff[:], PS[:, 0, 0:DIM]).then_inc(s_eff, 1)
                dve.wait_ge(s_lora_ps, 1)
                for i, w in enumerate((a_wqT[:, 1, :], a_wkT[:, 1, :], a_wvT[:, 1, :], a_woT[:])):
                    nc.vector.scalar_tensor_tensor(w, PS[:, 1, i * DIM:(i + 1) * DIM], 1.0 / LORA,
                                                   lora_raw[:, i, :], ALU.mult, ALU.add).then_inc(s_lora, 1)

            @block.tensor
            def _(pe):
                pe.wait_ge(s_load, 16 * len(table))
                nc.tensor.matmul(PS[:, 0, 0:DIM], ffn0_vT[:], ffn0_cT[:], start=True, stop=False)
                nc.tensor.matmul(PS[:, 0, 0:DIM], ident[:], ffn0_wT[:], start=False,
                                 stop=True).then_inc(s_eff_ps, 1)
                pe.wait_ge(s_late, 16 * len(late))
                for i in range(4):
                    last = nc.tensor.matmul(PS[:, 1, i * DIM:(i + 1) * DIM], lora_a[:, i, :], lora_bT[:, i, :],
                                            start=True, stop=True)
                last.then_inc(s_lora_ps, 1)

        with nc.Block() as block:
            raw = w_wide[:, 0, :, :].rearrange("p a b -> p (a b)")
            size = UNITS * P
            raws = [raw[:, i * size:(i + 1) * size].rearrange("p (u c) -> p u c", u=UNITS) for i in range(3)]
            his, los = (wg_hi, wu_hi, wd_hi), (wg_lo, wu_lo, wd_lo)

            @block.sync
            def _(sp):
                for dst, name in zip(raws, ("wg", "wu", "wd")):
                    sp.dma_start(dst, io[name]).then_inc(s_wl, 16)
                for dst, name in ((wr_raw, "wr"), (m_bg, "bg"), (m_bu, "bu"), (m_bd, "bd")):
                    sp.dma_start(dst[:], io[name]).then_inc(s_wl, 16)
                sp.dma_start(m_br[:], io["br"].partition_broadcast(P)).then_inc(s_wl, 16)

            @block.gpsimd
            def _(pool):
                nc.gpsimd.memset(wT[EXPERTS:EXPERTS + 1, :, :], 1.0).then_inc(s_vzero, 1)

            @block.scalar
            def _(act):
                act.wait_ge(s_wl, 8 * 16)
                for hi, w in zip(his, raws):
                    nc.scalar.mul(hi[:], w, WS).then_inc(s_split, 1)
                nc.scalar.copy(wr[:, 0, :], wr_raw[:]).then_inc(s_split, 1)

            @block.vector
            def _(dve):
                dve.wait_ge(s_wl, 8 * 16)
                nc.vector.tensor_scalar(m_bu[:], m_bu[:], WS, None, ALU.mult).then_inc(s_split_lo, 1)
                nc.vector.tensor_scalar(m_bd[:], m_bd[:], WS * WS, None, ALU.mult).then_inc(s_split_lo, 1)
                for i, (hi, lo, w) in enumerate(zip(his, los, raws)):
                    dve.wait_ge(s_split, i + 1)
                    nc.vector.scalar_tensor_tensor(lo[:], w, WS, hi[:], ALU.mult, ALU.subtract).then_inc(s_split_lo, 1)
                dve.wait_ge(s_split, 4)
                nc.vector.tensor_tensor(wr[:, 1, :], wr_raw[:], wr[:, 0, :], ALU.subtract).then_inc(s_split_lo, 1)

        n_ln = [0]
        n_st = [BATCH]

        def ffn0(first):
            g0, st0, ln0 = first, n_st[0], n_ln[0]

            def transpose_step(pe, b, par):
                g = ln0 + b
                pe.wait_ge(s_xn, g + 1)
                wait(pe, s_xT, g - 1)
                for t in range(TPB):
                    last = nc.tensor.transpose(PS[:, par, t * P:(t + 1) * P], xn[:, par, t, :], ident[:])
                last.then_inc(s_xnT_ps, 1)

            def product_step(pe, b, par):
                g = ln0 + b
                pe.wait_ge(s_xT, g + 1)
                wait(pe, s_xup, g0 + b - 1)
                for t in range(TPB):
                    o = PS[:, 2 + par, t * DIM:(t + 1) * DIM]
                    nc.tensor.matmul(o, xT[:, par, t * P:(t + 1) * P], ffn0_eff[:], start=True, stop=False)
                    last = nc.tensor.matmul(o, ones_row[:], ffn0_b[:], start=False, stop=True)
                last.then_inc(s_ffn, 1)

            def apply_step(dve, b, par):
                wait(dve, s_xnT_ps, ln0 + b - 1)
                for t in range(TPB):
                    T = b * TPB + t
                    last = nc.vector.tensor_scalar(xn[:, par, t, :], X[:, T, :], mean[:, bass.ds(T, 1)],
                                                   rstd[:, bass.ds(T, 1)], ALU.subtract, ALU.mult)
                last.then_inc(s_xn, 1)

            def update_step(dve, b, par):
                dve.wait_ge(s_ffn, g0 + b + 1)
                x2 = X[:, bass.ds(b * TPB, TPB), :]
                nc.vector.scalar_tensor_tensor(x2, PS[:, 2 + par, 0:SEQ].rearrange("p (t h) -> p t h", t=TPB),
                                               0.5, x2, ALU.mult, ALU.add).then_inc(s_xup, 1)
                stats(dve, b * TPB, TPB)

            def copy_step(act, b, par):
                g = ln0 + b
                act.wait_ge(s_xnT_ps, g + 1)
                wait(act, s_ffn, g0 + b - 1)
                nc.scalar.copy(xT[:, par, :], PS[:, par, 0:SEQ]).then_inc(s_xT, 1)

            with nc.Block() as block:
                @block.vector
                def _(dve):
                    dve.wait_ge(s_rstd, st0)
                    for b in range(2):
                        apply_step(dve, b, b)
                    with dve.Fori(0, BATCH // 2 - 1) as two:
                        for par in range(2):
                            update_step(dve, two * 2 + par, par)
                            apply_step(dve, two * 2 + (par + 2), par)
                    for b in range(BATCH - 2, BATCH):
                        update_step(dve, b, b % 2)

                @block.tensor
                def _(pe):
                    for b in range(2):
                        transpose_step(pe, b, b)
                    for b in range(2):
                        product_step(pe, b, b)
                        transpose_step(pe, b + 2, b)
                    with pe.Fori(1, BATCH // 2 - 1) as two:
                        for par in range(2):
                            product_step(pe, two * 2 + par, par)
                            transpose_step(pe, two * 2 + (par + 2), par)
                    for b in range(BATCH - 2, BATCH):
                        product_step(pe, b, b % 2)

                @block.scalar
                def _(act):
                    for b in range(2):
                        copy_step(act, b, b)
                    with act.Fori(1, BATCH // 2) as two:
                        for par in range(2):
                            copy_step(act, two * 2 + par, par)

                @block.gpsimd
                def _(pool):
                    with pool.Fori(0, BATCH) as b:
                        rstds(pool, b * TPB, TPB, st0 + b)
            n_st[0] += BATCH
            n_ln[0] += BATCH

        ffn0(0)

        def apply_ln(dve, b, par, g):
            wait(dve, s_xnT_ps, g - 1)
            for t in range(TPB):
                T = b * TPB + t
                last = nc.vector.tensor_scalar(xn[:, par, t, :], X[:, T, :], mean[:, bass.ds(T, 1)],
                                               rstd[:, bass.ds(T, 1)], ALU.subtract, ALU.mult)
            last.then_inc(s_xn, 1)

        def transpose_ln(pe, bank, par, g):
            pe.wait_ge(s_xn, g + 1)
            for t in range(TPB):
                last = nc.tensor.transpose(PS[:, bank, t * P:(t + 1) * P], xn[:, par, t, :], ident[:])
            last.then_inc(s_xnT_ps, 1)

        def router0():
            st0, ln0 = n_st[0], n_ln[0]
            half_rows = BATCH // 2

            def transposes(pe, b):
                wait(pe, s_xT, ln0 + b - 1)
                transpose_ln(pe, b % 2, b % 2, ln0 + b)

            def hidden(pe, b):
                pe.wait_ge(s_xT, ln0 + b + 1)
                wait(pe, s_h1, b - 1)
                nc.tensor.matmul(PS[0:RRANK, 2 + b % 2, 0:SEQ], r_w1T[:], xT[:, b % 2, :], start=True,
                                 stop=True).then_inc(s_h1_ps, 1)

            def scores(pe, b):
                half, i = divmod(b, half_rows)
                pe.wait_ge(s_h1, b + 1)
                col = P - HEADS - HEADS * i
                nc.tensor.matmul(PS[:, 4 + half, 0:SEQ], r_w2pad[:, col:col + P], h1[:, b % 2, :],
                                 start=(i == 0), stop=(i == half_rows - 1)).then_inc(s_z_ps, 1)

            with nc.Block() as block:
                @block.vector
                def _(dve):
                    dve.wait_ge(s_rstd, st0)
                    with dve.Fori(0, BATCH // 2) as two:
                        for par in range(2):
                            apply_ln(dve, two * 2 + par, par, two * 2 + (par + ln0))
                    full, rest = divmod(KEEP, 8)
                    dve.wait_ge(s_z, 2)
                    for r in range(full):
                        for h in range(2):
                            wait(dve, s_taken[h], r)
                            nc.vector.max(top8[:, h, :], z[:, h, :]).then_inc(s_top[h], 1)
                        for h in range(2):
                            dve.wait_ge(s_top[h], r + 1)
                            nc.vector.match_replace(z[:, h, :], top8[:, h, :], z[:, h, :],
                                                    NEG).then_inc(s_taken[h], 1)
                    for h in range(2):
                        dve.wait_ge(s_taken[h], full)
                        nc.vector.max(top8[:, h, :], z[:, h, :]).then_inc(s_top[h], 1)
                    for h in range(2):
                        dve.wait_ge(s_top[h], full + 1)
                        nc.vector.memset(top8[:, h, rest:8], NEG).then_inc(s_top[h], 1)
                    for h in range(2):
                        dve.wait_ge(s_top[h], full + 2)
                        nc.vector.match_replace(z[:, h, :], top8[:, h, :], z[:, h, :],
                                                NEG).then_inc(s_taken[h], 1)
                    for h in range(2):
                        dve.wait_ge(s_taken[h], full + 1)
                        nc.vector.tensor_scalar(dropped[:, h, :], z[:, h, :], NEG, -MASKED, ALU.is_gt,
                                                ALU.mult).then_inc(s_drop, 1)

                @block.tensor
                def _(pe):
                    transposes(pe, 0)
                    for b in range(BATCH):
                        if b + 1 < BATCH:
                            transposes(pe, b + 1)
                        hidden(pe, b)
                        if b >= 1:
                            scores(pe, b - 1)
                    scores(pe, BATCH - 1)

                @block.scalar
                def _(act):
                    def copy_xT(b):
                        act.wait_ge(s_xnT_ps, ln0 + b + 1)
                        wait(act, s_h1_ps, b - 1)
                        nc.scalar.copy(xT[:, b % 2, :], PS[:, b % 2, 0:SEQ]).then_inc(s_xT, 1)

                    def rectify(act, b):
                        act.wait_ge(s_h1_ps, b + 1)
                        wait(act, s_z_ps, b - 1)
                        nc.scalar.activation(h1[:, b % 2, :], PS[0:RRANK, 2 + b % 2, 0:SEQ], ACT.Relu,
                                             bias=r_b1[:, 0:1]).then_inc(s_h1, 1)

                    for b in range(BATCH):
                        copy_xT(b)
                        if b >= 1:
                            rectify(act, b - 1)
                    rectify(act, BATCH - 1)
                    for h in range(2):
                        act.wait_ge(s_z_ps, (h + 1) * half_rows)
                        nc.scalar.activation(z[:, h, :], PS[:, 4 + h, 0:SEQ], ACT.Identity,
                                             bias=r_b2[:, 0:1]).then_inc(s_z, 1)

                @block.sync
                def _(sp):
                    sp.wait_ge(s_drop, 2)
                    sp.dma_start(dropped_dram.rearrange("(h p) k -> p h k", p=P),
                                 dropped[:, :, :]).then_inc(s_drop_out, 16)
                    sp.wait_ge(s_drop_out, 16)
            n_ln[0] += BATCH

        def attention(layer):
            st0, ln0, a0 = n_st[0], n_ln[0], layer * BATCH
            S1, S2, OB, MB = 0, 2, 4, 6
            masked = layer == 0

            def pe_transposes(pe, n, par, has_cur):
                if has_cur:
                    pe.wait_ge(s_madd, a0 + n)
                if has_cur and not masked:
                    wait(pe, s_aT, n - 1)
                transpose_ln(pe, MB, par, ln0 + n)

            def pe_qk(pe, n, par, has_cur):
                pe.wait_ge(s_xT, ln0 + n + 1)
                if has_cur and masked:
                    wait(pe, s_norm, 4 * (a0 + n - 1))
                if has_cur and not masked:
                    wait(pe, s_att1, n - 1)
                for i, w in enumerate((a_wqT, a_wkT)):
                    last = nc.tensor.matmul(PS[:, MB + 1, i * SEQ:(i + 1) * SEQ], w[:, layer, :], xT[:, par, :],
                                            start=True, stop=True)
                last.then_inc(s_qk_ps, 1)

            def pe_v(pe, n, par):
                for t in range(TPB):
                    o = PS[:, MB, t * DIM:(t + 1) * DIM]
                    last = nc.tensor.matmul(o, xT[:, par, t * P:(t + 1) * P], a_wvT[:, layer, :], start=True,
                                            stop=not masked)
                    if masked:
                        last = nc.tensor.matmul(o, ones_row[:], a_v_bias[:], start=False, stop=True)
                last.then_inc(s_v_ps, 1)

            def pe_stack(pe, n, par, piece, after):
                which, half = divmod(piece, 2)
                if piece == 0:
                    pe.wait_ge(s_hi, a0 + n + 1)
                    pe.wait_ge(s_lo, a0 + n + 1)
                if piece == 2 and masked:
                    pe.wait_ge(s_drop_in[par], after[1])
                pe.wait_ge(*after[0])
                bank = MB + (1, 0, 0, 1)[piece]
                for i in range(2):
                    v = 2 * half + i
                    o = PS[:, bank, i * SEQ:(i + 1) * SEQ]
                    nc.tensor.matmul(o, sel[:, 2 * which, v, :], qk_nat[:, 0, which, :], start=True, stop=False)
                    last = nc.tensor.matmul(o, sel[:, 2 * which + 1, v, :], qk_nat[:, 1, which, :], start=False,
                                            stop=not (masked and which == 1))
                    if masked and which == 1:
                        last = nc.tensor.matmul(o, sel_drop[:, v, :], drop_row[:, par, :], start=False, stop=True)
                last.then_inc(s_stack_ps, 1)

            def pe_s1(pe, n, par, h):
                u = (a0 + n) * HEADS + h
                v, j = divmod(h, LANES)
                if h == 0:
                    pe.wait_ge(s_stack, 4 * (a0 + n) + 4)
                wait(pe, s_max, u - 1)
                lane = slice(32 * j, 32 * j + 32)
                for t in range(TPB):
                    last = nc.tensor.matmul(PS[:, S1 + h % 2, t * SEQ:(t + 1) * SEQ], qs[lane, par, v, t * P:(t + 1) * P],
                                            ks[lane, par, v, :], start=True, stop=True, tile_position=(32 * j, 0))
                last.then_inc(s_s1, 1)

            def pe_maxT(pe, n):
                pe.wait_ge(s_max, (a0 + n + 1) * HEADS)
                bank = PS[:, MB, :].bitcast(F16)
                for v in range(GROUPS):
                    for t in range(TPB):
                        last = nc.tensor.transpose(bank[:, v * SEQ + t * P:v * SEQ + (t + 1) * P], mz[:, t, v, :],
                                                   ident16[:])
                last.then_inc(s_mT, 1)

            def pe_s2(pe, c, par, h):
                u = (a0 + c) * HEADS + h
                v, j = divmod(h, LANES)
                if h == 0:
                    pe.wait_ge(s_madd, a0 + c + 1)
                wait(pe, s_exp, u - 1)
                lane = slice(32 * j, 32 * j + 32)
                for t in range(TPB):
                    last = nc.tensor.matmul(PS[:, S2 + h % 2, t * SEQ:(t + 1) * SEQ], ks[lane, par, v, t * P:(t + 1) * P],
                                            qs[lane, par, v, :], start=True, stop=True, tile_position=(32 * j, 0))
                last.then_inc(s_s2, 1)

            def pe_av(pe, c, par, v):
                g = 4 * (a0 + c) + v
                pe.wait_ge(s_exp, 4 * g + 4)
                if v == 0:
                    pe.wait_ge(s_v, a0 + c + 1)
                wait(pe, s_o, g - 1)
                for t in range(TPB):
                    for j in range(LANES):
                        h = LANES * v + j
                        last = nc.tensor.matmul(PS[32 * j:32 * j + 32, OB + v % 2, 0:SEQ], vp[:, par, t, h, :],
                                                probs[:, h % 8, t, :], start=(t == 0), stop=(t == TPB - 1),
                                                skip_group_check=True)
                last.then_inc(s_av, 1)

            def pe_oT(pe, c, v, bank, *after):
                g = 4 * (a0 + c) + v
                pe.wait_ge(s_o, g + 1)
                for a in after:
                    wait(pe, *a)
                for t in range(TPB):
                    last = nc.tensor.transpose(PS[:, bank, t * P:(t + 1) * P], o_sb[:, v % 2, t * P:(t + 1) * P], ident[:])
                last.then_inc(s_oT, 1)

            def pe_project(pe, c, par):
                pe.wait_ge(s_norm, 4 * (a0 + c) + 4)
                for t in range(TPB):
                    last = nc.tensor.transpose(PS[:, MB, t * P:(t + 1) * P], att[:, par, t, :], ident[:])
                last.then_inc(s_aT_ps, 1)
                pe.wait_ge(s_aT, c + 1)
                for t in range(TPB):
                    o = PS[:, MB + 1, t * DIM:(t + 1) * DIM]
                    nc.tensor.matmul(o, attT[:, t * P:(t + 1) * P], a_woT[:], start=True, stop=False)
                    last = nc.tensor.matmul(o, ones_row[:], a_bo[:], start=False, stop=True)
                last.then_inc(s_proj, 1)

            def pe_step(pe, n, c, par, has_next, has_cur):
                cp = 1 - par
                g4 = 4 * (a0 + c)
                if has_next:
                    st4 = 4 * (a0 + n)
                    pe_transposes(pe, n, par, has_cur)
                s2 = (lambda h: pe_s2(pe, c, cp, h)) if has_cur else (lambda h: None)
                s1 = (lambda h: pe_s1(pe, n, par, h)) if has_next else (lambda h: None)
                s2(0), s2(1)
                if has_next:
                    pe_qk(pe, n, par, has_cur)
                s2(2), s2(3)
                if has_next:
                    pe_v(pe, n, par)
                s2(4)
                if has_cur:
                    pe_av(pe, c, cp, 0)
                if has_next:
                    pe_stack(pe, n, par, 0, [(s_lo, a0 + n + 1)])
                s2(5)
                if has_next:
                    pe_stack(pe, n, par, 1, [(s_v, a0 + n + 1)])
                s2(6)
                if has_cur and has_next:
                    pe_oT(pe, c, 0, MB + 1, (s_stack, st4 + 1))
                elif has_cur:
                    pe_oT(pe, c, 0, MB + 1, (s_norm, g4), (s_att1, 0 if masked else c))
                if has_next:
                    pe_stack(pe, n, par, 2, [(s_stack, st4 + 2), loaded(n, par)])
                s2(7)
                if has_next:
                    pe_stack(pe, n, par, 3, [(s_norm, g4 + 1) if has_cur else (s_stack, st4 + 1)])
                s2(8)
                if has_cur:
                    pe_av(pe, c, cp, 1)
                s1(0), s1(1), s2(9), s1(2), s1(3)
                if has_cur:
                    pe_oT(pe, c, 1, MB, *([(s_stack, st4 + 3)] if has_next else [(s_madd, a0 + c + 1), (s_aT, 0 if masked else c)]))
                s2(10), s1(4), s1(5), s2(11), s1(6), s1(7), s2(12)
                if has_cur:
                    pe_av(pe, c, cp, 2)
                s1(8), s1(9), s2(13)
                if has_cur:
                    pe_oT(pe, c, 2, MB + 1, *([(s_stack, st4 + 4)] if has_next else []), (s_norm, g4 + 1))
                s1(10), s1(11), s2(14), s1(12), s1(13), s2(15), s1(14), s1(15)
                if has_cur:
                    pe_av(pe, c, cp, 3)
                if has_next:
                    if has_cur:
                        pe.wait_ge(s_norm, g4 + 2)
                    pe_maxT(pe, n)
                if has_cur:
                    pe_oT(pe, c, 3, MB + 1, (s_norm, g4 + 3))
                    if not masked:
                        if has_next:
                            pe.wait_ge(s_madd, a0 + n + 1)
                        pe_project(pe, c, cp)

            def loaded(n, par):
                return (n - par) * 8 + 16

            def act_step(act, n, c, par, has_next, has_cur):
                cp = 1 - par

                def exps(*hs):
                    if not has_cur:
                        return
                    for h in hs:
                        u = (a0 + c) * HEADS + h
                        act.wait_ge(s_s2, u + 1)
                        if h % LANES == 0:
                            wait(act, s_av, 4 * (a0 + c) + h // LANES - 1)
                        nc.scalar.activation(probs[:, h % 8, :, :], PS[:, S2 + h % 2, :].rearrange("p (t q) -> p t q", t=TPB),
                                             ACT.Exp, scale=SCORE_SCALE).then_inc(s_exp, 1)

                def out_copy(v):
                    if not has_cur:
                        return
                    g = 4 * (a0 + c) + v
                    act.wait_ge(s_av, g + 1)
                    wait(act, s_oT, g - 1)
                    nc.scalar.copy(o_sb[:, v % 2, :], PS[:, OB + v % 2, 0:SEQ]).then_inc(s_o, 1)

                def stack_copy(piece):
                    if not has_next:
                        return
                    which, half = divmod(piece, 2)
                    act.wait_ge(s_stack_ps, 4 * (a0 + n) + piece + 1)
                    if piece == 0:
                        wait(act, s_s2, (a0 + n - 1) * HEADS)
                    bank = MB + (1, 0, 0, 1)[piece]
                    dst = (qs, ks)[which]
                    nc.scalar.activation(dst[:, par, 2 * half:2 * half + 2, :],
                                         PS[:, bank, :].rearrange("p (v q) -> p v q", v=2), ACT.Identity,
                                         bias=lane_bias[:, which:which + 1]).then_inc(s_stack, 1)

                if has_next:
                    act.wait_ge(s_xnT_ps, ln0 + n + 1)
                    wait(act, s_v_ps, a0 + n - 1)
                    nc.scalar.copy(xT[:, par, :], PS[:, MB, 0:SEQ]).then_inc(s_xT, 1)
                exps(0, 1)
                if has_next:
                    act.wait_ge(s_qk_ps, a0 + n + 1)
                    wait(act, s_stack_ps, 4 * (a0 + n))
                    for i in range(2):
                        last = nc.scalar.activation(qk_nat[:, 0, i, :], PS[:, MB + 1, i * SEQ:(i + 1) * SEQ],
                                                    ACT.Identity, bias=a_qk_bias[:, layer, i:i + 1])
                    last.then_inc(s_hi, 1)
                exps(2, 3)
                if has_next:
                    act.wait_ge(s_v_ps, a0 + n + 1)
                    wait(act, s_av, 4 * (a0 + n - 1))
                    nc.scalar.copy(vp[:, par, :, :, 0:HD],
                                   PS[:, MB, 0:SEQ].rearrange("p (t h d) -> p t h d", t=TPB, h=HEADS)).then_inc(s_v, 1)
                exps(4)
                out_copy(0)
                stack_copy(0)
                exps(5)
                stack_copy(1)
                exps(6)
                stack_copy(2)
                exps(7)
                stack_copy(3)
                exps(8)
                out_copy(1)
                exps(9, 10, 11, 12)
                out_copy(2)
                exps(13, 14, 15)
                out_copy(3)
                if has_cur and not masked:
                    act.wait_ge(s_aT_ps, c + 2)
                    wait(act, s_proj, c)
                    nc.scalar.copy(attT[:], PS[:, MB, 0:SEQ]).then_inc(s_aT, 1)

            def dve_step(dve, n, c, par, has_next, has_cur, has_old):
                cp = 1 - par

                def reduces(*hs):
                    if not has_next:
                        return
                    for h in hs:
                        u = (a0 + n) * HEADS + h
                        v, j = divmod(h, LANES)
                        dve.wait_ge(s_s1, u + 1)
                        if h == 0:
                            wait(dve, s_mT, a0 + n)
                        nc.vector.tensor_reduce(mz[:, :, v, 32 * j + ROW_MAX], PS[:, S1 + h % 2, :].rearrange("p (t k) -> p t k", t=TPB),
                                                AX.X, ALU.max).then_inc(s_max, 1)

                def norm(v):
                    if not has_cur:
                        return
                    g = 4 * (a0 + c) + v
                    bank = MB + (1, 0, 1, 1)[v]
                    T = PS[:, bank, 0:SEQ].rearrange("p (t j d) -> p t j d", t=TPB, j=LANES)
                    dve.wait_ge(s_oT, g + 1)
                    wait(dve, s_norm, g - 1)
                    nc.vector.reciprocal(rec[:, v % 2, :, :], T[:, :, :, HD]).then_inc(s_rec, 1)
                    if v == 0:
                        dve.wait_ge(s_att0 if masked else s_aT_ps, c)
                    dve.wait_ge(s_rec, g + 1)
                    o = att[:, cp, :, v * LANES * HD:(v + 1) * LANES * HD].rearrange("p t (j d) -> p t j d", j=LANES)
                    nc.vector.tensor_tensor(o, T[:, :, :, 0:HD],
                                            rec[:, v % 2, :, :].unsqueeze(3).broadcast_to([P, TPB, LANES, HD]),
                                            ALU.mult).then_inc(s_norm, 1)

                if has_old and masked:
                    dve.wait_ge(s_att0, c + 1)
                if has_next:
                    dve.wait_ge(s_hi, a0 + n + 1)
                    wait(dve, s_stack_ps, 4 * (a0 + n))
                    for i in range(2):
                        last = nc.vector.scalar_tensor_tensor(
                            qk_nat[:, 1, i, :], PS[:, MB + 1, i * SEQ:(i + 1) * SEQ], a_qk_bias[:, layer, i:i + 1],
                            qk_nat[:, 0, i, :], ALU.add, ALU.subtract)
                    last.then_inc(s_lo, 1)
                if has_old:
                    o = c - 1
                    stats(dve, o * TPB, TPB)
                norm(0)
                reduces(0, 1, 2, 3)
                norm(1)
                reduces(4, 5, 6, 7, 8, 9)
                norm(2)
                if has_next and not (isinstance(n, int) and n + 1 >= BATCH):
                    apply_ln(dve, n + 1, cp, ln0 + n + 1)
                reduces(10, 11, 12, 13, 14, 15)
                if has_next:
                    dve.wait_ge(s_mT, a0 + n + 1)
                    dve.wait_ge(s_stack, 4 * (a0 + n) + 4)
                    m = PS[:, MB, :].bitcast(F16).rearrange("p (v q) -> p v q", v=GROUPS)
                    nc.vector.tensor_tensor(qs[:, par, :, :], qs[:, par, :, :], m, ALU.add).then_inc(s_madd, 1)
                norm(3)
                if has_cur and not masked:
                    dve.wait_ge(s_proj, c + 1)
                    x2 = X[:, bass.ds(c * TPB, TPB), :]
                    nc.vector.tensor_tensor(x2, x2, PS[:, MB + 1, 0:SEQ].rearrange("p (t h) -> p t h", t=TPB),
                                            ALU.add).then_inc(s_att1, 1)

            def run(step, engine):
                step(0, -1, 0, True, False, False)
                step(1, 0, 1, True, True, False)
                with engine.Fori(1, BATCH // 2 - 1) as two:
                    for par in range(2):
                        step(two * 2 + par, two * 2 + (par - 1), par, True, True, True)
                for n in range(BATCH - 2, BATCH):
                    step(n, n - 1, n % 2, True, True, True)
                step(BATCH, BATCH - 1, 0, False, True, True)
                step(BATCH + 1, BATCH, 1, False, False, True)

            with nc.Block() as block:
                @block.tensor
                def _(pe):
                    run(lambda n, c, par, hn, hc, ho: pe_step(pe, n, c, par, hn, hc), pe)

                @block.scalar
                def _(act):
                    run(lambda n, c, par, hn, hc, ho: act_step(act, n, c, par, hn, hc), act)

                @block.vector
                def _(dve):
                    dve.wait_ge(s_rstd, st0)
                    apply_ln(dve, 0, 0, ln0)
                    run(lambda n, c, par, hn, hc, ho: dve_step(dve, n, c, par, hn, hc, ho), dve)

                @block.gpsimd
                def _(pool):
                    def row(b, par):
                        if masked:
                            pool.wait_ge(s_norm, 4 * (a0 + b) + 4)
                            x2 = X[:, bass.ds(b * TPB, TPB), :]
                            nc.gpsimd.tensor_tensor(x2, x2, att[:, par, :, :], ALU.add).then_inc(s_att0, 1)
                        rstds(pool, b * TPB, TPB, st0 + b)

                    with pool.Fori(0, BATCH // 2) as two:
                        for par in range(2):
                            row(two * 2 + par, par)

                if masked:
                    @block.sync
                    def _(sp):
                        def load(b, par):
                            wait(sp, s_stack_ps, 4 * (a0 + b - 1))
                            sp.dma_start(drop_row[:, par, :], dropped_dram[bass.ds(b * HEADS, HEADS), :])\
                                .then_inc(s_drop_in[par], 16)

                        for par in range(2):
                            load(par, par)
                        with sp.Fori(1, BATCH // 2) as two:
                            for par in range(2):
                                load(two * 2 + par, par)
            n_st[0] += BATCH
            n_ln[0] += BATCH

        def experts(turn):
            st0, m0 = n_st[0], turn * SUPERS

            def pe_prep_x(pe, n, par):
                g = m0 + n
                pe.wait_ge(s_xap, g + 1)
                wait(pe, s_wT, g)
                for t in range(TPS):
                    last = nc.tensor.transpose(PS[:, 6, t * P:(t + 1) * P], xn[:, par, t, :], ident[:])
                last.then_inc(s_xps, 1)

            def pe_logits(pe, n, par):
                g = m0 + n
                pe.wait_ge(s_xlo, g + 1)
                wait(pe, s_mup, g - 1)
                for t in range(TPS):
                    o = PS[:, 7, t * EXPERTS:(t + 1) * EXPERTS]
                    parts = [(a, b) for a in (x_hi, x_lo) for b in range(2)]
                    for i, (a, b) in enumerate(parts):
                        last = nc.tensor.matmul(o, a[:, par, t * P:(t + 1) * P], wr[:, b, :], start=(i == 0),
                                                stop=(i == len(parts) - 1))
                last.then_inc(s_lg_ps, 1)

            def pe_wT(pe, n):
                pe.wait_ge(s_w, m0 + n + 1)
                for t in range(TPS):
                    last = nc.tensor.transpose(PS[0:EXPERTS, 6, t * P:(t + 1) * P], w_tok[:, t, :], ident[:])
                last.then_inc(s_wT_ps, 1)

            def rows(k):
                return (INTER, PAIRS) if k == 0 else (P, k - 1)

            def pe_unit(pe, c, par, k):
                u = (m0 + c) * UNITS + k
                bank = (par + k) % 2
                m, e = rows(k)
                if k == 0:
                    pe.wait_ge(s_xlo, m0 + c + 1)
                for ready, free, lo_bank, hi_w, lo_w in ((s_g, s_silu, 0, wg_hi, wg_lo), (s_u, s_hid, 2, wu_hi, wu_lo)):
                    wait(pe, free, u - 1)
                    o = PS[0:m, lo_bank + bank, :]
                    nc.tensor.matmul(o, hi_w[:, e, 0:m], x_hi[:, par, :], start=True, stop=False)
                    nc.tensor.matmul(o, hi_w[:, e, 0:m], x_lo[:, par, :], start=False, stop=False)
                    nc.tensor.matmul(o, lo_w[:, e, 0:m], x_hi[:, par, :], start=False, stop=True).then_inc(ready, 1)

            def pe_down(pe, c, par, k):
                u = (m0 + c) * UNITS + k
                m, e = rows(k)
                r = slot(k)
                pe.wait_ge(s_hlo, u + 1)
                if k == 0:
                    pe.wait_ge(s_dT, m0 + c)
                o = PS[:, 4 + par, :]
                nc.tensor.matmul(o, wd_hi[0:m, e, :], hid_hi[0:m, r, :], start=(k == 0), stop=False)
                nc.tensor.matmul(o, wd_hi[0:m, e, :], hid_lo[0:m, r, :], start=False, stop=False)
                nc.tensor.matmul(o, wd_lo[0:m, e, :], hid_hi[0:m, r, :], start=False, stop=False).then_inc(s_down, 1)

            def slot(k):
                return RING if k == 0 else (k - 1) % RING

            def pe_biases(pe, o, par):
                nc.tensor.matmul(PS[:, 4 + par, :], m_bd[:], wT[:, par, :], start=False, stop=True).then_inc(s_dsum, 1)

            def pe_dT(pe, o):
                pe.wait_ge(s_dT, m0 + o + 2)
                for t in range(TPS):
                    last = nc.tensor.transpose(PS[:, 7, t * P:(t + 1) * P], downT[:, t * P:(t + 1) * P], ident[:])
                last.then_inc(s_dT_ps, 1)

            def pe_step(pe, n, c, o, par, has_next, has_cur, has_old):
                cp = 1 - par
                for k in range(UNITS):
                    if has_cur:
                        pe_unit(pe, c, cp, k)
                    if has_next and k == 0:
                        pe_prep_x(pe, n, par)
                    if k < LAG:
                        if has_old:
                            pe_down(pe, o, par, UNITS - LAG + k)
                    elif has_cur:
                        pe_down(pe, c, cp, k - LAG)
                    if k == LAG and has_old:
                        pe_biases(pe, o, par)
                    if k == LAG + 1 and has_old:
                        pe_dT(pe, o)
                    if k == LAG + 2 and has_next:
                        pe_logits(pe, n, par)
                    if k == LAG + 8 and has_next:
                        pe_wT(pe, n)

            def act_step(act, n, c, o, par, has_next, has_cur, has_old):
                cp = 1 - par

                def high(c_, p_, k):
                    u = (m0 + c_) * UNITS + k
                    m, _ = rows(k)
                    act.wait_ge(s_hid, u + 1)
                    wait(act, s_down, u - RING + 1)
                    nc.scalar.copy(hid_hi[0:m, slot(k), :], hid[0:m, slot(k), :]).then_inc(s_hhi, 1)

                for k in range(UNITS):
                    if has_cur:
                        u = (m0 + c) * UNITS + k
                        m, e = rows(k)
                        act.wait_ge(s_g, u + 1)
                        wait(act, s_hid, u - RING + 1)
                        nc.scalar.activation(gate_shared if k == 0 else gate[:, slot(k), :], PS[0:m, (cp + k) % 2, :], ACT.Silu,
                                             bias=m_bg[0:m, e:e + 1], scale=1.0 / WS).then_inc(s_silu, 1)
                        if k >= 1:
                            high(c, cp, k - 1)
                    if k == 0 and has_old:
                        high(o, par, UNITS - 1)
                    if k == 1 and has_next:
                        act.wait_ge(s_xps, m0 + n + 1)
                        nc.scalar.copy(x_hi[:, par, :], PS[:, 6, :]).then_inc(s_xhi, 1)
                    if k == LAG and has_old:
                        act.wait_ge(s_dsum, m0 + o + 1)
                        act.wait_ge(s_dT_ps, m0 + o + 1)
                        nc.scalar.copy(downT, PS[:, 4 + par, :]).then_inc(s_dT, 1)
                    if k == LAG + 3 and has_next:
                        act.wait_ge(s_lg, m0 + n + 1)
                        nc.scalar.activation(aff[:], logits[:], ACT.Tanh, scale=0.5).then_inc(s_th, 1)
                    if k == LAG + 8 and has_next:
                        act.wait_ge(s_wT_ps, m0 + n + 1)
                        wait(act, s_wst[par], (n - par) * 8)
                        wait(act, s_dsum, m0 + n - 1)
                        nc.scalar.copy(wT[0:EXPERTS, par, :], PS[0:EXPERTS, 6, :]).then_inc(s_wT, 1)

            def dve_step(dve, n, c, o, par, has_next, has_cur, has_old):
                cp = 1 - par
                g = m0 + n

                def low(c_, p_, k):
                    u = (m0 + c_) * UNITS + k
                    m, _ = rows(k)
                    r = slot(k)
                    dve.wait_ge(s_hhi, u + 1)
                    nc.vector.tensor_tensor(hid_lo[0:m, r, :], hid[0:m, r, :], hid_hi[0:m, r, :],
                                            ALU.subtract).then_inc(s_hlo, 1)

                for k in range(UNITS):
                    if has_cur:
                        u = (m0 + c) * UNITS + k
                        m, e = rows(k)
                        r = slot(k)
                        dve.wait_ge(s_u, u + 1)
                        if k == 0:
                            dve.wait_ge(s_silu, u + 1)
                        else:
                            dve.wait_ge(s_gw, (m0 + c) * PAIRS + k)
                        wait(dve, s_hlo, u - RING + 1)
                        nc.vector.scalar_tensor_tensor(hid[0:m, r, :], PS[0:m, 2 + (cp + k) % 2, :], m_bu[0:m, e:e + 1],
                                                       gate_shared if k == 0 else gw[:, r, :], ALU.add,
                                                       ALU.mult).then_inc(s_hid, 1)
                        if k >= 1:
                            low(c, cp, k - 1)
                    if k == 0 and has_old:
                        low(o, par, UNITS - 1)
                    if k == 1 and has_next:
                        dve.wait_ge(s_xhi, g + 1)
                        nc.vector.tensor_tensor(x_lo[:, par, :], PS[:, 6, :], x_hi[:, par, :],
                                                ALU.subtract).then_inc(s_xlo, 1)
                    if k == LAG + 1 and has_old:
                        dve.wait_ge(s_dT_ps, m0 + o + 2)
                        x4 = X[:, bass.ds(o * TPS, TPS), :]
                        nc.vector.scalar_tensor_tensor(x4, PS[:, 7, :].rearrange("p (t h) -> p t h", t=TPS),
                                                       0.5 / (WS * WS), x4, ALU.mult, ALU.add).then_inc(s_mup, 1)
                    if k == LAG + 2:
                        if has_next:
                            dve.wait_ge(s_lg_ps, g + 1)
                            nc.vector.tensor_tensor(logits[:], PS[:, 7, 0:TPS * EXPERTS].rearrange("p (t e) -> p t e", t=TPS),
                                                    m_br[:].unsqueeze(1).broadcast_to([P, TPS, EXPERTS]),
                                                    ALU.add).then_inc(s_lg, 1)
                        if has_old and turn == 0:
                            stats(dve, o * TPS, TPS)
                    if has_next and k == LAG + 3:
                        dve.drain()
                        for t in range(TPS):
                            nc.vector.max(best[:, t, :], logits[:, t, :])
                    if has_next and k == LAG + 4:
                        dve.drain()
                        for t in range(TPS):
                            last = nc.vector.match_replace(ranked[:, t, :], best[:, t, :], logits[:, t, :], NEG)
                        last.then_inc(s_rank, 1)
                        dve.wait_ge(s_th, g + 1)
                        nc.vector.tensor_scalar(aff[:], aff[:], 0.5, 0.5, ALU.mult, ALU.add).then_inc(s_aff, 1)
                    if has_next and k == LAG + 5:
                        dve.wait_ge(s_rank, g + 1)
                        dve.wait_ge(s_aff, g + 1)
                        nc.vector.scalar_tensor_tensor(ranked[:], ranked[:], NEG, aff[:], ALU.is_le,
                                                       ALU.mult).then_inc(s_wv, 1)
                    if has_next and k == LAG + 6:
                        dve.wait_ge(s_wv, g + 1)
                        nc.vector.tensor_reduce(wsum[:], ranked[:], AX.X, ALU.add).then_inc(s_ws, 1)
                        dve.wait_ge(s_ws, 3 * g + 1)
                        nc.vector.tensor_scalar(wsum[:], wsum[:], 1e-9, None, ALU.add).then_inc(s_ws, 1)
                    if has_next and k == LAG + 7:
                        dve.wait_ge(s_ws, 3 * g + 2)
                        nc.vector.reciprocal(wsum[:], wsum[:]).then_inc(s_ws, 1)
                        dve.wait_ge(s_ws, 3 * g + 3)
                        wait(dve, s_wT_ps, g)
                        nc.vector.tensor_tensor(w_tok[:], ranked[:], wsum[:].unsqueeze(2).broadcast_to([P, TPS, EXPERTS]),
                                                ALU.mult).then_inc(s_w, 1)
                    if has_next and k == UNITS - 3 and not (isinstance(n, int) and n + 1 >= SUPERS):
                        apply_wide(dve, n + 1, cp)

            def apply_wide(dve, n, par):
                wait(dve, s_xps, m0 + n - 1)
                for t in range(TPS):
                    T = n * TPS + t
                    last = nc.vector.tensor_scalar(xn[:, par, t, :], X[:, T, :], mean[:, bass.ds(T, 1)],
                                                   rstd[:, bass.ds(T, 1)], ALU.subtract, ALU.mult)
                last.then_inc(s_xap, 1)

            def pool_step(pool, n, c, o, par, has_next, has_cur, has_old):
                cp = 1 - par
                for k in range(1, UNITS):
                    if has_cur:
                        u = (m0 + c) * UNITS + k
                        pool.wait_ge(s_silu, u + 1)
                        if (k - 1) % 4 == 0:
                            pool.wait_ge(s_wide[cp][(k - 1) // 4], (turn * SUPERS + (c - cp) + 2) * 16)
                        wait(pool, s_hid, u - RING + 1)
                        nc.gpsimd.tensor_tensor(gw[:, slot(k), :], gate[:, slot(k), :], w_wide[:, cp, k - 1, :],
                                                ALU.mult).then_inc(s_gw, 1)
                    if k == LAG + 3 and has_old and turn == 0:
                        rstds(pool, o * TPS, TPS, st0 + o)

            def sp_step(sp, n, par):
                sp.wait_ge(s_wT, m0 + n + 1)
                done = (turn * SUPERS + (n - par) + 2) * 8
                sp.dma_start(w_dram[bass.ds(n, 1), :, :].rearrange("a e t -> (a e) t"), wT[0:EXPERTS, par, :])\
                    .then_inc(s_wst[par], 16)
                sp.wait_ge(s_wst[par], done)
                rows_of = w_dram[bass.ds(n, 1), :, :].rearrange("a (k e) t -> e (a k) t", e=2)
                for q in range(4):
                    wait(sp, s_gw, (m0 + n - 2) * PAIRS + 4 * q + 4)
                    for e in range(2):
                        sp.dma_start(w_wide[64 * e:64 * e + 64, par, 4 * q:4 * q + 4, :],
                                     rows_of[e, 4 * q:4 * q + 4, :].partition_broadcast(INTER))\
                            .then_inc(s_wide[par][q], 16)

            def run(step, engine):
                step(0, -1, -2, 0, True, False, False)
                step(1, 0, -1, 1, True, True, False)
                with engine.Fori(1, SUPERS // 2 - 1) as two:
                    for par in range(2):
                        step(two * 2 + par, two * 2 + (par - 1), two * 2 + (par - 2), par, True, True, True)
                for n in range(SUPERS - 2, SUPERS):
                    step(n, n - 1, n - 2, n % 2, True, True, True)
                step(SUPERS, SUPERS - 1, SUPERS - 2, 0, False, True, True)
                step(SUPERS + 1, SUPERS, SUPERS - 1, 1, False, False, True)

            with nc.Block() as block:
                @block.tensor
                def _(pe):
                    run(lambda *a: pe_step(pe, *a), pe)

                @block.scalar
                def _(act):
                    run(lambda *a: act_step(act, *a), act)

                @block.vector
                def _(dve):
                    dve.wait_ge(s_rstd, st0)
                    apply_wide(dve, 0, 0)
                    run(lambda *a: dve_step(dve, *a), dve)

                @block.gpsimd
                def _(pool):
                    run(lambda *a: pool_step(pool, *a), pool)

                @block.sync
                def _(sp):
                    for n in range(2):
                        sp_step(sp, n, n)
                    with sp.Fori(1, SUPERS // 2) as two:
                        for par in range(2):
                            sp_step(sp, two * 2 + par, par)
            if turn == 0:
                n_st[0] += SUPERS

        if stages >= 2:
            router0()
            attention(0)
        if stages >= 3:
            ffn0(BATCH)
        if stages >= 4:
            experts(0)
        if stages >= 5:
            attention(1)
        if stages >= 6:
            experts(1)

        with nc.Block() as block:
            @block.sync
            def _(sp):
                sp.dma_start(out_dram, X[:, :, :]).then_inc(s_out, 16)
                sp.wait_ge(s_out, 16)


def layout(inp):
    import numpy as np
    c = np.ascontiguousarray
    a = {k: np.asarray(v) for k, v in inp.items()}
    f = {}
    f["x"] = c(a["L0_attn_hidden_states"])
    f["ident"] = np.eye(128, dtype=np.float32)
    f["ffn0_wT"] = c(a["L0_ffn_W"].T)
    f["ffn0_vT"] = c(a["L0_ffn_V_r"].T)
    f["ffn0_cT"] = c(a["L0_ffn_C"].T)
    f["ffn0_b"] = c(a["L0_ffn_b"].reshape(1, -1))
    w = a["L0_attn_qkv_w"]
    f["qkv_wT"] = c(w.T)
    f["qk_bias"] = c(a["L0_attn_qkv_b"].reshape(3, 128)[0:2].T)
    f["v_bias"] = c(a["L0_attn_qkv_b"].reshape(3, 128)[2:3])
    f["r_w1T"] = c(a["L0_attn_r_w1"].T)
    f["r_b1"] = c(a["L0_attn_r_b1"].reshape(-1, 1))
    f["r_w2T"] = c(a["L0_attn_r_w2"].T)
    f["r_b2"] = c(np.tile(a["L0_attn_r_b2"], 8).reshape(-1, 1))
    f["bo"] = c(a["L1_attn_bo"].reshape(1, -1))
    f["lora_w"] = c(np.stack([a["L1_attn_W" + k].T for k in "qkvo"], 1))
    f["lora_a"] = c(np.stack([a["L1_attn_A" + k] for k in "qkvo"], 1))
    f["lora_bT"] = c(np.stack([a["L1_attn_B" + k].T for k in "qkvo"], 1))
    sel = np.zeros((128, 4, GROUPS, 128), np.float16)
    drop = np.zeros((HEADS, GROUPS, 128), np.float16)
    lane = np.zeros((128, 2), np.float32)
    for v in range(GROUPS):
        for j in range(LANES):
            drop[v * LANES + j, v, 32 * j + ROW_MASK] = 1
            for d in range(HD):
                src = (v * LANES + j) * HD + d
                for copy, (q, k) in enumerate(((0, 2), (1, 2), (0, 3))):
                    sel[src, q, v, 32 * j + copy * HD + d] = 1
                    sel[src, k, v, 32 * j + copy * HD + d] = 1
    lane[ROW_MASK::32, 0] = MASKED
    lane[ROW_MAX::32, 1] = -1.0
    f["sel"], f["sel_drop"], f["lane_bias"] = sel, drop, lane
    f["ident16"] = np.eye(128, dtype=np.float16)
    def cols(we, ws):
        w = np.zeros((128, UNITS, 128), np.float32)
        w[:, :PAIRS] = we.transpose(1, 0, 2).reshape(128, PAIRS, 128)
        w[:, PAIRS, :INTER] = ws
        return w

    def column(be, bs):
        w = np.zeros((128, UNITS), np.float32)
        w[:, :PAIRS] = be.reshape(PAIRS, 128).T
        w[:INTER, PAIRS] = bs
        return w

    f["wg"] = cols(a["L1_ffn_Wg"], a["L1_ffn_Wg_s"])
    f["wu"] = cols(a["L1_ffn_Wu"], a["L1_ffn_Wu_s"])
    wd = np.zeros((128, UNITS, 128), np.float32)
    wd[:, :PAIRS] = a["L1_ffn_Wd"].reshape(PAIRS, 128, 128).transpose(1, 0, 2)
    wd[:INTER, PAIRS] = a["L1_ffn_Wd_s"]
    f["wd"] = wd
    f["bg"] = column(a["L1_ffn_bg"], a["L1_ffn_bg_s"])
    f["bu"] = column(a["L1_ffn_bu"], a["L1_ffn_bu_s"])
    f["bd"] = np.concatenate([a["L1_ffn_bd"], a["L1_ffn_bd_s"].reshape(1, -1)])
    f["wr"] = c(a["L1_ffn_Wr"])
    f["br"] = c(a["L1_ffn_br"])
    return f


def kernel(**inputs):
    import concourse.bacc as _bacc
    from concourse import mybir as _mybir
    from concourse.bass_utils import run_bass_kernel_spmd as _run

    nc = _bacc.Bacc("TRN2", target_bir_lowering=False, num_devices=1)
    arrays = layout(inputs)
    io = {}
    for name, a in arrays.items():
        io[name] = nc.dram_tensor(name + "_dram", a.shape, _mybir.dt.from_np(a.dtype), kind="ExternalInput").ap()
    io["out"] = nc.dram_tensor("out_dram", (16, 256, 128), F32, kind="ExternalOutput").ap()
    program(nc, io)
    r = _run(nc, [{name + "_dram": a for name, a in arrays.items()}], core_ids=[0])
    return r.results[0]["out_dram"]
```

```python
import concourse.bass as bass
from concourse import mybir
from contextlib import ExitStack

F32 = mybir.dt.float32
F16 = mybir.dt.float16
ALU = mybir.AluOpType
ACT = mybir.ActivationFunctionType
AX = mybir.AxisListType

P = 128
BATCH, SEQ, DIM = 16, 256, 128
TILES = BATCH * SEQ // P
TPB = SEQ // P
HEADS, HD = 16, 8
LANES = 4
GROUPS = HEADS // LANES
KEEP = int(SEQ * 0.4)
RRANK = 32
LORA = 16
EXPERTS, TOPK, INTER = 32, 8, 64
PAIRS = EXPERTS // 2
EPS = 1e-5
NEG = -3.0e38
MASKED = 60000.0
SCORE_SCALE = HD ** -0.5
WS = 32.0
ROW_MASK, ROW_MAX = 24, 25
UNITS = PAIRS + 1
TPS = 4
WIDE = TPS * P
SUPERS = TILES // TPS
RING = 4
LAG = 3
NBATCH_R = P // HEADS


def wait(eng, sem, n):
    if isinstance(n, int) and n <= 0:
        return
    eng.wait_ge(sem, n)


def program(nc, io, stages=99):
    ctx = ExitStack()
    with ctx:
        def sb(name, shape, dt=F32):
            return ctx.enter_context(nc.sbuf_tensor(name, shape, dt))

        def sem(name):
            return ctx.enter_context(nc.semaphore(name))

        X = sb("X", [P, TILES, DIM])
        mean = sb("mean", [P, TILES])
        var_eps = sb("var_eps", [P, TILES])
        rstd = sb("rstd", [P, TILES])
        minus_half = sb("minus_half", [P, TILES])
        bnst = sb("bnst", [P, 4, 6])
        bnmv = sb("bnmv", [P, 4, 2])
        ident = sb("ident", [P, P])
        ones_row = sb("ones_row", [1, P])
        PS = ctx.enter_context(nc.psum_tensor("PS", [P, 8, 512], F32))

        ffn0_wT = sb("ffn0_wT", [P, DIM])
        ffn0_vT = sb("ffn0_vT", [RRANK, DIM])
        ffn0_cT = sb("ffn0_cT", [RRANK, DIM])
        ffn0_b = sb("ffn0_b", [1, DIM])
        ffn0_eff = sb("ffn0_eff", [P, DIM])

        xn = sb("xn", [P, 2, 4, DIM])
        xT = sb("xT", [P, 2, SEQ])

        r_w1T = sb("r_w1T", [P, RRANK])
        r_b1 = sb("r_b1", [RRANK, 1])
        r_w2pad = sb("r_w2pad", [RRANK, 2 * P - HEADS])
        r_b2 = sb("r_b2", [P, 1])
        h1 = sb("h1", [RRANK, 2, SEQ])
        z = sb("z", [P, 2, SEQ])
        top8 = sb("top8", [P, 2, 8])
        dropped = sb("dropped", [P, 2, SEQ], F16)
        dropped_dram = nc.dram_tensor("dropped_scratch", (BATCH * HEADS, SEQ), F16, kind="Internal").ap()

        w_wide = sb("w_wide", [P, 2, PAIRS, WIDE])

        a_wqT = sb("a_wqT", [P, 2, DIM])
        a_wkT = sb("a_wkT", [P, 2, DIM])
        a_wvT = sb("a_wvT", [P, 2, DIM])
        a_woT = sb("a_woT", [P, DIM])
        a_qk_bias = sb("a_qk_bias", [P, 2, 2])
        a_v_bias = sb("a_v_bias", [1, DIM])
        a_bo = sb("a_bo", [1, DIM])
        lora_raw = sb("lora_raw", [P, 4, DIM])
        lora_a = sb("lora_a", [LORA, 4, DIM])
        lora_bT = sb("lora_bT", [LORA, 4, DIM])
        sel = sb("sel", [P, 4, GROUPS, P], F16)
        sel_drop = sb("sel_drop", [HEADS, GROUPS, P], F16)
        lane_bias = sb("lane_bias", [P, 2])
        ident16 = sb("ident16", [P, P], F16)
        qk_nat = sb("qk_nat", [P, 2, 2, SEQ], F16)
        stacks = sb("stacks", [P, 4 * GROUPS * SEQ], F16)
        qs, ks = (stacks[:, i * 2 * GROUPS * SEQ:(i + 1) * 2 * GROUPS * SEQ].rearrange(
            "p (b v q) -> p b v q", b=2, v=GROUPS) for i in range(2))
        k_lanes_flat = w_wide[:, 1, :, :].bitcast(F16)[:, 0:8, :].rearrange("p a b -> p (a b)")
        k_lanes = k_lanes_flat.rearrange("p (b v j q) -> p b v j q", b=2, v=GROUPS, j=LANES)
        drop_row = sb("drop_row", [HEADS, 2, SEQ], F16)
        mz = sb("mz", [P, TPB, GROUPS, P], F16)
        vp = sb("vp", [P, 2, TPB, HEADS, 32])
        probs = sb("probs", [P, 2 * LANES, TPB, SEQ])
        o_sb = sb("o_sb", [P, 2, SEQ])
        rec = sb("rec", [P, 2, TPB, LANES])
        att = sb("att", [P, 2, TPB, DIM])
        attT = sb("attT", [P, SEQ])

        wg_hi = sb("wg_hi", [P, UNITS, P], F16)
        wg_lo = sb("wg_lo", [P, UNITS, P], F16)
        wu_hi = sb("wu_hi", [P, UNITS, P], F16)
        wu_lo = sb("wu_lo", [P, UNITS, P], F16)
        wd_hi = sb("wd_hi", [P, UNITS, P], F16)
        wd_lo = sb("wd_lo", [P, UNITS, P], F16)
        wr_raw = sb("wr_raw", [P, EXPERTS])
        wr = sb("wr", [P, 2, EXPERTS], F16)
        m_bg = sb("m_bg", [P, UNITS])
        m_bu = sb("m_bu", [P, UNITS])
        m_bd = sb("m_bd", [EXPERTS + 1, DIM])
        m_br = sb("m_br", [P, EXPERTS])
        x_hi = sb("x_hi", [P, 2, WIDE], F16)
        x_lo = sb("x_lo", [P, 2, WIDE], F16)
        logits = sb("logits", [P, TPS, EXPERTS])
        ranked = sb("ranked", [P, TPS, EXPERTS])
        aff = sb("aff", [P, TPS, EXPERTS])
        best = sb("best", [P, TPS, TOPK])
        wsum = sb("wsum", [P, TPS])
        w_tok = sb("w_tok", [P, TPS, EXPERTS])
        wT = sb("wT", [EXPERTS + 1, 2, WIDE])
        w_dram = nc.dram_tensor("w_scratch", (SUPERS, EXPERTS, WIDE), F32, kind="Internal").ap()
        gate_pair = probs[:].rearrange("p (i r) t q -> p i r (t q)", i=2)
        gate = gate_pair[:, 0, :, :]
        gw = gate_pair[:, 1, :, :]
        gate_shared = lora_raw[0:INTER].rearrange("p i c -> p (i c)")
        hid = sb("hid", [P, RING + 1, WIDE])
        hid_hi = sb("hid_hi", [P, RING + 1, WIDE], F16)
        hid_lo = stacks[:, 0:(RING + 1) * WIDE].rearrange("p (r q) -> p r q", r=RING + 1)
        downT = z[:].rearrange("p h k -> p (h k)")

        x_dram = io["x"].rearrange("b (t p) h -> p (b t) h", p=P)
        out_dram = io["out"].rearrange("b (t p) h -> p (b t) h", p=P)

        s_load = sem("s_load")
        s_late = sem("s_late")
        s_x = sem("s_x")
        s_out = sem("s_out")
        s_vzero = sem("s_vzero")
        s_const = sem("s_const")
        s_stat = sem("s_stat")
        s_rstd = sem("s_rstd")
        s_xn = sem("s_xn")
        s_xnT_ps = sem("s_xnT_ps")
        s_xT = sem("s_xT")
        s_ffn = sem("s_ffn")
        s_xup = sem("s_xup")
        s_eff_ps = sem("s_eff_ps")
        s_eff = sem("s_eff")
        s_h1_ps = sem("s_h1_ps")
        s_h1 = sem("s_h1")
        s_z_ps = sem("s_z_ps")
        s_z = sem("s_z")
        s_top = [sem("s_top0"), sem("s_top1")]
        s_taken = [sem("s_taken0"), sem("s_taken1")]
        s_drop = sem("s_drop")
        s_drop_out = sem("s_drop_out")
        s_drop_in = [sem("s_drop_in0"), sem("s_drop_in1")]
        s_lora_ps = sem("s_lora_ps")
        s_lora = sem("s_lora")
        s_qk_ps = sem("s_qk_ps")
        s_hi = sem("s_hi")
        s_lo = sem("s_lo")
        s_v_ps = sem("s_v_ps")
        s_v = sem("s_v")
        s_stack_ps = sem("s_stack_ps")
        s_kst = sem("s_kst")
        s_qst = sem("s_qst")
        s_km = [sem("s_km0"), sem("s_km1")]
        s_km0 = sem("s_km_zero")
        s_s1 = sem("s_s1")
        s_max = sem("s_max")
        s_mT = sem("s_mT")
        s_madd = sem("s_madd")
        s_s2 = sem("s_s2")
        s_exp = sem("s_exp")
        s_av = sem("s_av")
        s_o = sem("s_o")
        s_oT = sem("s_oT")
        s_rec = sem("s_rec")
        s_norm = sem("s_norm")
        s_att0 = sem("s_att0")
        s_aT_ps = sem("s_aT_ps")
        s_aT = sem("s_aT")
        s_proj = sem("s_proj")
        s_att1 = sem("s_att1")
        s_split = sem("s_split")
        s_split_lo = sem("s_split_lo")
        s_wl = sem("s_wl")
        s_xps = sem("s_xps")
        s_xap = sem("s_xap")
        s_xhi = sem("s_xhi")
        s_xlo = sem("s_xlo")
        s_lg_ps = sem("s_lg_ps")
        s_lg = sem("s_lg")
        s_th = sem("s_th")
        s_aff = sem("s_aff")
        s_rank = sem("s_rank")
        s_wv = sem("s_wv")
        s_ws = sem("s_ws")
        s_w = sem("s_w")
        s_wT_ps = sem("s_wT_ps")
        s_wT = sem("s_wT")
        s_wst = [sem("s_wst0"), sem("s_wst1")]
        s_wide = [[sem(f"s_wide{i}{q}") for q in range(4)] for i in range(2)]
        s_g = sem("s_g")
        s_u = sem("s_u")
        s_silu = sem("s_silu")
        s_gw = sem("s_gw")
        s_hid = sem("s_hid")
        s_hhi = sem("s_hhi")
        s_hlo = sem("s_hlo")
        s_down = sem("s_down")
        s_dsum = sem("s_dsum")
        s_dT = sem("s_dT")
        s_dT_ps = sem("s_dT_ps")
        s_mup = sem("s_mup")

        def stats(dve, tile0, n):
            dve.drain()
            for t in range(n):
                nc.vector.bn_stats(bnst[:, t, :], X[:, tile0 + t, :])
            dve.drain()
            for t in range(n):
                nc.vector.bn_aggr(bnmv[:, t, :], bnst[:, t, :])
            dve.drain()
            nc.vector.tensor_copy(mean[:, bass.ds(tile0, n)], bnmv[:, 0:n, 0])
            nc.vector.tensor_scalar(var_eps[:, bass.ds(tile0, n)], bnmv[:, 0:n, 1], EPS, None,
                                    ALU.add).then_inc(s_stat, 1)

        def rstds(pool, tile0, n, g):
            pool.wait_ge(s_stat, g + 1)
            nc.gpsimd.tensor_tensor(rstd[:, bass.ds(tile0, n)], var_eps[:, bass.ds(tile0, n)],
                                    minus_half[:, 0:n], ALU.pow).then_inc(s_rstd, 1)

        with nc.Block() as block:
            table = [(ident, io["ident"]), (ffn0_wT, io["ffn0_wT"]), (ffn0_vT, io["ffn0_vT"]),
                     (ffn0_cT, io["ffn0_cT"]), (ffn0_b, io["ffn0_b"])]
            late = [(r_w1T, io["r_w1T"]), (r_b1, io["r_b1"]), (r_b2, io["r_b2"]),
                    (r_w2pad[:, P - HEADS:P], io["r_w2T"]),
                    (a_wqT[:, 0, :], io["qkv_wT"][:, 0:DIM]), (a_wkT[:, 0, :], io["qkv_wT"][:, DIM:2 * DIM]),
                    (a_wvT[:, 0, :], io["qkv_wT"][:, 2 * DIM:3 * DIM]), (a_qk_bias[:, 0, :], io["qk_bias"]),
                    (a_v_bias, io["v_bias"]), (a_bo, io["bo"]), (lora_raw, io["lora_w"]),
                    (lora_a, io["lora_a"]), (lora_bT, io["lora_bT"]), (sel, io["sel"]),
                    (sel_drop, io["sel_drop"]), (lane_bias, io["lane_bias"]), (ident16, io["ident16"])]

            @block.sync
            def _(sp):
                sp.dma_start(X[:, :, :], x_dram).then_inc(s_x, 16)
                for dst, src in table:
                    sp.dma_start(dst[:], src).then_inc(s_load, 16)
                sp.wait_ge(s_const, 3)
                for dst, src in late:
                    sp.dma_start(dst[:] if dst.shape == src.shape else dst[:], src).then_inc(s_late, 16)

            @block.gpsimd
            def _(pool):
                nc.gpsimd.memset(minus_half[:], -0.5).then_inc(s_const, 1)
                nc.gpsimd.memset(vp[:], 0.0).then_inc(s_vzero, 1)
                nc.gpsimd.memset(mz[:], 0.0).then_inc(s_vzero, 1)
                nc.gpsimd.memset(a_qk_bias[:, 1, :], 0.0).then_inc(s_vzero, 1)
                pool.wait_ge(s_vzero, 1)
                nc.gpsimd.memset(vp[:, :, :, :, HD:HD + 1], 1.0).then_inc(s_vzero, 1)
                for s in (s_att0, s_aT_ps, s_dT, s_dT_ps, s_proj):
                    pool.sem_inc(s, 1)
                pool.wait_ge(s_const, 1)
                with pool.Fori(0, BATCH) as b:
                    rstds(pool, b * TPB, TPB, b)

            @block.vector
            def _(dve):
                nc.vector.memset(ones_row[:], 1.0).then_inc(s_const, 1)
                nc.vector.memset(r_w2pad[:], 0.0).then_inc(s_const, 1)
                dve.wait_ge(s_x, 16)
                with dve.Fori(0, BATCH) as b:
                    stats(dve, b * TPB, TPB)
                dve.wait_ge(s_eff_ps, 1)
                nc.vector.tensor_copy(ffn0_eff[:], PS[:, 0, 0:DIM]).then_inc(s_eff, 1)
                dve.wait_ge(s_lora_ps, 1)
                for i, w in enumerate((a_wqT[:, 1, :], a_wkT[:, 1, :], a_wvT[:, 1, :], a_woT[:])):
                    nc.vector.scalar_tensor_tensor(w, PS[:, 1, i * DIM:(i + 1) * DIM], 1.0 / LORA,
                                                   lora_raw[:, i, :], ALU.mult, ALU.add).then_inc(s_lora, 1)

            @block.tensor
            def _(pe):
                pe.wait_ge(s_load, 16 * len(table))
                nc.tensor.matmul(PS[:, 0, 0:DIM], ffn0_vT[:], ffn0_cT[:], start=True, stop=False)
                nc.tensor.matmul(PS[:, 0, 0:DIM], ident[:], ffn0_wT[:], start=False,
                                 stop=True).then_inc(s_eff_ps, 1)
                pe.wait_ge(s_late, 16 * len(late))
                for i in range(4):
                    last = nc.tensor.matmul(PS[:, 1, i * DIM:(i + 1) * DIM], lora_a[:, i, :], lora_bT[:, i, :],
                                            start=True, stop=True)
                last.then_inc(s_lora_ps, 1)

        with nc.Block() as block:
            raw = w_wide[:, 0, :, :].rearrange("p a b -> p (a b)")
            size = UNITS * P
            raws = [raw[:, i * size:(i + 1) * size].rearrange("p (u c) -> p u c", u=UNITS) for i in range(3)]
            his, los = (wg_hi, wu_hi, wd_hi), (wg_lo, wu_lo, wd_lo)

            @block.sync
            def _(sp):
                for dst, name in zip(raws, ("wg", "wu", "wd")):
                    sp.dma_start(dst, io[name]).then_inc(s_wl, 16)
                for dst, name in ((wr_raw, "wr"), (m_bg, "bg"), (m_bu, "bu"), (m_bd, "bd")):
                    sp.dma_start(dst[:], io[name]).then_inc(s_wl, 16)
                sp.dma_start(m_br[:], io["br"].partition_broadcast(P)).then_inc(s_wl, 16)

            @block.gpsimd
            def _(pool):
                nc.gpsimd.memset(wT[EXPERTS:EXPERTS + 1, :, :], 1.0).then_inc(s_vzero, 1)

            @block.scalar
            def _(act):
                act.wait_ge(s_wl, 8 * 16)
                for hi, w in zip(his, raws):
                    nc.scalar.mul(hi[:], w, WS).then_inc(s_split, 1)
                nc.scalar.copy(wr[:, 0, :], wr_raw[:]).then_inc(s_split, 1)

            @block.vector
            def _(dve):
                dve.wait_ge(s_wl, 8 * 16)
                nc.vector.tensor_scalar(m_bu[:], m_bu[:], WS, None, ALU.mult).then_inc(s_split_lo, 1)
                nc.vector.tensor_scalar(m_bd[:], m_bd[:], WS * WS, None, ALU.mult).then_inc(s_split_lo, 1)
                for i, (hi, lo, w) in enumerate(zip(his, los, raws)):
                    dve.wait_ge(s_split, i + 1)
                    nc.vector.scalar_tensor_tensor(lo[:], w, WS, hi[:], ALU.mult, ALU.subtract).then_inc(s_split_lo, 1)
                dve.wait_ge(s_split, 4)
                nc.vector.tensor_tensor(wr[:, 1, :], wr_raw[:], wr[:, 0, :], ALU.subtract).then_inc(s_split_lo, 1)

        n_ln = [0]
        n_st = [BATCH]

        def ffn0(first):
            g0, st0, ln0 = first, n_st[0], n_ln[0]

            def transpose_step(pe, b, par):
                g = ln0 + b
                pe.wait_ge(s_xn, g + 1)
                wait(pe, s_xT, g - 1)
                for t in range(TPB):
                    last = nc.tensor.transpose(PS[:, par, t * P:(t + 1) * P], xn[:, par, t, :], ident[:])
                last.then_inc(s_xnT_ps, 1)

            def product_step(pe, b, par):
                g = ln0 + b
                pe.wait_ge(s_xT, g + 1)
                wait(pe, s_xup, g0 + b - 1)
                for t in range(TPB):
                    o = PS[:, 2 + par, t * DIM:(t + 1) * DIM]
                    nc.tensor.matmul(o, xT[:, par, t * P:(t + 1) * P], ffn0_eff[:], start=True, stop=False)
                    last = nc.tensor.matmul(o, ones_row[:], ffn0_b[:], start=False, stop=True)
                last.then_inc(s_ffn, 1)

            def apply_step(dve, b, par):
                wait(dve, s_xnT_ps, ln0 + b - 1)
                for t in range(TPB):
                    T = b * TPB + t
                    last = nc.vector.tensor_scalar(xn[:, par, t, :], X[:, T, :], mean[:, bass.ds(T, 1)],
                                                   rstd[:, bass.ds(T, 1)], ALU.subtract, ALU.mult)
                last.then_inc(s_xn, 1)

            def update_step(dve, b, par):
                dve.wait_ge(s_ffn, g0 + b + 1)
                x2 = X[:, bass.ds(b * TPB, TPB), :]
                nc.vector.scalar_tensor_tensor(x2, PS[:, 2 + par, 0:SEQ].rearrange("p (t h) -> p t h", t=TPB),
                                               0.5, x2, ALU.mult, ALU.add).then_inc(s_xup, 1)
                stats(dve, b * TPB, TPB)

            def copy_step(act, b, par):
                g = ln0 + b
                act.wait_ge(s_xnT_ps, g + 1)
                wait(act, s_ffn, g0 + b - 1)
                nc.scalar.copy(xT[:, par, :], PS[:, par, 0:SEQ]).then_inc(s_xT, 1)

            with nc.Block() as block:
                @block.vector
                def _(dve):
                    dve.wait_ge(s_rstd, st0)
                    for b in range(2):
                        apply_step(dve, b, b)
                    with dve.Fori(0, BATCH // 2 - 1) as two:
                        for par in range(2):
                            apply_step(dve, two * 2 + (par + 2), par)
                            update_step(dve, two * 2 + par, par)
                    for b in range(BATCH - 2, BATCH):
                        update_step(dve, b, b % 2)

                @block.tensor
                def _(pe):
                    for b in range(2):
                        transpose_step(pe, b, b)
                    for b in range(2):
                        product_step(pe, b, b)
                        transpose_step(pe, b + 2, b)
                    with pe.Fori(1, BATCH // 2 - 1) as two:
                        for par in range(2):
                            product_step(pe, two * 2 + par, par)
                            transpose_step(pe, two * 2 + (par + 2), par)
                    for b in range(BATCH - 2, BATCH):
                        product_step(pe, b, b % 2)

                @block.scalar
                def _(act):
                    for b in range(2):
                        copy_step(act, b, b)
                    with act.Fori(1, BATCH // 2) as two:
                        for par in range(2):
                            copy_step(act, two * 2 + par, par)

                @block.gpsimd
                def _(pool):
                    with pool.Fori(0, BATCH) as b:
                        rstds(pool, b * TPB, TPB, st0 + b)
            n_st[0] += BATCH
            n_ln[0] += BATCH

        ffn0(0)

        def apply_ln(dve, b, par, g):
            wait(dve, s_xnT_ps, g - 1)
            for t in range(TPB):
                T = b * TPB + t
                last = nc.vector.tensor_scalar(xn[:, par, t, :], X[:, T, :], mean[:, bass.ds(T, 1)],
                                               rstd[:, bass.ds(T, 1)], ALU.subtract, ALU.mult)
            last.then_inc(s_xn, 1)

        def transpose_ln(pe, bank, par, g):
            pe.wait_ge(s_xn, g + 1)
            for t in range(TPB):
                last = nc.tensor.transpose(PS[:, bank, t * P:(t + 1) * P], xn[:, par, t, :], ident[:])
            last.then_inc(s_xnT_ps, 1)

        def router0():
            st0, ln0 = n_st[0], n_ln[0]
            half_rows = BATCH // 2

            def transposes(pe, b):
                wait(pe, s_xT, ln0 + b - 1)
                transpose_ln(pe, b % 2, b % 2, ln0 + b)

            def hidden(pe, b):
                pe.wait_ge(s_xT, ln0 + b + 1)
                wait(pe, s_h1, b - 1)
                nc.tensor.matmul(PS[0:RRANK, 2 + b % 2, 0:SEQ], r_w1T[:], xT[:, b % 2, :], start=True,
                                 stop=True).then_inc(s_h1_ps, 1)

            def scores(pe, b):
                half, i = divmod(b, half_rows)
                pe.wait_ge(s_h1, b + 1)
                col = P - HEADS - HEADS * i
                nc.tensor.matmul(PS[:, 4 + half, 0:SEQ], r_w2pad[:, col:col + P], h1[:, b % 2, :],
                                 start=(i == 0), stop=(i == half_rows - 1)).then_inc(s_z_ps, 1)

            with nc.Block() as block:
                @block.vector
                def _(dve):
                    dve.wait_ge(s_rstd, st0)
                    with dve.Fori(0, BATCH // 2) as two:
                        for par in range(2):
                            apply_ln(dve, two * 2 + par, par, two * 2 + (par + ln0))
                    full, rest = divmod(KEEP, 8)
                    dve.wait_ge(s_z, 2)
                    for r in range(full):
                        for h in range(2):
                            wait(dve, s_taken[h], r)
                            nc.vector.max(top8[:, h, :], z[:, h, :]).then_inc(s_top[h], 1)
                        for h in range(2):
                            dve.wait_ge(s_top[h], r + 1)
                            nc.vector.match_replace(z[:, h, :], top8[:, h, :], z[:, h, :],
                                                    NEG).then_inc(s_taken[h], 1)
                    for h in range(2):
                        dve.wait_ge(s_taken[h], full)
                        nc.vector.max(top8[:, h, :], z[:, h, :]).then_inc(s_top[h], 1)
                    for h in range(2):
                        dve.wait_ge(s_top[h], full + 1)
                        nc.vector.memset(top8[:, h, rest:8], NEG).then_inc(s_top[h], 1)
                    for h in range(2):
                        dve.wait_ge(s_top[h], full + 2)
                        nc.vector.match_replace(z[:, h, :], top8[:, h, :], z[:, h, :],
                                                NEG).then_inc(s_taken[h], 1)
                    for h in range(2):
                        dve.wait_ge(s_taken[h], full + 1)
                        nc.vector.tensor_scalar(dropped[:, h, :], z[:, h, :], NEG, -MASKED, ALU.is_gt,
                                                ALU.mult).then_inc(s_drop, 1)

                @block.tensor
                def _(pe):
                    transposes(pe, 0)
                    for b in range(BATCH):
                        if b + 1 < BATCH:
                            transposes(pe, b + 1)
                        hidden(pe, b)
                        if b >= 1:
                            scores(pe, b - 1)
                    scores(pe, BATCH - 1)

                @block.scalar
                def _(act):
                    def copy_xT(b):
                        act.wait_ge(s_xnT_ps, ln0 + b + 1)
                        wait(act, s_h1_ps, b - 1)
                        nc.scalar.copy(xT[:, b % 2, :], PS[:, b % 2, 0:SEQ]).then_inc(s_xT, 1)

                    def rectify(act, b):
                        act.wait_ge(s_h1_ps, b + 1)
                        wait(act, s_z_ps, b - 1)
                        nc.scalar.activation(h1[:, b % 2, :], PS[0:RRANK, 2 + b % 2, 0:SEQ], ACT.Relu,
                                             bias=r_b1[:, 0:1]).then_inc(s_h1, 1)

                    for b in range(BATCH):
                        copy_xT(b)
                        if b >= 1:
                            rectify(act, b - 1)
                    rectify(act, BATCH - 1)
                    for h in range(2):
                        act.wait_ge(s_z_ps, (h + 1) * half_rows)
                        nc.scalar.activation(z[:, h, :], PS[:, 4 + h, 0:SEQ], ACT.Identity,
                                             bias=r_b2[:, 0:1]).then_inc(s_z, 1)

                @block.sync
                def _(sp):
                    sp.wait_ge(s_drop, 2)
                    sp.dma_start(dropped_dram.rearrange("(h p) k -> p h k", p=P),
                                 dropped[:, :, :]).then_inc(s_drop_out, 16)
                    sp.wait_ge(s_drop_out, 16)
            n_ln[0] += BATCH

        def attention(layer):
            st0, ln0, a0 = n_st[0], n_ln[0], layer * BATCH
            S1, S2, OB, MB = 0, 2, 4, 6
            masked = layer == 0
            K0, K1, Q0, Q1 = range(4)

            def spread(n, par):
                return (n - par + 2) * 32 + layer * BATCH * 32

            def pe_qk(pe, n, par):
                pe.wait_ge(s_xT, ln0 + n + 1)
                for i, w in enumerate((a_wqT, a_wkT)):
                    last = nc.tensor.matmul(PS[:, MB + 1, i * SEQ:(i + 1) * SEQ], w[:, layer, :], xT[:, par, :],
                                            start=True, stop=True)
                last.then_inc(s_qk_ps, 1)

            def pe_v(pe, n, par):
                pe.wait_ge(s_qst, 2 * (a0 + n) + 1)
                for t in range(TPB):
                    o = PS[:, MB, t * DIM:(t + 1) * DIM]
                    last = nc.tensor.matmul(o, xT[:, par, t * P:(t + 1) * P], a_wvT[:, layer, :], start=True,
                                            stop=not masked)
                    if masked:
                        last = nc.tensor.matmul(o, ones_row[:], a_v_bias[:], start=False, stop=True)
                last.then_inc(s_v_ps, 1)

            def pe_stack(pe, n, par, piece):
                is_k, half = piece in (K0, K1), piece % 2
                src = 1 if is_k else 0
                dropping = masked and is_k
                if piece == K0:
                    pe.wait_ge(s_lo, a0 + n + 1)
                    if masked:
                        pe.wait_ge(s_drop_in[par], (n - par) * 8 + 16)
                if piece in (Q0, Q1):
                    pe.wait_ge(s_kst, 2 * (a0 + n) + half + 1)
                for i in range(2):
                    v = 2 * half + i
                    o = PS[:, MB + half, i * SEQ:(i + 1) * SEQ]
                    nc.tensor.matmul(o, sel[:, 2 * src, v, :], qk_nat[:, 0, src, :], start=True, stop=False)
                    last = nc.tensor.matmul(o, sel[:, 2 * src + 1, v, :], qk_nat[:, 1, src, :], start=False,
                                            stop=not dropping)
                    if dropping:
                        last = nc.tensor.matmul(o, sel_drop[:, v, :], drop_row[:, par, :], start=False, stop=True)
                last.then_inc(s_stack_ps, 1)

            def pe_s1(pe, n, par, h):
                u = (a0 + n) * HEADS + h
                v, j = divmod(h, LANES)
                if h == 0:
                    pe.wait_ge(s_qst, 2 * (a0 + n) + 1)
                    pe.wait_ge(s_km[par], spread(n, par))
                    wait(pe, s_madd, a0 + n)
                if h == 1:
                    wait(pe, s_norm, 4 * (a0 + n - 1))
                if h == HEADS // 2:
                    pe.wait_ge(s_qst, 2 * (a0 + n) + 2)
                wait(pe, s_max, u - 1)
                for t in range(TPB):
                    last = nc.tensor.matmul(PS[:, S1 + h % 2, t * SEQ:(t + 1) * SEQ], qs[:, par, v, t * P:(t + 1) * P],
                                            k_lanes[:, par, v, j, :], start=True, stop=True)
                last.then_inc(s_s1, 1)

            def pe_maxT(pe, n):
                pe.wait_ge(s_max, (a0 + n + 1) * HEADS)
                bank = PS[:, S1, :].bitcast(F16)
                for v in range(GROUPS):
                    for t in range(TPB):
                        last = nc.tensor.transpose(bank[:, v * SEQ + t * P:v * SEQ + (t + 1) * P], mz[:, t, v, :],
                                                   ident16[:])
                last.then_inc(s_mT, 1)

            def pe_s2(pe, c, par, h):
                u = (a0 + c) * HEADS + h
                v, j = divmod(h, LANES)
                if h == 0:
                    pe.wait_ge(s_madd, a0 + c + 1)
                wait(pe, s_exp, u - 1)
                for t in range(TPB):
                    last = nc.tensor.matmul(PS[:, S2 + h % 2, t * SEQ:(t + 1) * SEQ],
                                            k_lanes[:, par, v, j, t * P:(t + 1) * P], qs[:, par, v, :],
                                            start=True, stop=True)
                last.then_inc(s_s2, 1)

            def pe_av(pe, c, par, v):
                g = 4 * (a0 + c) + v
                pe.wait_ge(s_exp, 4 * g + 4)
                if v == 0:
                    pe.wait_ge(s_v, a0 + c + 1)
                wait(pe, s_o, g - 1)
                for t in range(TPB):
                    for j in range(LANES):
                        h = LANES * v + j
                        last = nc.tensor.matmul(PS[32 * j:32 * j + 32, OB + v % 2, 0:SEQ], vp[:, par, t, h, :],
                                                probs[:, h % 8, t, :], start=(t == 0), stop=(t == TPB - 1),
                                                skip_group_check=True)
                last.then_inc(s_av, 1)

            def pe_oT(pe, c, v, bank):
                pe.wait_ge(s_o, 4 * (a0 + c) + v + 1)
                for t in range(TPB):
                    last = nc.tensor.transpose(PS[:, bank, t * P:(t + 1) * P], o_sb[:, v % 2, t * P:(t + 1) * P], ident[:])
                last.then_inc(s_oT, 1)

            def pe_attT(pe, o, par):
                pe.wait_ge(s_norm, 4 * (a0 + o) + 4)
                for t in range(TPB):
                    last = nc.tensor.transpose(PS[:, MB + 1, t * P:(t + 1) * P], att[:, par, t, :], ident[:])
                last.then_inc(s_aT_ps, 1)

            def pe_project(pe, o):
                pe.wait_ge(s_aT, o + 1)
                for t in range(TPB):
                    r = PS[:, MB, t * DIM:(t + 1) * DIM]
                    nc.tensor.matmul(r, attT[:, t * P:(t + 1) * P], a_woT[:], start=True, stop=False)
                    last = nc.tensor.matmul(r, ones_row[:], a_bo[:], start=False, stop=True)
                last.then_inc(s_proj, 1)

            def pe_step(pe, n, c, par, has_next, has_ahead, has_cur, has_old):
                cp = 1 - par
                o = c - 1
                st4, g4 = 4 * (a0 + n), 4 * (a0 + c)
                projects = has_old and not masked

                def s2(h):
                    if has_cur:
                        pe_s2(pe, c, cp, h)

                def s1(*hs):
                    if has_next:
                        for h in hs:
                            pe_s1(pe, n, par, h)

                if has_next:
                    pe_stack(pe, n, par, Q0)
                s2(0)
                if has_next:
                    pe_stack(pe, n, par, Q1)
                s2(1)
                if has_next:
                    pe_v(pe, n, par)
                s2(2), s1(0), s2(3), s1(1), s2(4), s1(2)
                if projects:
                    if has_next:
                        pe.wait_ge(s_qst, 2 * (a0 + n) + 2)
                    else:
                        pe.wait_ge(s_norm, g4 - 1)
                    pe_attT(pe, o, par)
                s2(5)
                if has_cur:
                    pe_av(pe, c, cp, 0)
                s1(3)
                if projects:
                    if has_next:
                        pe.wait_ge(s_v, a0 + n + 1)
                    pe_project(pe, o)
                s1(4), s2(6), s1(5)
                if has_cur:
                    if has_next:
                        pe.wait_ge(s_qst, 2 * (a0 + n) + 2)
                    elif masked:
                        pe.wait_ge(s_norm, g4 - 1)
                    if projects:
                        pe.wait_ge(s_aT, c)
                    pe_oT(pe, c, 0, MB + 1)
                s2(7), s1(6), s2(8), s1(7)
                if has_ahead:
                    pe.wait_ge(s_v, a0 + n + 1)
                    if projects:
                        pe.wait_ge(s_att1, c)
                    transpose_ln(pe, MB, cp, ln0 + n + 1)
                s2(9)
                if has_cur:
                    pe_av(pe, c, cp, 1)
                s1(8)
                if has_ahead:
                    if has_cur:
                        pe.wait_ge(s_norm, g4 + 1)
                    else:
                        pe.wait_ge(s_qst, 2 * (a0 + n) + 2)
                    pe_qk(pe, n + 1, cp)
                s2(10), s1(9)
                if has_cur:
                    if has_ahead:
                        pe.wait_ge(s_xT, ln0 + n + 2)
                    elif has_next:
                        pe.wait_ge(s_v, a0 + n + 1)
                    else:
                        pe.wait_ge(s_norm, g4 - 2)
                    if projects:
                        pe.wait_ge(s_att1, c)
                    pe_oT(pe, c, 1, MB)
                s2(11), s1(10), s2(12), s1(11)
                if has_ahead:
                    if has_cur:
                        pe.wait_ge(s_norm, g4 + 2)
                    pe_stack(pe, n + 1, cp, K0)
                s2(13)
                if has_cur:
                    pe_av(pe, c, cp, 2)
                s1(12), s2(14), s1(13)
                if has_cur:
                    if has_ahead:
                        pe.wait_ge(s_lo, a0 + n + 2)
                    else:
                        pe.wait_ge(s_norm, g4 + 1)
                    pe_oT(pe, c, 2, MB + 1)
                s2(15), s1(14, 15)
                if has_ahead:
                    if has_cur:
                        pe.wait_ge(s_norm, g4 + 3)
                    pe_stack(pe, n + 1, cp, K1)
                if has_cur:
                    pe_av(pe, c, cp, 3)
                if has_next:
                    pe_maxT(pe, n)
                if has_cur:
                    pe_oT(pe, c, 3, S1 + 1)

            def act_hi(act, n):
                act.wait_ge(s_qk_ps, a0 + n + 1)
                wait(act, s_stack_ps, 4 * (a0 + n))
                for i in range(2):
                    last = nc.scalar.activation(qk_nat[:, 0, i, :], PS[:, MB + 1, i * SEQ:(i + 1) * SEQ],
                                                ACT.Identity, bias=a_qk_bias[:, layer, i:i + 1])
                last.then_inc(s_hi, 1)

            def act_xT(act, n, par):
                act.wait_ge(s_xnT_ps, ln0 + n + 1)
                wait(act, s_v_ps, a0 + n - 1)
                nc.scalar.copy(xT[:, par, :], PS[:, MB, 0:SEQ]).then_inc(s_xT, 1)

            def act_step(act, n, c, par, has_next, has_ahead, has_cur, has_old):
                cp = 1 - par

                def exps(*hs):
                    if not has_cur:
                        return
                    for h in hs:
                        u = (a0 + c) * HEADS + h
                        act.wait_ge(s_s2, u + 1)
                        if h % LANES == 0:
                            wait(act, s_av, 4 * (a0 + c) + h // LANES - 1)
                        nc.scalar.activation(probs[:, h % 8, :, :], PS[:, S2 + h % 2, :].rearrange("p (t q) -> p t q", t=TPB),
                                             ACT.Exp, scale=SCORE_SCALE).then_inc(s_exp, 1)

                def out_copy(v):
                    if not has_cur:
                        return
                    g = 4 * (a0 + c) + v
                    act.wait_ge(s_av, g + 1)
                    wait(act, s_oT, g - 1)
                    nc.scalar.copy(o_sb[:, v % 2, :], PS[:, OB + v % 2, 0:SEQ]).then_inc(s_o, 1)

                def q_copy(half):
                    if not has_next:
                        return
                    act.wait_ge(s_stack_ps, 4 * (a0 + n) + Q0 + half + 1)
                    if half == 0:
                        wait(act, s_s2, (a0 + n - 1) * HEADS)
                    nc.scalar.activation(qs[:, par, 2 * half:2 * half + 2, :],
                                         PS[:, MB + half, :].rearrange("p (v q) -> p v q", v=2), ACT.Identity,
                                         bias=lane_bias[:, 0:1]).then_inc(s_qst, 1)

                q_copy(0)
                exps(0)
                q_copy(1)
                exps(1)
                if has_next:
                    act.wait_ge(s_v_ps, a0 + n + 1)
                    wait(act, s_av, 4 * (a0 + n - 1))
                    nc.scalar.copy(vp[:, par, :, :, 0:HD],
                                   PS[:, MB, 0:SEQ].rearrange("p (t h d) -> p t h d", t=TPB, h=HEADS)).then_inc(s_v, 1)
                exps(2, 3, 4)
                if has_old and not masked:
                    act.wait_ge(s_aT_ps, c + 1)
                    act.wait_ge(s_proj, c)
                    nc.scalar.copy(attT[:], PS[:, MB + 1, 0:SEQ]).then_inc(s_aT, 1)
                exps(5)
                out_copy(0)
                exps(6, 7, 8)
                if has_ahead:
                    act_xT(act, n + 1, cp)
                exps(9)
                out_copy(1)
                if has_ahead:
                    act_hi(act, n + 1)
                exps(10, 11, 12, 13)
                out_copy(2)
                exps(14, 15)
                out_copy(3)

            def dve_lo(dve, n):
                dve.wait_ge(s_hi, a0 + n + 1)
                for i in range(2):
                    last = nc.vector.scalar_tensor_tensor(
                        qk_nat[:, 1, i, :], PS[:, MB + 1, i * SEQ:(i + 1) * SEQ], a_qk_bias[:, layer, i:i + 1],
                        qk_nat[:, 0, i, :], ALU.add, ALU.subtract)
                last.then_inc(s_lo, 1)

            def k_copy(dve, n, par, half):
                dve.wait_ge(s_stack_ps, 4 * (a0 + n) + half + 1)
                if half == 0:
                    wait(dve, s_km[par], spread(n, par) - 64)
                nc.vector.tensor_scalar(ks[:, par, 2 * half:2 * half + 2, :],
                                        PS[:, MB + half, :].rearrange("p (v q) -> p v q", v=2), lane_bias[:, 1:2],
                                        None, ALU.add).then_inc(s_kst, 1)

            def dve_step(dve, n, c, par, has_next, has_ahead, has_cur, has_old):
                cp = 1 - par
                o = c - 1

                def reduces(*hs):
                    if not has_next:
                        return
                    for h in hs:
                        u = (a0 + n) * HEADS + h
                        v, j = divmod(h, LANES)
                        dve.wait_ge(s_s1, u + 1)
                        if h == 0:
                            wait(dve, s_mT, a0 + n)
                        nc.vector.tensor_reduce(mz[:, :, v, 32 * j + ROW_MAX], PS[:, S1 + h % 2, :].rearrange("p (t k) -> p t k", t=TPB),
                                                AX.X, ALU.max).then_inc(s_max, 1)

                def norm(v):
                    if not has_cur:
                        return
                    g = 4 * (a0 + c) + v
                    bank = (MB + 1, MB, MB + 1, S1 + 1)[v]
                    T = PS[:, bank, 0:SEQ].rearrange("p (t j d) -> p t j d", t=TPB, j=LANES)
                    dve.wait_ge(s_oT, g + 1)
                    wait(dve, s_norm, g - 1)
                    nc.vector.reciprocal(rec[:, v % 2, :, :], T[:, :, :, HD]).then_inc(s_rec, 1)
                    if v == 0:
                        dve.wait_ge(s_att0 if masked else s_aT_ps, c)
                    dve.wait_ge(s_rec, g + 1)
                    r = att[:, cp, :, v * LANES * HD:(v + 1) * LANES * HD].rearrange("p t (j d) -> p t j d", j=LANES)
                    nc.vector.tensor_tensor(r, T[:, :, :, 0:HD],
                                            rec[:, v % 2, :, :].unsqueeze(3).broadcast_to([P, TPB, LANES, HD]),
                                            ALU.mult).then_inc(s_norm, 1)

                if has_old and masked:
                    dve.wait_ge(s_att0, c + 1)
                reduces(0)
                if has_old and masked:
                    stats(dve, o * TPB, TPB)
                reduces(1, 2, 3)
                if has_old and not masked:
                    dve.wait_ge(s_proj, c + 1)
                    x2 = X[:, bass.ds(o * TPB, TPB), :]
                    nc.vector.tensor_tensor(x2, x2, PS[:, MB, 0:SEQ].rearrange("p (t h) -> p t h", t=TPB),
                                            ALU.add).then_inc(s_att1, 1)
                    stats(dve, o * TPB, TPB)
                reduces(4, 5)
                norm(0)
                reduces(6, 7, 8)
                if has_ahead:
                    dve_lo(dve, n + 1)
                reduces(9)
                norm(1)
                reduces(10, 11)
                if has_ahead:
                    k_copy(dve, n + 1, cp, 0)
                reduces(12)
                if has_ahead and not (isinstance(n, int) and n + 2 >= BATCH):
                    apply_ln(dve, n + 2, par, ln0 + n + 2)
                reduces(13)
                norm(2)
                reduces(14, 15)
                if has_ahead:
                    k_copy(dve, n + 1, cp, 1)
                if has_next:
                    dve.wait_ge(s_mT, a0 + n + 1)
                    m = PS[:, S1, :].bitcast(F16).rearrange("p (v q) -> p v q", v=GROUPS)
                    nc.vector.tensor_tensor(qs[:, par, :, :], qs[:, par, :, :], m, ALU.add).then_inc(s_madd, 1)
                norm(3)

            def run(step, engine):
                step(0, -1, 0, True, True, False, False)
                step(1, 0, 1, True, True, True, False)
                with engine.Fori(1, BATCH // 2 - 1) as two:
                    for par in range(2):
                        step(two * 2 + par, two * 2 + (par - 1), par, True, True, True, True)
                step(BATCH - 2, BATCH - 3, 0, True, True, True, True)
                step(BATCH - 1, BATCH - 2, 1, True, False, True, True)
                step(BATCH, BATCH - 1, 0, False, False, True, True)
                step(BATCH + 1, BATCH, 1, False, False, False, True)

            with nc.Block() as block:
                @block.tensor
                def _(pe):
                    transpose_ln(pe, MB, 0, ln0)
                    pe_qk(pe, 0, 0)
                    pe_stack(pe, 0, 0, K0), pe_stack(pe, 0, 0, K1)
                    run(lambda *a: pe_step(pe, *a), pe)

                @block.scalar
                def _(act):
                    act_xT(act, 0, 0)
                    act_hi(act, 0)
                    run(lambda *a: act_step(act, *a), act)

                @block.vector
                def _(dve):
                    dve.wait_ge(s_rstd, st0)
                    apply_ln(dve, 0, 0, ln0)
                    apply_ln(dve, 1, 1, ln0 + 1)
                    nc.vector.memset(k_lanes_flat, 0.0).then_inc(s_km0, 1)
                    dve_lo(dve, 0)
                    k_copy(dve, 0, 0, 0), k_copy(dve, 0, 0, 1)
                    run(lambda *a: dve_step(dve, *a), dve)

                @block.gpsimd
                def _(pool):
                    def pool_sum(pool, b, par):
                        pool.wait_ge(s_norm, 4 * (a0 + b) + 4)
                        x2 = X[:, bass.ds(b * TPB, TPB), :]
                        nc.gpsimd.tensor_tensor(x2, x2, att[:, par, :, :], ALU.add).then_inc(s_att0, 1)

                    if masked:
                        pool_sum(pool, 0, 0)
                        pool_sum(pool, 1, 1)
                        with pool.Fori(1, BATCH // 2) as two:
                            for par in range(2):
                                rstds(pool, (two * 2 + (par - 2)) * TPB, TPB, two * 2 + (par - 2 + st0))
                                pool_sum(pool, two * 2 + par, par)
                        for b in range(BATCH - 2, BATCH):
                            rstds(pool, b * TPB, TPB, st0 + b)
                    else:
                        with pool.Fori(0, BATCH) as b:
                            rstds(pool, b * TPB, TPB, b + st0)

                @block.sync
                def _(sp):
                    def load(b, par):
                        wait(sp, s_stack_ps, 4 * (a0 + b - 1))
                        sp.dma_start(drop_row[:, par, :], dropped_dram[bass.ds(b * HEADS, HEADS), :])\
                            .then_inc(s_drop_in[par], 16)

                    def spread_k(b, par):
                        wait(sp, s_s2, (a0 + b - 1) * HEADS)
                        sp.wait_ge(s_kst, 2 * (a0 + b) + 2)
                        for j in range(LANES):
                            lane = slice(32 * j, 32 * j + 32)
                            sp.dma_start(k_lanes[lane, par, :, j, :], ks[lane, par, :, :]).then_inc(s_km[par], 16)

                    if masked:
                        load(0, 0), load(1, 1)
                    sp.wait_ge(s_km0, layer + 1)
                    spread_k(0, 0), spread_k(1, 1)
                    with sp.Fori(1, BATCH // 2) as two:
                        for par in range(2):
                            if masked:
                                load(two * 2 + par, par)
                            spread_k(two * 2 + par, par)
            n_st[0] += BATCH
            n_ln[0] += BATCH

        def experts(turn):
            st0, m0 = n_st[0], turn * SUPERS

            def pe_prep_x(pe, n, par):
                g = m0 + n
                pe.wait_ge(s_xap, g + 1)
                wait(pe, s_wT, g)
                for t in range(TPS):
                    last = nc.tensor.transpose(PS[:, 6, t * P:(t + 1) * P], xn[:, par, t, :], ident[:])
                last.then_inc(s_xps, 1)

            def pe_logits(pe, n, par):
                g = m0 + n
                pe.wait_ge(s_xlo, g + 1)
                wait(pe, s_mup, g - 1)
                for t in range(TPS):
                    o = PS[:, 7, t * EXPERTS:(t + 1) * EXPERTS]
                    parts = [(a, b) for a in (x_hi, x_lo) for b in range(2)]
                    for i, (a, b) in enumerate(parts):
                        last = nc.tensor.matmul(o, a[:, par, t * P:(t + 1) * P], wr[:, b, :], start=(i == 0),
                                                stop=(i == len(parts) - 1))
                last.then_inc(s_lg_ps, 1)

            def pe_wT(pe, n):
                pe.wait_ge(s_w, m0 + n + 1)
                for t in range(TPS):
                    last = nc.tensor.transpose(PS[0:EXPERTS, 6, t * P:(t + 1) * P], w_tok[:, t, :], ident[:])
                last.then_inc(s_wT_ps, 1)

            def rows(k):
                return (INTER, PAIRS) if k == 0 else (P, k - 1)

            def pe_unit(pe, c, par, k):
                u = (m0 + c) * UNITS + k
                bank = (par + k) % 2
                m, e = rows(k)
                if k == 0:
                    pe.wait_ge(s_xlo, m0 + c + 1)
                for ready, free, lo_bank, hi_w, lo_w in ((s_g, s_silu, 0, wg_hi, wg_lo), (s_u, s_hid, 2, wu_hi, wu_lo)):
                    wait(pe, free, u - 1)
                    o = PS[0:m, lo_bank + bank, :]
                    nc.tensor.matmul(o, hi_w[:, e, 0:m], x_hi[:, par, :], start=True, stop=False)
                    nc.tensor.matmul(o, hi_w[:, e, 0:m], x_lo[:, par, :], start=False, stop=False)
                    nc.tensor.matmul(o, lo_w[:, e, 0:m], x_hi[:, par, :], start=False, stop=True).then_inc(ready, 1)

            def pe_down(pe, c, par, k):
                u = (m0 + c) * UNITS + k
                m, e = rows(k)
                r = slot(k)
                pe.wait_ge(s_hlo, u + 1)
                if k == 0:
                    pe.wait_ge(s_dT, m0 + c)
                o = PS[:, 4 + par, :]
                nc.tensor.matmul(o, wd_hi[0:m, e, :], hid_hi[0:m, r, :], start=(k == 0), stop=False)
                nc.tensor.matmul(o, wd_hi[0:m, e, :], hid_lo[0:m, r, :], start=False, stop=False)
                nc.tensor.matmul(o, wd_lo[0:m, e, :], hid_hi[0:m, r, :], start=False, stop=False).then_inc(s_down, 1)

            def slot(k):
                return RING if k == 0 else (k - 1) % RING

            def pe_biases(pe, o, par):
                nc.tensor.matmul(PS[:, 4 + par, :], m_bd[:], wT[:, par, :], start=False, stop=True).then_inc(s_dsum, 1)

            def pe_dT(pe, o):
                pe.wait_ge(s_dT, m0 + o + 2)
                for t in range(TPS):
                    last = nc.tensor.transpose(PS[:, 7, t * P:(t + 1) * P], downT[:, t * P:(t + 1) * P], ident[:])
                last.then_inc(s_dT_ps, 1)

            def pe_step(pe, n, c, o, par, has_next, has_cur, has_old):
                cp = 1 - par
                for k in range(UNITS):
                    if has_cur:
                        pe_unit(pe, c, cp, k)
                    if has_next and k == 0:
                        pe_prep_x(pe, n, par)
                    if k < LAG:
                        if has_old:
                            pe_down(pe, o, par, UNITS - LAG + k)
                    elif has_cur:
                        pe_down(pe, c, cp, k - LAG)
                    if k == LAG and has_old:
                        pe_biases(pe, o, par)
                    if k == LAG + 1 and has_old:
                        pe_dT(pe, o)
                    if k == LAG + 2 and has_next:
                        pe_logits(pe, n, par)
                    if k == LAG + 8 and has_next:
                        pe_wT(pe, n)

            def act_step(act, n, c, o, par, has_next, has_cur, has_old):
                cp = 1 - par

                def high(c_, p_, k):
                    u = (m0 + c_) * UNITS + k
                    m, _ = rows(k)
                    act.wait_ge(s_hid, u + 1)
                    wait(act, s_down, u - RING + 1)
                    nc.scalar.copy(hid_hi[0:m, slot(k), :], hid[0:m, slot(k), :]).then_inc(s_hhi, 1)

                for k in range(UNITS):
                    if has_cur:
                        u = (m0 + c) * UNITS + k
                        m, e = rows(k)
                        act.wait_ge(s_g, u + 1)
                        wait(act, s_hid, u - RING + 1)
                        nc.scalar.activation(gate_shared if k == 0 else gate[:, slot(k), :], PS[0:m, (cp + k) % 2, :], ACT.Silu,
                                             bias=m_bg[0:m, e:e + 1], scale=1.0 / WS).then_inc(s_silu, 1)
                        if k >= 1:
                            high(c, cp, k - 1)
                    if k == 0 and has_old:
                        high(o, par, UNITS - 1)
                    if k == 1 and has_next:
                        act.wait_ge(s_xps, m0 + n + 1)
                        nc.scalar.copy(x_hi[:, par, :], PS[:, 6, :]).then_inc(s_xhi, 1)
                    if k == LAG and has_old:
                        act.wait_ge(s_dsum, m0 + o + 1)
                        act.wait_ge(s_dT_ps, m0 + o + 1)
                        nc.scalar.copy(downT, PS[:, 4 + par, :]).then_inc(s_dT, 1)
                    if k == LAG + 3 and has_next:
                        act.wait_ge(s_lg, m0 + n + 1)
                        nc.scalar.activation(aff[:], logits[:], ACT.Tanh, scale=0.5).then_inc(s_th, 1)
                    if k == LAG + 8 and has_next:
                        act.wait_ge(s_wT_ps, m0 + n + 1)
                        wait(act, s_wst[par], (n - par) * 8)
                        wait(act, s_dsum, m0 + n - 1)
                        nc.scalar.copy(wT[0:EXPERTS, par, :], PS[0:EXPERTS, 6, :]).then_inc(s_wT, 1)

            def dve_step(dve, n, c, o, par, has_next, has_cur, has_old):
                cp = 1 - par
                g = m0 + n

                def low(c_, p_, k):
                    u = (m0 + c_) * UNITS + k
                    m, _ = rows(k)
                    r = slot(k)
                    dve.wait_ge(s_hhi, u + 1)
                    nc.vector.tensor_tensor(hid_lo[0:m, r, :], hid[0:m, r, :], hid_hi[0:m, r, :],
                                            ALU.subtract).then_inc(s_hlo, 1)

                for k in range(UNITS):
                    if has_cur:
                        u = (m0 + c) * UNITS + k
                        m, e = rows(k)
                        r = slot(k)
                        dve.wait_ge(s_u, u + 1)
                        if k == 0:
                            dve.wait_ge(s_silu, u + 1)
                        else:
                            dve.wait_ge(s_gw, (m0 + c) * PAIRS + k)
                        wait(dve, s_hlo, u - RING + 1)
                        nc.vector.scalar_tensor_tensor(hid[0:m, r, :], PS[0:m, 2 + (cp + k) % 2, :], m_bu[0:m, e:e + 1],
                                                       gate_shared if k == 0 else gw[:, r, :], ALU.add,
                                                       ALU.mult).then_inc(s_hid, 1)
                        if k >= 1:
                            low(c, cp, k - 1)
                    if k == 0 and has_old:
                        low(o, par, UNITS - 1)
                    if k == 1 and has_next:
                        dve.wait_ge(s_xhi, g + 1)
                        nc.vector.tensor_tensor(x_lo[:, par, :], PS[:, 6, :], x_hi[:, par, :],
                                                ALU.subtract).then_inc(s_xlo, 1)
                    if k == LAG + 1 and has_old:
                        dve.wait_ge(s_dT_ps, m0 + o + 2)
                        x4 = X[:, bass.ds(o * TPS, TPS), :]
                        nc.vector.scalar_tensor_tensor(x4, PS[:, 7, :].rearrange("p (t h) -> p t h", t=TPS),
                                                       0.5 / (WS * WS), x4, ALU.mult, ALU.add).then_inc(s_mup, 1)
                    if k == LAG + 2:
                        if has_next:
                            dve.wait_ge(s_lg_ps, g + 1)
                            nc.vector.tensor_tensor(logits[:], PS[:, 7, 0:TPS * EXPERTS].rearrange("p (t e) -> p t e", t=TPS),
                                                    m_br[:].unsqueeze(1).broadcast_to([P, TPS, EXPERTS]),
                                                    ALU.add).then_inc(s_lg, 1)
                        if has_old and turn == 0:
                            stats(dve, o * TPS, TPS)
                    if has_next and k == LAG + 3:
                        dve.drain()
                        for t in range(TPS):
                            nc.vector.max(best[:, t, :], logits[:, t, :])
                    if has_next and k == LAG + 4:
                        dve.drain()
                        for t in range(TPS):
                            last = nc.vector.match_replace(ranked[:, t, :], best[:, t, :], logits[:, t, :], NEG)
                        last.then_inc(s_rank, 1)
                        dve.wait_ge(s_th, g + 1)
                        nc.vector.tensor_scalar(aff[:], aff[:], 0.5, 0.5, ALU.mult, ALU.add).then_inc(s_aff, 1)
                    if has_next and k == LAG + 5:
                        dve.wait_ge(s_rank, g + 1)
                        dve.wait_ge(s_aff, g + 1)
                        nc.vector.scalar_tensor_tensor(ranked[:], ranked[:], NEG, aff[:], ALU.is_le,
                                                       ALU.mult).then_inc(s_wv, 1)
                    if has_next and k == LAG + 6:
                        dve.wait_ge(s_wv, g + 1)
                        nc.vector.tensor_reduce(wsum[:], ranked[:], AX.X, ALU.add).then_inc(s_ws, 1)
                        dve.wait_ge(s_ws, 3 * g + 1)
                        nc.vector.tensor_scalar(wsum[:], wsum[:], 1e-9, None, ALU.add).then_inc(s_ws, 1)
                    if has_next and k == LAG + 7:
                        dve.wait_ge(s_ws, 3 * g + 2)
                        nc.vector.reciprocal(wsum[:], wsum[:]).then_inc(s_ws, 1)
                        dve.wait_ge(s_ws, 3 * g + 3)
                        wait(dve, s_wT_ps, g)
                        nc.vector.tensor_tensor(w_tok[:], ranked[:], wsum[:].unsqueeze(2).broadcast_to([P, TPS, EXPERTS]),
                                                ALU.mult).then_inc(s_w, 1)
                    if has_next and k == UNITS - 3 and not (isinstance(n, int) and n + 1 >= SUPERS):
                        apply_wide(dve, n + 1, cp)

            def apply_wide(dve, n, par):
                wait(dve, s_xps, m0 + n - 1)
                for t in range(TPS):
                    T = n * TPS + t
                    last = nc.vector.tensor_scalar(xn[:, par, t, :], X[:, T, :], mean[:, bass.ds(T, 1)],
                                                   rstd[:, bass.ds(T, 1)], ALU.subtract, ALU.mult)
                last.then_inc(s_xap, 1)

            def pool_step(pool, n, c, o, par, has_next, has_cur, has_old):
                cp = 1 - par
                for k in range(1, UNITS):
                    if has_cur:
                        u = (m0 + c) * UNITS + k
                        pool.wait_ge(s_silu, u + 1)
                        if (k - 1) % 4 == 0:
                            pool.wait_ge(s_wide[cp][(k - 1) // 4], (turn * SUPERS + (c - cp) + 2) * 16)
                        wait(pool, s_hid, u - RING + 1)
                        nc.gpsimd.tensor_tensor(gw[:, slot(k), :], gate[:, slot(k), :], w_wide[:, cp, k - 1, :],
                                                ALU.mult).then_inc(s_gw, 1)
                    if k == LAG + 3 and has_old and turn == 0:
                        rstds(pool, o * TPS, TPS, st0 + o)

            def sp_step(sp, n, par):
                sp.wait_ge(s_wT, m0 + n + 1)
                done = (turn * SUPERS + (n - par) + 2) * 8
                sp.dma_start(w_dram[bass.ds(n, 1), :, :].rearrange("a e t -> (a e) t"), wT[0:EXPERTS, par, :])\
                    .then_inc(s_wst[par], 16)
                sp.wait_ge(s_wst[par], done)
                rows_of = w_dram[bass.ds(n, 1), :, :].rearrange("a (k e) t -> e (a k) t", e=2)
                for q in range(4):
                    wait(sp, s_gw, (m0 + n - 2) * PAIRS + 4 * q + 4)
                    for e in range(2):
                        sp.dma_start(w_wide[64 * e:64 * e + 64, par, 4 * q:4 * q + 4, :],
                                     rows_of[e, 4 * q:4 * q + 4, :].partition_broadcast(INTER))\
                            .then_inc(s_wide[par][q], 16)

            def run(step, engine):
                step(0, -1, -2, 0, True, False, False)
                step(1, 0, -1, 1, True, True, False)
                with engine.Fori(1, SUPERS // 2 - 1) as two:
                    for par in range(2):
                        step(two * 2 + par, two * 2 + (par - 1), two * 2 + (par - 2), par, True, True, True)
                for n in range(SUPERS - 2, SUPERS):
                    step(n, n - 1, n - 2, n % 2, True, True, True)
                step(SUPERS, SUPERS - 1, SUPERS - 2, 0, False, True, True)
                step(SUPERS + 1, SUPERS, SUPERS - 1, 1, False, False, True)

            with nc.Block() as block:
                @block.tensor
                def _(pe):
                    run(lambda *a: pe_step(pe, *a), pe)

                @block.scalar
                def _(act):
                    run(lambda *a: act_step(act, *a), act)

                @block.vector
                def _(dve):
                    dve.wait_ge(s_rstd, st0)
                    apply_wide(dve, 0, 0)
                    run(lambda *a: dve_step(dve, *a), dve)

                @block.gpsimd
                def _(pool):
                    run(lambda *a: pool_step(pool, *a), pool)

                @block.sync
                def _(sp):
                    for n in range(2):
                        sp_step(sp, n, n)
                    with sp.Fori(1, SUPERS // 2) as two:
                        for par in range(2):
                            sp_step(sp, two * 2 + par, par)
            if turn == 0:
                n_st[0] += SUPERS

        if stages >= 2:
            router0()
            attention(0)
        if stages >= 3:
            ffn0(BATCH)
        if stages >= 4:
            experts(0)
        if stages >= 5:
            attention(1)
        if stages >= 6:
            experts(1)

        with nc.Block() as block:
            @block.sync
            def _(sp):
                sp.dma_start(out_dram, X[:, :, :]).then_inc(s_out, 16)
                sp.wait_ge(s_out, 16)


def layout(inp):
    import numpy as np
    c = np.ascontiguousarray
    a = {k: np.asarray(v) for k, v in inp.items()}
    f = {}
    f["x"] = c(a["L0_attn_hidden_states"])
    f["ident"] = np.eye(128, dtype=np.float32)
    f["ffn0_wT"] = c(a["L0_ffn_W"].T)
    f["ffn0_vT"] = c(a["L0_ffn_V_r"].T)
    f["ffn0_cT"] = c(a["L0_ffn_C"].T)
    f["ffn0_b"] = c(a["L0_ffn_b"].reshape(1, -1))
    w = a["L0_attn_qkv_w"]
    f["qkv_wT"] = c(w.T)
    f["qk_bias"] = c(a["L0_attn_qkv_b"].reshape(3, 128)[0:2].T)
    f["v_bias"] = c(a["L0_attn_qkv_b"].reshape(3, 128)[2:3])
    f["r_w1T"] = c(a["L0_attn_r_w1"].T)
    f["r_b1"] = c(a["L0_attn_r_b1"].reshape(-1, 1))
    f["r_w2T"] = c(a["L0_attn_r_w2"].T)
    f["r_b2"] = c(np.tile(a["L0_attn_r_b2"], 8).reshape(-1, 1))
    f["bo"] = c(a["L1_attn_bo"].reshape(1, -1))
    f["lora_w"] = c(np.stack([a["L1_attn_W" + k].T for k in "qkvo"], 1))
    f["lora_a"] = c(np.stack([a["L1_attn_A" + k] for k in "qkvo"], 1))
    f["lora_bT"] = c(np.stack([a["L1_attn_B" + k].T for k in "qkvo"], 1))
    sel = np.zeros((128, 4, GROUPS, 128), np.float16)
    drop = np.zeros((HEADS, GROUPS, 128), np.float16)
    lane = np.zeros((128, 2), np.float32)
    for v in range(GROUPS):
        for j in range(LANES):
            drop[v * LANES + j, v, 32 * j + ROW_MASK] = 1
            for d in range(HD):
                src = (v * LANES + j) * HD + d
                for copy, (q, k) in enumerate(((0, 2), (1, 2), (0, 3))):
                    sel[src, q, v, 32 * j + copy * HD + d] = 1
                    sel[src, k, v, 32 * j + copy * HD + d] = 1
    lane[ROW_MASK::32, 0] = MASKED
    lane[ROW_MAX::32, 1] = -1.0
    f["sel"], f["sel_drop"], f["lane_bias"] = sel, drop, lane
    f["ident16"] = np.eye(128, dtype=np.float16)
    def cols(we, ws):
        w = np.zeros((128, UNITS, 128), np.float32)
        w[:, :PAIRS] = we.transpose(1, 0, 2).reshape(128, PAIRS, 128)
        w[:, PAIRS, :INTER] = ws
        return w

    def column(be, bs):
        w = np.zeros((128, UNITS), np.float32)
        w[:, :PAIRS] = be.reshape(PAIRS, 128).T
        w[:INTER, PAIRS] = bs
        return w

    f["wg"] = cols(a["L1_ffn_Wg"], a["L1_ffn_Wg_s"])
    f["wu"] = cols(a["L1_ffn_Wu"], a["L1_ffn_Wu_s"])
    wd = np.zeros((128, UNITS, 128), np.float32)
    wd[:, :PAIRS] = a["L1_ffn_Wd"].reshape(PAIRS, 128, 128).transpose(1, 0, 2)
    wd[:INTER, PAIRS] = a["L1_ffn_Wd_s"]
    f["wd"] = wd
    f["bg"] = column(a["L1_ffn_bg"], a["L1_ffn_bg_s"])
    f["bu"] = column(a["L1_ffn_bu"], a["L1_ffn_bu_s"])
    f["bd"] = np.concatenate([a["L1_ffn_bd"], a["L1_ffn_bd_s"].reshape(1, -1)])
    f["wr"] = c(a["L1_ffn_Wr"])
    f["br"] = c(a["L1_ffn_br"])
    return f


def kernel(**inputs):
    import concourse.bacc as _bacc
    from concourse import mybir as _mybir
    from concourse.bass_utils import run_bass_kernel_spmd as _run

    nc = _bacc.Bacc("TRN2", target_bir_lowering=False, num_devices=1)
    arrays = layout(inputs)
    io = {}
    for name, a in arrays.items():
        io[name] = nc.dram_tensor(name + "_dram", a.shape, _mybir.dt.from_np(a.dtype), kind="ExternalInput").ap()
    io["out"] = nc.dram_tensor("out_dram", (16, 256, 128), F32, kind="ExternalOutput").ap()
    program(nc, io)
    r = _run(nc, [{name + "_dram": a for name, a in arrays.items()}], core_ids=[0])
    return r.results[0]["out_dram"]
```

```python
import concourse.bass as bass
from concourse import mybir
from contextlib import ExitStack

F32 = mybir.dt.float32
F16 = mybir.dt.float16
ALU = mybir.AluOpType
ACT = mybir.ActivationFunctionType
AX = mybir.AxisListType

P = 128
BATCH, SEQ, DIM = 16, 256, 128
TILES = BATCH * SEQ // P
TPB = SEQ // P
HEADS, HD = 16, 8
LANES = 4
GROUPS = HEADS // LANES
KEEP = int(SEQ * 0.4)
RRANK = 32
LORA = 16
EXPERTS, TOPK, INTER = 32, 8, 64
PAIRS = EXPERTS // 2
EPS = 1e-5
NEG = -3.0e38
MASKED = 60000.0
SCORE_SCALE = HD ** -0.5
WS = 32.0
ROW_MASK, ROW_MAX = 24, 25
UNITS = PAIRS + 1
TPS = 4
WIDE = TPS * P
SUPERS = TILES // TPS
RING = 4
LAG = 3
LO_ROW = 32
B_FFN, B_V, B_O = range(3)
HALF_LAG = 4


def wait(eng, sem, n):
    if isinstance(n, int) and n <= 0:
        return
    eng.wait_ge(sem, n)


def program(nc, io):
    ctx = ExitStack()
    with ctx:
        def sb(name, shape, dt=F32):
            return ctx.enter_context(nc.sbuf_tensor(name, shape, dt))

        def sem(name):
            return ctx.enter_context(nc.semaphore(name))

        X = sb("X", [P, TILES, DIM])
        moments = sb("moments", [P, TILES, 2])
        var_eps = sb("var_eps", [P, 4, TPS])
        rstd = sb("rstd", [P, TILES])
        minus_half = sb("minus_half", [P, TPS])
        epsilon = sb("epsilon", [P, TPS])
        bnst = sb("bnst", [P, 4, 6])
        bnmv = sb("bnmv", [P, 4, 2])
        ident = sb("ident", [P, P])
        ones16 = sb("ones16", [LO_ROW + 1, P], F16)
        biases = sb("biases", [LO_ROW + 1, 3, DIM], F16)
        PS = ctx.enter_context(nc.psum_tensor("PS", [P, 8, 512], F32))

        ffn0_wT = sb("ffn0_wT", [P, DIM])
        ffn0_vT = sb("ffn0_vT", [RRANK, DIM])
        ffn0_cT = sb("ffn0_cT", [RRANK, DIM])
        ffn0_eff = sb("ffn0_eff", [P, DIM])

        xn = sb("xn", [P, 2, 4, DIM])
        xT = sb("xT", [P, 2, SEQ])

        r_w1T = sb("r_w1T", [P, RRANK])
        r_b1 = sb("r_b1", [RRANK, 1])
        r_w2pad = sb("r_w2pad", [RRANK, 2 * P - HEADS])
        r_b2 = sb("r_b2", [P, 1])
        h1 = sb("h1", [RRANK, 2, SEQ])
        z = sb("z", [P, 2, SEQ])
        top8 = sb("top8", [P, 2, 8])
        dropped = sb("dropped", [P, 2, SEQ], F16)
        dropped_dram = nc.dram_tensor("dropped_scratch", (BATCH * HEADS, SEQ), F16, kind="Internal").ap()

        w_wide = sb("w_wide", [P, 2, PAIRS, WIDE])

        a_wqT = sb("a_wqT", [P, 2, DIM])
        a_wkT = sb("a_wkT", [P, 2, DIM])
        a_wvT = sb("a_wvT", [P, 2, DIM])
        a_woT = sb("a_woT", [P, DIM])
        a_qk_bias = sb("a_qk_bias", [P, 2, 2])
        lora_raw = sb("lora_raw", [P, 4, DIM])
        lora_a = sb("lora_a", [LORA, 4, DIM])
        lora_bT = sb("lora_bT", [LORA, 4, DIM])
        sel = sb("sel", [P, 4, GROUPS, P], F16)
        sel_drop = sb("sel_drop", [HEADS, GROUPS, P], F16)
        lane_bias = sb("lane_bias", [P, 2])
        ident16 = sb("ident16", [P, P], F16)
        qk_nat = sb("qk_nat", [P, 2, 2, SEQ], F16)
        stacks = sb("stacks", [P, 4 * GROUPS * SEQ], F16)
        qs, ks = (stacks[:, i * 2 * GROUPS * SEQ:(i + 1) * 2 * GROUPS * SEQ].rearrange(
            "p (b v q) -> p b v q", b=2, v=GROUPS) for i in range(2))
        k_lanes_flat = w_wide[:, 1, :, :].bitcast(F16)[:, 0:8, :].rearrange("p a b -> p (a b)")
        k_lanes = k_lanes_flat.rearrange("p (b v j q) -> p b v j q", b=2, v=GROUPS, j=LANES)
        drop_row = sb("drop_row", [HEADS, 2, SEQ], F16)
        mz = sb("mz", [P, TPB, GROUPS, P], F16)
        vp = sb("vp", [P, 2, TPB, HEADS, 32])
        probs = sb("probs", [P, 2 * LANES, TPB, SEQ])
        o_sb = sb("o_sb", [P, 2, SEQ])
        rec = sb("rec", [P, 2, TPB, LANES])
        att = sb("att", [P, 2, TPB, DIM])
        attT = sb("attT", [P, SEQ])

        wg_hi = sb("wg_hi", [P, UNITS, P], F16)
        wg_lo = sb("wg_lo", [P, UNITS, P], F16)
        wu_hi = sb("wu_hi", [P, UNITS, P], F16)
        wu_lo = sb("wu_lo", [P, UNITS, P], F16)
        wd_hi = sb("wd_hi", [P, UNITS, P], F16)
        wd_lo = sb("wd_lo", [P, UNITS, P], F16)
        wr_raw = sb("wr_raw", [P, EXPERTS])
        wr = sb("wr", [P, 2, EXPERTS], F16)
        m_bg = sb("m_bg", [P, UNITS])
        m_bu = sb("m_bu", [P, UNITS])
        m_bd = sb("m_bd", [EXPERTS + 1, DIM])
        m_br = sb("m_br", [P, EXPERTS])
        x_hi = sb("x_hi", [P, 2, WIDE], F16)
        x_lo = sb("x_lo", [P, 2, WIDE], F16)
        logits = sb("logits", [P, TPS, EXPERTS])
        ranked = sb("ranked", [P, TPS, EXPERTS])
        aff = sb("aff", [P, TPS, EXPERTS])
        best = sb("best", [P, TPS, TOPK])
        wsum = sb("wsum", [P, TPS])
        w_tok = sb("w_tok", [P, TPS, EXPERTS])
        wT = sb("wT", [EXPERTS + 1, 2, WIDE])
        w_dram = nc.dram_tensor("w_scratch", (SUPERS, EXPERTS, WIDE), F32, kind="Internal").ap()
        gate_pair = probs[:].rearrange("p (i r) t q -> p i r (t q)", i=2)
        gate = gate_pair[:, 0, :, :]
        gw = gate_pair[:, 1, :, :]
        gate_shared = lora_raw[0:INTER].rearrange("p i c -> p (i c)")
        hid = sb("hid", [P, RING + 1, WIDE])
        hid_hi = sb("hid_hi", [P, RING + 1, WIDE], F16)
        hid_lo = stacks[:, 0:(RING + 1) * WIDE].rearrange("p (r q) -> p r q", r=RING + 1)
        downT = z[:].rearrange("p h k -> p (h k)")

        x_dram = io["x"].rearrange("b (t p) h -> p (b t) h", p=P)
        out_dram = io["out"].rearrange("b (t p) h -> p (b t) h", p=P)

        s_load = sem("s_load")
        s_rload = sem("s_rload")
        s_eps = sem("s_eps")
        s_late = sem("s_late")
        s_x = [sem(f"s_x{i}") for i in range(3)]
        s_out = sem("s_out")
        s_vzero = sem("s_vzero")
        s_const = sem("s_const")
        s_stat = sem("s_stat")
        s_veps = sem("s_veps")
        s_rstd = sem("s_rstd")
        s_first = [sem("s_stat_x"), sem("s_veps_x"), sem("s_rstd_x")]
        s_rxn = sem("s_rxn")
        s_rxnT_ps = sem("s_rxnT_ps")
        s_rxT = sem("s_rxT")
        s_bias = sem("s_bias")
        s_bias_in = sem("s_bias_in")
        s_scaled = sem("s_scaled")
        s_xn = sem("s_xn")
        s_xnT_ps = sem("s_xnT_ps")
        s_xT = sem("s_xT")
        s_ffn = sem("s_ffn")
        s_xup = sem("s_xup")
        s_eff_ps = sem("s_eff_ps")
        s_eff = sem("s_eff")
        s_h1_ps = sem("s_h1_ps")
        s_h1 = sem("s_h1")
        s_z_ps = sem("s_z_ps")
        s_z = sem("s_z")
        s_top = [sem("s_top0"), sem("s_top1")]
        s_taken = [sem("s_taken0"), sem("s_taken1")]
        s_drop = sem("s_drop")
        s_drop_out = sem("s_drop_out")
        s_drop_in = [sem("s_drop_in0"), sem("s_drop_in1")]
        s_lora_ps = sem("s_lora_ps")
        s_lora = sem("s_lora")
        s_qk_ps = sem("s_qk_ps")
        s_hi = sem("s_hi")
        s_lo = sem("s_lo")
        s_v_ps = sem("s_v_ps")
        s_v = sem("s_v")
        s_stack_ps = sem("s_stack_ps")
        s_kst = sem("s_kst")
        s_qst = sem("s_qst")
        s_km = [[sem(f"s_km{h}{i}") for i in range(2)] for h in range(2)]
        s_km0 = sem("s_km_zero")
        s_s1 = sem("s_s1")
        s_max = sem("s_max")
        s_mT = sem("s_mT")
        s_madd = sem("s_madd")
        s_s2 = sem("s_s2")
        s_exp = sem("s_exp")
        s_av = sem("s_av")
        s_o = sem("s_o")
        s_oT = sem("s_oT")
        s_rec = sem("s_rec")
        s_norm = sem("s_norm")
        s_att0 = sem("s_att0")
        s_aT_ps = sem("s_aT_ps")
        s_aT = sem("s_aT")
        s_proj = sem("s_proj")
        s_att1 = sem("s_att1")
        s_split = sem("s_split")
        s_split_lo = sem("s_split_lo")
        s_wl = sem("s_wl")
        s_xps = sem("s_xps")
        s_xap = sem("s_xap")
        s_xhi = sem("s_xhi")
        s_xlo = sem("s_xlo")
        s_lg_ps = sem("s_lg_ps")
        s_lg = sem("s_lg")
        s_th = sem("s_th")
        s_aff = sem("s_aff")
        s_rank = sem("s_rank")
        s_wv = sem("s_wv")
        s_ws = sem("s_ws")
        s_w = sem("s_w")
        s_wT_ps = sem("s_wT_ps")
        s_wT = sem("s_wT")
        s_wst = [sem("s_wst0"), sem("s_wst1")]
        s_wide = [[sem(f"s_wide{i}{q}") for q in range(4)] for i in range(2)]
        s_g = sem("s_g")
        s_u = sem("s_u")
        s_silu = sem("s_silu")
        s_gw = sem("s_gw")
        s_hid = sem("s_hid")
        s_hhi = sem("s_hhi")
        s_hlo = sem("s_hlo")
        s_down = sem("s_down")
        s_dsum = sem("s_dsum")
        s_dT = sem("s_dT")
        s_dT_ps = sem("s_dT_ps")
        s_mup = sem("s_mup")

        def stats(dve, tile0, n, done=s_stat):
            dve.drain()
            for t in range(n):
                nc.vector.bn_stats(bnst[:, t, :], X[:, tile0 + t, :])
            dve.drain()
            for t in range(n):
                nc.vector.bn_aggr(bnmv[:, t, :], bnst[:, t, :])
            dve.drain()
            nc.vector.tensor_copy(moments[:, bass.ds(tile0, n), :], bnmv[:, 0:n, :]).then_inc(done, 1)

        def rstds(pool, tile0, n, g, par, counts=(s_stat, s_veps, s_rstd)):
            moments_known, eps_added, done = counts
            pool.wait_ge(moments_known, g + 1)
            nc.gpsimd.tensor_tensor(var_eps[:, par, 0:n], moments[:, bass.ds(tile0, n), 1], epsilon[:, 0:n],
                                    ALU.add).then_inc(eps_added, 1)
            pool.wait_ge(eps_added, g + 1)
            nc.gpsimd.tensor_tensor(rstd[:, bass.ds(tile0, n)], var_eps[:, par, 0:n],
                                    minus_half[:, 0:n], ALU.pow).then_inc(done, 1)

        def zero_lanes(engine):
            engine.memset(w_wide[:, 1, 0:PAIRS // 2, :], 0.0).then_inc(s_km0, 1)

        early = [(ident, io["ident"]), (ffn0_wT, io["ffn0_wT"]), (ffn0_vT, io["ffn0_vT"]), (ffn0_cT, io["ffn0_cT"])]
        router_table = [(r_w1T, io["r_w1T"]), (r_b1, io["r_b1"]), (r_b2, io["r_b2"]),
                        (r_w2pad[:, P - HEADS:P], io["r_w2T"])]
        late = [(a_wqT[:, 0, :], io["qkv_wT"][:, 0:DIM]), (a_wkT[:, 0, :], io["qkv_wT"][:, DIM:2 * DIM]),
                (a_wvT[:, 0, :], io["qkv_wT"][:, 2 * DIM:3 * DIM]), (a_qk_bias[:, 0, :], io["qk_bias"]),
                (lora_raw, io["lora_w"]), (lora_a, io["lora_a"]), (lora_bT, io["lora_bT"]), (sel, io["sel"]),
                (sel_drop, io["sel_drop"]), (lane_bias, io["lane_bias"]), (ident16, io["ident16"])]
        raw = w_wide[:, 0, :, :].rearrange("p a b -> p (a b)")
        size = UNITS * P

        def apply_ln(dve, b, par, g):
            wait(dve, s_xnT_ps, g - 1)
            for t in range(TPB):
                T = b * TPB + t
                last = nc.vector.tensor_scalar(xn[:, par, t, :], X[:, T, :], moments[:, bass.ds(T, 1), 0],
                                               rstd[:, bass.ds(T, 1)], ALU.subtract, ALU.mult)
            last.then_inc(s_xn, 1)

        def transpose_ln(pe, bank, par, g):
            pe.wait_ge(s_xn, g + 1)
            for t in range(TPB):
                last = nc.tensor.transpose(PS[:, bank, t * P:(t + 1) * P], xn[:, par, t, :], ident[:])
            last.then_inc(s_xnT_ps, 1)

        def apply_wide(dve, n, par, before):
            wait(dve, s_xps, before + n - 1)
            for t in range(TPS):
                T = n * TPS + t
                last = nc.vector.tensor_scalar(xn[:, par, t, :], X[:, T, :], moments[:, bass.ds(T, 1), 0],
                                               rstd[:, bass.ds(T, 1)], ALU.subtract, ALU.mult)
            last.then_inc(s_xap, 1)

        X_BANK = 6

        def wide_transposes(pe, n, par, before):
            g = before + n
            pe.wait_ge(s_xap, g + 1)
            wait(pe, s_wT, g)
            for t in range(TPS):
                last = nc.tensor.transpose(PS[:, X_BANK, t * P:(t + 1) * P], xn[:, par, t, :], ident[:])
            last.then_inc(s_xps, 1)

        def wide_high(act, n, par, before):
            act.wait_ge(s_xps, before + n + 1)
            nc.scalar.copy(x_hi[:, par, :], PS[:, X_BANK, :]).then_inc(s_xhi, 1)

        def wide_low(dve, n, par, before):
            dve.wait_ge(s_xhi, before + n + 1)
            nc.vector.tensor_tensor(x_lo[:, par, :], PS[:, X_BANK, :], x_hi[:, par, :],
                                    ALU.subtract).then_inc(s_xlo, 1)

        def first_rows(dve, ln0, st, wide_done=0):
            dve.wait_ge(s_rstd, st)
            wait(dve, s_xps, wide_done)
            for b in range(2):
                apply_ln(dve, b, b, ln0 + b)

        def first_wide(dve, before, st, ln_done):
            dve.wait_ge(s_rstd, st)
            dve.wait_ge(s_xnT_ps, ln_done)
            apply_wide(dve, 0, 0, before)

        n_ln = [BATCH]
        n_st = [BATCH]

        def ffn0():
            g0, st0, ln0 = BATCH, n_st[0], n_ln[0]

            def transpose_step(pe, b, par):
                g = ln0 + b
                pe.wait_ge(s_xn, g + 1)
                wait(pe, s_xT, g - 1)
                for t in range(TPB):
                    last = nc.tensor.transpose(PS[:, par, t * P:(t + 1) * P], xn[:, par, t, :], ident[:])
                last.then_inc(s_xnT_ps, 1)

            def product_step(pe, b, par):
                g = ln0 + b
                pe.wait_ge(s_xT, g + 1)
                wait(pe, s_xup, g0 + b - 1)
                for t in range(TPB):
                    o = PS[:, 2 + par, t * DIM:(t + 1) * DIM]
                    nc.tensor.matmul(o, xT[:, par, t * P:(t + 1) * P], ffn0_eff[:], start=True, stop=False)
                    last = nc.tensor.matmul(o, ones16[:], biases[:, B_FFN, :], start=False, stop=True)
                last.then_inc(s_ffn, 1)

            def update_step(dve, b, par):
                dve.wait_ge(s_ffn, g0 + b + 1)
                x2 = X[:, bass.ds(b * TPB, TPB), :]
                nc.vector.scalar_tensor_tensor(x2, PS[:, 2 + par, 0:SEQ].rearrange("p (t h) -> p t h", t=TPB),
                                               0.5, x2, ALU.mult, ALU.add).then_inc(s_xup, 1)
                stats(dve, b * TPB, TPB)

            def copy_step(act, b, par):
                g = ln0 + b
                act.wait_ge(s_xnT_ps, g + 1)
                wait(act, s_ffn, g0 + b - 1)
                nc.scalar.copy(xT[:, par, :], PS[:, par, 0:SEQ]).then_inc(s_xT, 1)

            with nc.Block() as block:
                @block.vector
                def _(dve):
                    dve.wait_ge(s_rstd, st0)
                    for b in range(BATCH):
                        if b + 2 < BATCH:
                            apply_ln(dve, b + 2, b % 2, ln0 + b + 2)
                        if b == BATCH - 1:
                            first_wide(dve, 0, st0 + 2, ln0 + BATCH)
                        update_step(dve, b, b % 2)
                    wide_low(dve, 0, 0, 0)

                @block.tensor
                def _(pe):
                    for b in range(2):
                        transpose_step(pe, b, b)
                    for b in range(2):
                        product_step(pe, b, b)
                        transpose_step(pe, b + 2, b)
                    with pe.Fori(1, BATCH // 2 - 1) as two:
                        for par in range(2):
                            product_step(pe, two * 2 + par, par)
                            transpose_step(pe, two * 2 + (par + 2), par)
                    for b in range(BATCH - 2, BATCH):
                        product_step(pe, b, b % 2)
                    wide_transposes(pe, 0, 0, 0)

                @block.scalar
                def _(act):
                    for b in range(2):
                        copy_step(act, b, b)
                    with act.Fori(1, BATCH // 2) as two:
                        for par in range(2):
                            copy_step(act, two * 2 + par, par)
                    wide_high(act, 0, 0, 0)

                @block.gpsimd
                def _(pool):
                    with pool.Fori(0, BATCH // 2) as two:
                        for par in range(2):
                            rstds(pool, (two * 2 + par) * TPB, TPB, two * 2 + (par + st0), par)
            n_st[0] += BATCH
            n_ln[0] += BATCH

        def front():
            half_rows = BATCH // 2
            F, FO, H, Z = 0, 2, 4, 6
            r_xT = att[:].rearrange("p b t c -> p b (t c)")
            bias_raw = probs[0:LO_ROW + 1, 0:3, 0, 0:DIM]
            raws = [raw[:, i * size:(i + 1) * size].rearrange("p (u c) -> p u c", u=UNITS) for i in range(3)]

            his, los = (wg_hi, wu_hi, wd_hi), (wg_lo, wu_lo, wd_lo)

            with nc.Block() as block:
                @block.sync
                def _(sp):
                    cuts = (0, 2 * TPB, 8 * TPB, TILES)
                    def x_piece(i):
                        sp.dma_start(X[:, cuts[i]:cuts[i + 1], :], x_dram[:, cuts[i]:cuts[i + 1], :]).then_inc(s_x[i], 16)

                    x_piece(0)
                    for dst, src in early:
                        sp.dma_start(dst[:], src).then_inc(s_load, 16)
                    sp.wait_ge(s_bias, 1)
                    for row in (0, LO_ROW):
                        sp.dma_start(bias_raw[row:row + 1], io["biases"]).then_inc(s_bias_in, 16)
                    x_piece(1), x_piece(2)
                    sp.wait_ge(s_const, 1)
                    for dst, src in router_table:
                        sp.dma_start(dst[:], src).then_inc(s_rload, 16)
                    for dst, src in late:
                        sp.dma_start(dst[:], src).then_inc(s_late, 16)
                    for dst, name in zip(raws, ("wg", "wu", "wd")):
                        sp.dma_start(dst, io[name]).then_inc(s_wl, 16)
                    for dst, name in ((wr_raw, "wr"), (m_bg, "bg"), (m_bu, "bu"), (m_bd, "bd")):
                        sp.dma_start(dst[:], io[name]).then_inc(s_wl, 16)
                    sp.dma_start(m_br[:], io["br"].partition_broadcast(P)).then_inc(s_wl, 16)
                    sp.wait_ge(s_drop, 2)
                    sp.dma_start(dropped_dram.rearrange("(h p) k -> p h k", p=P),
                                 dropped[:, :, :]).then_inc(s_drop_out, 16)
                    sp.wait_ge(s_drop_out, 16)

                @block.gpsimd
                def _(pool):
                    nc.gpsimd.memset(minus_half[:], -0.5).then_inc(s_eps, 1)
                    nc.gpsimd.memset(epsilon[:], EPS).then_inc(s_eps, 1)
                    for s in (s_att0, s_aT_ps, s_dT, s_dT_ps, s_proj):
                        pool.sem_inc(s, 1)
                    pool.wait_ge(s_eps, 2)

                    def pool_step(t, par, inputs, outputs):
                        if inputs:
                            rstds(pool, t * TPB, TPB, t, par, s_first)
                        if outputs:
                            rstds(pool, (t - 3) * TPB, TPB, t - 3, 3 - par)

                    for t in range(4):
                        pool_step(t, t % 2, True, t >= 3)
                    with pool.Fori(2, BATCH // 2) as two:
                        for par in range(2):
                            pool_step(two * 2 + par, par, True, True)
                    for t in range(BATCH, BATCH + 3):
                        pool_step(t, t % 2, False, True)
                    zero_lanes(nc.gpsimd)
                    nc.gpsimd.memset(vp[:], 0.0).then_inc(s_vzero, 1)
                    nc.gpsimd.memset(mz[:], 0.0).then_inc(s_vzero, 1)
                    nc.gpsimd.memset(a_qk_bias[:, 1, :], 0.0).then_inc(s_vzero, 1)
                    pool.wait_ge(s_vzero, 3)
                    nc.gpsimd.memset(wT[EXPERTS:EXPERTS + 1, :, :], 1.0).then_inc(s_vzero, 1)
                    pool.wait_ge(s_vzero, 4)
                    nc.gpsimd.memset(vp[:, :, :, :, HD:HD + 1], 1.0).then_inc(s_vzero, 1)
                    pool.wait_ge(s_split, 1)
                    nc.gpsimd.tensor_tensor(wr[:, 1, :], wr_raw[:], wr[:, 0, :], ALU.subtract).then_inc(s_split_lo, 1)
                    for i, (hi, lo, w) in enumerate(zip(his, los, raws)):
                        pool.wait_ge(s_split, 2 + i)
                        nc.gpsimd.tensor_tensor(lo[:], w, hi[:], ALU.subtract).then_inc(s_split_lo, 1)

                @block.vector
                def _(dve):
                    nc.vector.memset(bias_raw, 0.0).then_inc(s_bias, 1)
                    nc.vector.memset(r_w2pad[:], 0.0).then_inc(s_const, 1)
                    nc.vector.memset(ones16[:], 1.0).then_inc(s_const, 1)

                    def apply_step(b, par, first_tile, ready, transposed, done):
                        wait(dve, ready, b + 1)
                        wait(dve, transposed, b - 1)
                        for i in range(TPB):
                            T = b * TPB + i
                            last = nc.vector.tensor_scalar(xn[:, par, first_tile + i, :], X[:, T, :],
                                                           moments[:, bass.ds(T, 1), 0], rstd[:, bass.ds(T, 1)],
                                                           ALU.subtract, ALU.mult)
                        last.then_inc(done, 1)

                    def dve_step(t, par):
                        if t < BATCH:
                            stats(dve, t * TPB, TPB, s_first[0])
                        if 1 <= t <= BATCH:
                            apply_step(t - 1, 1 - par, 0, s_first[2], s_xnT_ps, s_xn)
                        if 3 <= t <= BATCH + 2:
                            b = t - 3
                            dve.wait_ge(s_ffn, b + 1)
                            x2 = X[:, bass.ds(b * TPB, TPB), :]
                            nc.vector.scalar_tensor_tensor(x2, PS[:, FO + 1 - par, 0:SEQ].rearrange("p (t h) -> p t h", t=TPB),
                                                           0.5, x2, ALU.mult, ALU.add).then_inc(s_xup, 1)
                            stats(dve, b * TPB, TPB)
                        if 5 <= t:
                            apply_step(t - 5, 1 - par, TPB, s_rstd, s_rxnT_ps, s_rxn)

                    dve.wait_ge(s_x[0], 16)
                    dve_step(0, 0), dve_step(1, 1)
                    dve.wait_ge(s_bias_in, 2 * 16)
                    nc.vector.tensor_copy(biases[:], bias_raw).then_inc(s_bias, 1)
                    dve.wait_ge(s_bias, 2)
                    low = slice(LO_ROW, LO_ROW + 1)
                    nc.vector.tensor_tensor(biases[low], bias_raw[low], biases[low], ALU.subtract).then_inc(s_bias, 1)
                    dve.wait_ge(s_eff_ps, 1)
                    nc.vector.tensor_copy(ffn0_eff[:], PS[:, H, 0:DIM]).then_inc(s_eff, 1)
                    dve.wait_ge(s_x[1], 16)
                    for t in range(2, BATCH + 5):
                        if t == 8:
                            dve.wait_ge(s_x[2], 16)
                        dve_step(t, t % 2)
                    for b in range(2):
                        apply_ln(dve, b, b, BATCH + b)

                    full, rest = divmod(KEEP, 8)

                    def find(h, r):
                        if r < 0 or r > full:
                            return
                        if r == 0:
                            dve.wait_ge(s_z, h + 1)
                        wait(dve, s_taken[h], r)
                        nc.vector.max(top8[:, h, :], z[:, h, :]).then_inc(s_top[h], 1)
                        if r == full:
                            dve.wait_ge(s_top[h], full + 1)
                            nc.vector.memset(top8[:, h, rest:8], NEG).then_inc(s_top[h], 1)

                    def strike(h, r):
                        if r < 0 or r > full:
                            return
                        dve.wait_ge(s_top[h], r + 1 if r < full else full + 2)
                        nc.vector.match_replace(z[:, h, :], top8[:, h, :], z[:, h, :], NEG).then_inc(s_taken[h], 1)

                    for r in range(full + 1 + HALF_LAG):
                        find(0, r), find(1, r - HALF_LAG)
                        strike(0, r), strike(1, r - HALF_LAG)
                    for h in range(2):
                        dve.wait_ge(s_taken[h], full + 1)
                        nc.vector.tensor_scalar(dropped[:, h, :], z[:, h, :], NEG, -MASKED, ALU.is_gt,
                                                ALU.mult).then_inc(s_drop, 1)
                    dve.wait_ge(s_lora_ps, 1)
                    for i, w in enumerate((a_wqT[:, 1, :], a_wkT[:, 1, :], a_wvT[:, 1, :], a_woT[:])):
                        nc.vector.scalar_tensor_tensor(w, PS[:, 0, i * DIM:(i + 1) * DIM], 1.0 / LORA,
                                                       lora_raw[:, i, :], ALU.mult, ALU.add).then_inc(s_lora, 1)

                @block.tensor
                def _(pe):
                    pe.wait_ge(s_load, 16 * len(early))
                    nc.tensor.matmul(PS[:, H, 0:DIM], ffn0_vT[:], ffn0_cT[:], start=True, stop=False)
                    nc.tensor.matmul(PS[:, H, 0:DIM], ident[:], ffn0_wT[:], start=False, stop=True).then_inc(s_eff_ps, 1)

                    def transposes(b, tile0, bank, ready, free, done):
                        pe.wait_ge(ready, b + 1)
                        wait(pe, free, b - 1)
                        for i in range(TPB):
                            last = nc.tensor.transpose(PS[:, bank + b % 2, i * P:(i + 1) * P],
                                                       xn[:, b % 2, tile0 + i, :], ident[:])
                        last.then_inc(done, 1)

                    def product(b):
                        pe.wait_ge(s_xT, b + 1)
                        if b == 0:
                            pe.wait_ge(s_eff, 1)
                            pe.wait_ge(s_bias, 3)
                            pe.wait_ge(s_const, 2)
                        wait(pe, s_xup, b - 1)
                        for i in range(TPB):
                            o = PS[:, FO + b % 2, i * DIM:(i + 1) * DIM]
                            nc.tensor.matmul(o, xT[:, b % 2, i * P:(i + 1) * P], ffn0_eff[:], start=True, stop=False)
                            last = nc.tensor.matmul(o, ones16[:], biases[:, B_FFN, :], start=False, stop=True)
                        last.then_inc(s_ffn, 1)

                    def hidden(b):
                        pe.wait_ge(s_rxT, b + 1)
                        if b == 0:
                            pe.wait_ge(s_rload, 16 * len(router_table))
                        wait(pe, s_h1, b - 1)
                        nc.tensor.matmul(PS[0:RRANK, H + b % 2, SEQ:2 * SEQ], r_w1T[:], r_xT[:, b % 2, :], start=True,
                                         stop=True).then_inc(s_h1_ps, 1)

                    def scores(b):
                        half, i = divmod(b, half_rows)
                        pe.wait_ge(s_h1, b + 1)
                        col = P - HEADS - HEADS * i
                        nc.tensor.matmul(PS[:, Z + half, 0:SEQ], r_w2pad[:, col:col + P], h1[:, b % 2, :],
                                         start=(i == 0), stop=(i == half_rows - 1)).then_inc(s_z_ps, 1)

                    for t in range(1, BATCH + 8):
                        if t - 2 in range(BATCH):
                            product(t - 2)
                        if t - 1 in range(BATCH):
                            transposes(t - 1, 0, F, s_xn, s_xT, s_xnT_ps)
                        if t - 7 in range(BATCH):
                            scores(t - 7)
                        if t - 6 in range(BATCH):
                            hidden(t - 6)
                        if t - 5 in range(BATCH):
                            if t - 5 == 0:
                                pe.wait_ge(s_eff, 1)
                            wait(pe, s_h1, t - 6)
                            transposes(t - 5, TPB, H, s_rxn, s_rxT, s_rxnT_ps)
                    pe.wait_ge(s_late, 16 * len(late))
                    for i in range(4):
                        last = nc.tensor.matmul(PS[:, 0, i * DIM:(i + 1) * DIM], lora_a[:, i, :], lora_bT[:, i, :],
                                                start=True, stop=True)
                    last.then_inc(s_lora_ps, 1)

                @block.scalar
                def _(act):
                    def copy(b, dst, bank, ready, used, done):
                        act.wait_ge(ready, b + 1)
                        wait(act, used, b - 1)
                        nc.scalar.copy(dst[:, b % 2, :], PS[:, bank + b % 2, 0:SEQ]).then_inc(done, 1)

                    def rectify(b):
                        act.wait_ge(s_h1_ps, b + 1)
                        wait(act, s_z_ps, b - 1)
                        nc.scalar.activation(h1[:, b % 2, :], PS[0:RRANK, H + b % 2, SEQ:2 * SEQ], ACT.Relu,
                                             bias=r_b1[:, 0:1]).then_inc(s_h1, 1)

                    def scores_of(h):
                        act.wait_ge(s_z_ps, (h + 1) * half_rows)
                        nc.scalar.activation(z[:, h, :], PS[:, Z + h, 0:SEQ], ACT.Identity,
                                             bias=r_b2[:, 0:1]).then_inc(s_z, 1)

                    for t in range(1, BATCH + 7):
                        if t - 1 in range(BATCH):
                            copy(t - 1, xT, F, s_xnT_ps, s_ffn, s_xT)
                        if t - 6 in range(BATCH):
                            rectify(t - 6)
                        if t - 5 in range(BATCH):
                            copy(t - 5, r_xT, H, s_rxnT_ps, s_h1_ps, s_rxT)
                        if t == half_rows + 7:
                            scores_of(0)
                    scores_of(1)
                    act.wait_ge(s_wl, 8 * 16)
                    nc.scalar.copy(wr[:, 0, :], wr_raw[:]).then_inc(s_split, 1)
                    for i, (hi, w) in enumerate(zip(his, raws)):
                        nc.scalar.mul(w, w, WS).then_inc(s_scaled, 1)
                        act.wait_ge(s_scaled, i + 1)
                        nc.scalar.copy(hi[:], w).then_inc(s_split, 1)
                    nc.scalar.mul(m_bu[:], m_bu[:], WS).then_inc(s_scaled, 1)
                    nc.scalar.mul(m_bd[:], m_bd[:], WS * WS).then_inc(s_scaled, 1)

        def attention(layer):
            st0, ln0, a0 = n_st[0], n_ln[0], layer * BATCH
            S1, S2, OB, MB = 0, 3, 5, 6

            def s1_bank(h):
                return S1 + (h % 3 if h < HEADS - 1 else 1)

            def s1_last(h):
                return {0: 4, 1: 2, 2: 4, HEADS - 1: 2}.get(h, 3)

            masked = layer == 0
            K0, Q0, K1, Q1 = range(4)

            def spread(n, par):
                return (n - par + 2) * 32 + layer * BATCH * 32

            def pe_qk(pe, n, par):
                pe.wait_ge(s_xT, ln0 + n + 1)
                for i, w in enumerate((a_wqT, a_wkT)):
                    last = nc.tensor.matmul(PS[:, MB + 1, i * SEQ:(i + 1) * SEQ], w[:, layer, :], xT[:, par, :],
                                            start=True, stop=True)
                last.then_inc(s_qk_ps, 1)

            def pe_v(pe, n, par):
                pe.wait_ge(s_kst, 2 * (a0 + n) + 2)
                for t in range(TPB):
                    o = PS[:, MB, t * DIM:(t + 1) * DIM]
                    last = nc.tensor.matmul(o, xT[:, par, t * P:(t + 1) * P], a_wvT[:, layer, :], start=True,
                                            stop=not masked)
                    if masked:
                        last = nc.tensor.matmul(o, ones16[:], biases[:, B_V, :], start=False, stop=True)
                last.then_inc(s_v_ps, 1)

            def pe_stack(pe, n, par, piece):
                is_k, half = piece in (K0, K1), piece // 2
                src = 1 if is_k else 0
                dropping = masked and is_k
                if piece == K0:
                    pe.wait_ge(s_lo, a0 + n + 1)
                    if masked:
                        pe.wait_ge(s_drop_in[par], (n - par) * 8 + 16)
                if half == 1:
                    pe.wait_ge(s_kst if is_k else s_qst, 2 * (a0 + n) + 1)
                for i in range(2):
                    v = 2 * half + i
                    o = PS[:, MB + (0 if is_k else 1), i * SEQ:(i + 1) * SEQ]
                    nc.tensor.matmul(o, sel[:, 2 * src, v, :], qk_nat[:, 0, src, :], start=True, stop=False)
                    last = nc.tensor.matmul(o, sel[:, 2 * src + 1, v, :], qk_nat[:, 1, src, :], start=False,
                                            stop=not dropping)
                    if dropping:
                        last = nc.tensor.matmul(o, sel_drop[:, v, :], drop_row[:, par, :], start=False, stop=True)
                last.then_inc(s_stack_ps, 1)

            def pe_s1(pe, n, par, h):
                u = (a0 + n) * HEADS + h
                v, j = divmod(h, LANES)
                if h % (HEADS // 2) == 0:
                    half = h // (HEADS // 2)
                    pe.wait_ge(s_qst, 2 * (a0 + n) + half + 1)
                    pe.wait_ge(s_km[half][par], spread(n, par))
                wait(pe, s_max, u - s1_last(h) + 1)
                for t in range(TPB):
                    last = nc.tensor.matmul(PS[:, s1_bank(h), t * SEQ:(t + 1) * SEQ], qs[:, par, v, t * P:(t + 1) * P],
                                            k_lanes[:, par, v, j, :], start=True, stop=True)
                last.then_inc(s_s1, 1)

            def pe_maxT(pe, n, half):
                pe.wait_ge(s_max, (a0 + n) * HEADS + (half + 1) * (HEADS // 2))
                bank = PS[:, MB + half, :].bitcast(F16)
                for i in range(2):
                    for t in range(TPB):
                        last = nc.tensor.transpose(bank[:, i * SEQ + t * P:i * SEQ + (t + 1) * P],
                                                   mz[:, t, 2 * half + i, :], ident16[:])
                last.then_inc(s_mT, 1)

            def pe_s2(pe, c, par, h):
                u = (a0 + c) * HEADS + h
                v, j = divmod(h, LANES)
                if h % (HEADS // 2) == 0:
                    pe.wait_ge(s_madd, 2 * (a0 + c) + h // (HEADS // 2) + 1)
                wait(pe, s_exp, u - 1)
                for t in range(TPB):
                    last = nc.tensor.matmul(PS[:, S2 + h % 2, t * SEQ:(t + 1) * SEQ],
                                            k_lanes[:, par, v, j, t * P:(t + 1) * P], qs[:, par, v, :],
                                            start=True, stop=True)
                last.then_inc(s_s2, 1)

            def pe_av(pe, c, par, v):
                g = 4 * (a0 + c) + v
                pe.wait_ge(s_exp, 4 * g + 4)
                if v == 0:
                    pe.wait_ge(s_v, a0 + c + 1)
                for t in range(TPB):
                    for j in range(LANES):
                        h = LANES * v + j
                        last = nc.tensor.matmul(PS[32 * j:32 * j + 32, OB, 0:SEQ], vp[:, par, t, h, :],
                                                probs[:, h % 8, t, :], start=(t == 0), stop=(t == TPB - 1),
                                                skip_group_check=True)
                last.then_inc(s_av, 1)

            def pe_oT(pe, c, v):
                pe.wait_ge(s_o, 4 * (a0 + c) + v + 1)
                for t in range(TPB):
                    last = nc.tensor.transpose(PS[:, OB, t * P:(t + 1) * P], o_sb[:, v % 2, t * P:(t + 1) * P], ident[:])
                last.then_inc(s_oT, 1)

            def pe_attT(pe, o, par):
                pe.wait_ge(s_norm, 4 * (a0 + o) + 4)
                for t in range(TPB):
                    last = nc.tensor.transpose(PS[:, MB + 1, t * P:(t + 1) * P], att[:, par, t, :], ident[:])
                last.then_inc(s_aT_ps, 1)

            def pe_project(pe, o):
                pe.wait_ge(s_aT, o + 1)
                for t in range(TPB):
                    r = PS[:, MB + 1, t * DIM:(t + 1) * DIM]
                    nc.tensor.matmul(r, attT[:, t * P:(t + 1) * P], a_woT[:], start=True, stop=False)
                    last = nc.tensor.matmul(r, ones16[:], biases[:, B_O, :], start=False, stop=True)
                last.then_inc(s_proj, 1)

            def pe_step(pe, n, c, par, has_next, has_ahead, has_cur, has_old):
                cp = 1 - par
                o = c - 1
                projects = has_old and not masked
                norms = 4 * (a0 + c)

                def s2(*hs):
                    if has_cur:
                        for h in hs:
                            pe_s2(pe, c, cp, h)

                def s1(*hs):
                    if has_next:
                        for h in hs:
                            pe_s1(pe, n, par, h)

                def last_of_side():
                    if has_next:
                        pe.wait_ge(s_qst, 2 * (a0 + n) + 2)
                    elif projects:
                        pe.wait_ge(s_att1, c - 1)

                s2(0), s1(0)
                if has_next:
                    pe_stack(pe, n, par, Q1)
                s2(1), s1(1)
                if has_old:
                    wait(pe, s_norm, norms - 1)
                    pe_av(pe, o, par, 3)
                s2(2), s1(2)
                if has_next:
                    pe_v(pe, n, par)
                if has_cur:
                    last_of_side()
                    pe_maxT(pe, c, 1)
                s2(3), s1(3)
                if has_old:
                    pe_oT(pe, o, 3)
                s2(4), s1(4), s2(5)
                if has_ahead:
                    pe.wait_ge(s_v, a0 + n + 1)
                    transpose_ln(pe, MB, cp, ln0 + n + 1)
                s1(5)
                if projects:
                    if has_cur:
                        pe.wait_ge(s_madd, 2 * (a0 + c) + 2)
                    else:
                        last_of_side()
                    pe_attT(pe, o, par)
                s2(6), s1(6)
                if has_cur:
                    wait(pe, s_norm, norms)
                    pe_av(pe, c, cp, 0)
                if projects:
                    pe_project(pe, o)
                s2(7), s1(7)
                if has_ahead:
                    if projects:
                        pe.wait_ge(s_att1, c)
                    elif has_cur:
                        pe.wait_ge(s_madd, 2 * (a0 + c) + 2)
                    else:
                        last_of_side()
                    pe_qk(pe, n + 1, cp)
                s2(8), s1(8)
                if has_cur:
                    pe_oT(pe, c, 0)
                s2(9), s1(9)
                if has_next:
                    if not has_ahead:
                        pe.wait_ge(s_v, a0 + n + 1)
                    pe_maxT(pe, n, 0)
                s2(10), s1(10)
                if has_cur:
                    pe.wait_ge(s_norm, norms + 1)
                    pe_av(pe, c, cp, 1)
                s2(11), s1(11)
                if has_ahead:
                    pe.wait_ge(s_madd, 2 * (a0 + n) + 1)
                    pe_stack(pe, n + 1, cp, K0)
                s2(12)
                if has_cur:
                    pe_oT(pe, c, 1)
                s1(12)
                if has_ahead:
                    pe_stack(pe, n + 1, cp, Q0)
                s2(13), s1(13), s2(14)
                if has_cur:
                    pe.wait_ge(s_norm, norms + 2)
                    pe_av(pe, c, cp, 2)
                s1(14)
                if has_ahead:
                    pe_stack(pe, n + 1, cp, K1)
                s2(15), s1(15)
                if has_cur:
                    pe_oT(pe, c, 2)

            def act_hi(act, n):
                act.wait_ge(s_qk_ps, a0 + n + 1)
                wait(act, s_stack_ps, 4 * (a0 + n))
                for i in range(2):
                    last = nc.scalar.activation(qk_nat[:, 0, i, :], PS[:, MB + 1, i * SEQ:(i + 1) * SEQ],
                                                ACT.Identity, bias=a_qk_bias[:, layer, i:i + 1])
                last.then_inc(s_hi, 1)

            def act_xT(act, n, par):
                act.wait_ge(s_xnT_ps, ln0 + n + 1)
                wait(act, s_v_ps, a0 + n - 1)
                nc.scalar.copy(xT[:, par, :], PS[:, MB, 0:SEQ]).then_inc(s_xT, 1)

            def q_copy(act, n, par, half):
                act.wait_ge(s_stack_ps, 4 * (a0 + n) + (Q0, Q1)[half] + 1)
                wait(act, s_s2, (a0 + n - 2) * HEADS + (half + 1) * (HEADS // 2))
                nc.scalar.activation(qs[:, par, 2 * half:2 * half + 2, :],
                                     PS[:, MB + 1, :].rearrange("p (v q) -> p v q", v=2), ACT.Identity,
                                     bias=lane_bias[:, 0:1]).then_inc(s_qst, 1)

            def act_step(act, n, c, par, has_next, has_ahead, has_cur, has_old):
                cp = 1 - par
                o = c - 1

                def exps(*hs):
                    if not has_cur:
                        return
                    for h in hs:
                        u = (a0 + c) * HEADS + h
                        act.wait_ge(s_s2, u + 1)
                        if h % LANES == 0:
                            wait(act, s_av, 4 * (a0 + c) + h // LANES - 1)
                        nc.scalar.activation(probs[:, h % 8, :, :], PS[:, S2 + h % 2, :].rearrange("p (t q) -> p t q", t=TPB),
                                             ACT.Exp, scale=SCORE_SCALE).then_inc(s_exp, 1)

                def out_copy(row, v):
                    g = 4 * (a0 + row) + v
                    act.wait_ge(s_av, g + 1)
                    wait(act, s_oT, g - 1)
                    nc.scalar.copy(o_sb[:, v % 2, :], PS[:, OB, 0:SEQ]).then_inc(s_o, 1)

                exps(0, 1)
                if has_next:
                    q_copy(act, n, par, 1)
                exps(2)
                if has_old:
                    out_copy(o, 3)
                exps(3)
                if has_next:
                    act.wait_ge(s_v_ps, a0 + n + 1)
                    wait(act, s_av, 4 * (a0 + n - 1))
                    nc.scalar.copy(vp[:, par, :, :, 0:HD],
                                   PS[:, MB, 0:SEQ].rearrange("p (t h d) -> p t h d", t=TPB, h=HEADS)).then_inc(s_v, 1)
                exps(4, 5)
                if has_ahead:
                    act_xT(act, n + 1, cp)
                exps(6)
                if has_old and not masked:
                    act.wait_ge(s_aT_ps, c + 1)
                    act.wait_ge(s_proj, c)
                    nc.scalar.copy(attT[:], PS[:, MB + 1, 0:SEQ]).then_inc(s_aT, 1)
                exps(7)
                if has_cur:
                    out_copy(c, 0)
                exps(8)
                if has_ahead:
                    act_hi(act, n + 1)
                exps(9, 10)
                if has_cur:
                    out_copy(c, 1)
                exps(11, 12, 13)
                if has_ahead:
                    q_copy(act, n + 1, cp, 0)
                exps(14)
                if has_cur:
                    out_copy(c, 2)
                exps(15)

            def dve_lo(dve, n):
                dve.wait_ge(s_hi, a0 + n + 1)
                for i in range(2):
                    last = nc.vector.scalar_tensor_tensor(
                        qk_nat[:, 1, i, :], PS[:, MB + 1, i * SEQ:(i + 1) * SEQ], a_qk_bias[:, layer, i:i + 1],
                        qk_nat[:, 0, i, :], ALU.add, ALU.subtract)
                last.then_inc(s_lo, 1)

            def k_copy(dve, n, par, half):
                dve.wait_ge(s_stack_ps, 4 * (a0 + n) + (K0, K1)[half] + 1)
                wait(dve, s_km[half][par], spread(n, par) - 64)
                nc.vector.tensor_scalar(ks[:, par, 2 * half:2 * half + 2, :],
                                        PS[:, MB, :].rearrange("p (v q) -> p v q", v=2), lane_bias[:, 1:2],
                                        None, ALU.add).then_inc(s_kst, 1)

            def dve_step(dve, n, c, par, has_next, has_ahead, has_cur, has_old):
                cp = 1 - par
                o = c - 1

                def reduces(*hs):
                    if not has_next:
                        return
                    for h in hs:
                        u = (a0 + n) * HEADS + h
                        v, j = divmod(h, LANES)
                        dve.wait_ge(s_s1, u + 1)
                        if h % (HEADS // 2) == 0:
                            wait(dve, s_mT, 2 * (a0 + n - 1) + h // (HEADS // 2) + 1)
                        nc.vector.tensor_reduce(mz[:, :, v, 32 * j + ROW_MAX], PS[:, s1_bank(h), :].rearrange("p (t k) -> p t k", t=TPB),
                                                AX.X, ALU.max).then_inc(s_max, 1)

                def norm(row, v, buf):
                    g = 4 * (a0 + row) + v
                    T = PS[:, OB, 0:SEQ].rearrange("p (t j d) -> p t j d", t=TPB, j=LANES)
                    dve.wait_ge(s_oT, g + 1)
                    wait(dve, s_norm, g - 1)
                    nc.vector.reciprocal(rec[:, v % 2, :, :], T[:, :, :, HD]).then_inc(s_rec, 1)
                    if v == 0:
                        dve.wait_ge(s_att0 if masked else s_aT_ps, row)
                    dve.wait_ge(s_rec, g + 1)
                    r = att[:, buf, :, v * LANES * HD:(v + 1) * LANES * HD].rearrange("p t (j d) -> p t j d", j=LANES)
                    nc.vector.tensor_tensor(r, T[:, :, :, 0:HD],
                                            rec[:, v % 2, :, :].unsqueeze(3).broadcast_to([P, TPB, LANES, HD]),
                                            ALU.mult).then_inc(s_norm, 1)

                def add_maxima(row, buf, half):
                    dve.wait_ge(s_mT, 2 * (a0 + row) + half + 1)
                    q = qs[:, buf, 2 * half:2 * half + 2, :]
                    m = PS[:, MB + half, :].bitcast(F16)[:, 0:2 * SEQ].rearrange("p (v q) -> p v q", v=2)
                    nc.vector.tensor_tensor(q, q, m, ALU.add).then_inc(s_madd, 1)

                if has_old and not has_cur:
                    if masked:
                        first_rows(dve, ln0 + BATCH, st0 + 2)
                    else:
                        first_wide(dve, SUPERS, st0 + 2, ln0 + BATCH)
                if has_old:
                    norm(o, 2, par)
                reduces(0, 1, 2)
                if has_cur:
                    add_maxima(c, cp, 1)
                reduces(3)
                if has_old:
                    norm(o, 3, par)
                reduces(4, 5)
                if has_old and masked:
                    dve.wait_ge(s_att0, c + 1)
                reduces(6)
                if has_old and masked:
                    stats(dve, o * TPB, TPB)
                if has_old and not masked:
                    dve.wait_ge(s_proj, c + 1)
                    x2 = X[:, bass.ds(o * TPB, TPB), :]
                    nc.vector.tensor_tensor(x2, x2, PS[:, MB + 1, 0:SEQ].rearrange("p (t h) -> p t h", t=TPB),
                                            ALU.add).then_inc(s_att1, 1)
                reduces(7, 8)
                if has_cur:
                    norm(c, 0, cp)
                if has_ahead:
                    dve_lo(dve, n + 1)
                reduces(9)
                if has_next:
                    add_maxima(n, par, 0)
                reduces(10)
                if has_ahead:
                    k_copy(dve, n + 1, cp, 0)
                reduces(11)
                if has_cur:
                    norm(c, 1, cp)
                reduces(12, 13)
                if has_ahead and not (isinstance(n, int) and n + 2 >= BATCH):
                    apply_ln(dve, n + 2, par, ln0 + n + 2)
                if has_old and not masked:
                    stats(dve, o * TPB, TPB)
                reduces(14)
                if has_ahead:
                    k_copy(dve, n + 1, cp, 1)
                reduces(15)

            def run(step, engine):
                step(0, -1, 0, True, True, False, False)
                step(1, 0, 1, True, True, True, False)
                with engine.Fori(1, BATCH // 2 - 1) as two:
                    for par in range(2):
                        step(two * 2 + par, two * 2 + (par - 1), par, True, True, True, True)
                step(BATCH - 2, BATCH - 3, 0, True, True, True, True)
                step(BATCH - 1, BATCH - 2, 1, True, False, True, True)
                step(BATCH, BATCH - 1, 0, False, False, True, True)
                step(BATCH + 1, BATCH, 1, False, False, False, True)

            with nc.Block() as block:
                @block.tensor
                def _(pe):
                    transpose_ln(pe, MB, 0, ln0)
                    pe_qk(pe, 0, 0)
                    for piece in (K0, Q0, K1):
                        pe_stack(pe, 0, 0, piece)
                    run(lambda *a: pe_step(pe, *a), pe)
                    if not masked:
                        pe.wait_ge(s_madd, 2 * (a0 + BATCH) - 1)
                        wide_transposes(pe, 0, 0, SUPERS)

                @block.scalar
                def _(act):
                    act_xT(act, 0, 0)
                    act_hi(act, 0)
                    q_copy(act, 0, 0, 0)
                    run(lambda *a: act_step(act, *a), act)
                    if not masked:
                        wide_high(act, 0, 0, SUPERS)

                @block.vector
                def _(dve):
                    dve.wait_ge(s_rstd, st0)
                    dve_lo(dve, 0)
                    k_copy(dve, 0, 0, 0), k_copy(dve, 0, 0, 1)
                    run(lambda *a: dve_step(dve, *a), dve)
                    if not masked:
                        wide_low(dve, 0, 0, SUPERS)

                @block.gpsimd
                def _(pool):
                    def pool_sum(pool, b, par):
                        pool.wait_ge(s_norm, 4 * (a0 + b) + 4)
                        x2 = X[:, bass.ds(b * TPB, TPB), :]
                        nc.gpsimd.tensor_tensor(x2, x2, att[:, par, :, :], ALU.add).then_inc(s_att0, 1)

                    if not masked:
                        zero_lanes(nc.gpsimd)
                    if masked:
                        with pool.Fori(0, BATCH // 2) as two:
                            for par in range(2):
                                pool_sum(pool, two * 2 + par, par)
                                rstds(pool, (two * 2 + par) * TPB, TPB, two * 2 + (par + st0), par)
                    else:
                        with pool.Fori(0, BATCH // 2) as two:
                            for par in range(2):
                                rstds(pool, (two * 2 + par) * TPB, TPB, two * 2 + (par + st0), par)

                @block.sync
                def _(sp):
                    def load(b, par):
                        wait(sp, s_stack_ps, 4 * (a0 + b - 1))
                        sp.dma_start(drop_row[:, par, :], dropped_dram[bass.ds(b * HEADS, HEADS), :])\
                            .then_inc(s_drop_in[par], 16)

                    def spread_k(b, par):
                        for half in range(2):
                            wait(sp, s_s2, (a0 + b - 1) * HEADS if half else (a0 + b - 2) * HEADS + HEADS // 2)
                            sp.wait_ge(s_kst, (a0 + b + 1) * 2 if half else (a0 + b - 2) * 2 + 5)
                            groups = slice(2 * half, 2 * half + 2)
                            for j in range(LANES):
                                lane = slice(32 * j, 32 * j + 32)
                                sp.dma_start(k_lanes[lane, par, groups, j, :], ks[lane, par, groups, :])\
                                    .then_inc(s_km[half][par], 16)

                    if masked:
                        load(0, 0), load(1, 1)
                    sp.wait_ge(s_km0, layer + 1)
                    spread_k(0, 0), spread_k(1, 1)
                    with sp.Fori(1, BATCH // 2) as two:
                        for par in range(2):
                            if masked:
                                load(two * 2 + par, par)
                            spread_k(two * 2 + par, par)
            n_st[0] += BATCH
            n_ln[0] += BATCH

        def experts(turn):
            st0, m0 = n_st[0], turn * SUPERS

            def pe_logits(pe, n, par):
                g = m0 + n
                pe.wait_ge(s_xlo, g + 1)
                wait(pe, s_mup, g - 1)
                for t in range(TPS):
                    o = PS[:, 7, t * EXPERTS:(t + 1) * EXPERTS]
                    parts = [(a, b) for a in (x_hi, x_lo) for b in range(2)]
                    for i, (a, b) in enumerate(parts):
                        last = nc.tensor.matmul(o, a[:, par, t * P:(t + 1) * P], wr[:, b, :], start=(i == 0),
                                                stop=(i == len(parts) - 1))
                last.then_inc(s_lg_ps, 1)

            def pe_wT(pe, n):
                pe.wait_ge(s_w, m0 + n + 1)
                for t in range(TPS):
                    last = nc.tensor.transpose(PS[0:EXPERTS, 6, t * P:(t + 1) * P], w_tok[:, t, :], ident[:])
                last.then_inc(s_wT_ps, 1)

            def rows(k):
                return (INTER, PAIRS) if k == 0 else (P, k - 1)

            def pe_unit(pe, c, par, k):
                u = (m0 + c) * UNITS + k
                bank = (par + k) % 2
                m, e = rows(k)
                if k == 0:
                    pe.wait_ge(s_xlo, m0 + c + 1)
                for ready, free, lo_bank, hi_w, lo_w in ((s_g, s_silu, 0, wg_hi, wg_lo), (s_u, s_hid, 2, wu_hi, wu_lo)):
                    wait(pe, free, u - 1)
                    o = PS[0:m, lo_bank + bank, :]
                    nc.tensor.matmul(o, hi_w[:, e, 0:m], x_hi[:, par, :], start=True, stop=False)
                    nc.tensor.matmul(o, hi_w[:, e, 0:m], x_lo[:, par, :], start=False, stop=False)
                    nc.tensor.matmul(o, lo_w[:, e, 0:m], x_hi[:, par, :], start=False, stop=True).then_inc(ready, 1)

            def pe_down(pe, c, par, k):
                u = (m0 + c) * UNITS + k
                m, e = rows(k)
                r = slot(k)
                pe.wait_ge(s_hlo, u + 1)
                if k == 0:
                    pe.wait_ge(s_dT, m0 + c)
                o = PS[:, 4 + par, :]
                nc.tensor.matmul(o, wd_hi[0:m, e, :], hid_hi[0:m, r, :], start=(k == 0), stop=False)
                nc.tensor.matmul(o, wd_hi[0:m, e, :], hid_lo[0:m, r, :], start=False, stop=False)
                nc.tensor.matmul(o, wd_lo[0:m, e, :], hid_hi[0:m, r, :], start=False, stop=False).then_inc(s_down, 1)

            def slot(k):
                return RING if k == 0 else (k - 1) % RING

            def pe_biases(pe, o, par):
                nc.tensor.matmul(PS[:, 4 + par, :], m_bd[:], wT[:, par, :], start=False, stop=True).then_inc(s_dsum, 1)

            def pe_dT(pe, o):
                pe.wait_ge(s_dT, m0 + o + 2)
                for t in range(TPS):
                    last = nc.tensor.transpose(PS[:, 7, t * P:(t + 1) * P], downT[:, t * P:(t + 1) * P], ident[:])
                last.then_inc(s_dT_ps, 1)

            def pe_step(pe, n, c, o, par, has_next, has_cur, has_old):
                cp = 1 - par
                for k in range(UNITS):
                    if has_cur:
                        pe_unit(pe, c, cp, k)
                    if has_cur and has_next and k == 0:
                        wide_transposes(pe, n, par, m0)
                    if k < LAG:
                        if has_old:
                            pe_down(pe, o, par, UNITS - LAG + k)
                    elif has_cur:
                        pe_down(pe, c, cp, k - LAG)
                    if k == LAG and has_old:
                        pe_biases(pe, o, par)
                    if k == LAG + 1 and has_old:
                        pe_dT(pe, o)
                    if k == LAG + 3 and has_next:
                        pe_logits(pe, n, par)
                    if k == LAG + 10 and has_next:
                        pe_wT(pe, n)

            def act_step(act, n, c, o, par, has_next, has_cur, has_old):
                cp = 1 - par

                def high(c_, p_, k):
                    u = (m0 + c_) * UNITS + k
                    m, _ = rows(k)
                    act.wait_ge(s_hid, u + 1)
                    wait(act, s_down, u - RING + 1)
                    nc.scalar.copy(hid_hi[0:m, slot(k), :], hid[0:m, slot(k), :]).then_inc(s_hhi, 1)

                for k in range(UNITS):
                    if has_cur:
                        u = (m0 + c) * UNITS + k
                        m, e = rows(k)
                        act.wait_ge(s_g, u + 1)
                        wait(act, s_hid, u - RING + 1)
                        nc.scalar.activation(gate_shared if k == 0 else gate[:, slot(k), :], PS[0:m, (cp + k) % 2, :], ACT.Silu,
                                             bias=m_bg[0:m, e:e + 1], scale=1.0 / WS).then_inc(s_silu, 1)
                        if k >= 1:
                            high(c, cp, k - 1)
                    if k == 0 and has_old:
                        high(o, par, UNITS - 1)
                    if k == 1 and has_cur and has_next:
                        wide_high(act, n, par, m0)
                    if k == LAG and has_old:
                        act.wait_ge(s_dsum, m0 + o + 1)
                        act.wait_ge(s_dT_ps, m0 + o + 1)
                        nc.scalar.copy(downT, PS[:, 4 + par, :]).then_inc(s_dT, 1)
                    if k == LAG + 4 and has_next:
                        act.wait_ge(s_lg, m0 + n + 1)
                        nc.scalar.activation(aff[:], logits[:], ACT.Tanh, scale=0.5).then_inc(s_th, 1)
                    if k == LAG + 10 and has_next:
                        act.wait_ge(s_wT_ps, m0 + n + 1)
                        wait(act, s_wst[par], (n - par) * 8)
                        wait(act, s_dsum, m0 + n - 1)
                        nc.scalar.copy(wT[0:EXPERTS, par, :], PS[0:EXPERTS, 6, :]).then_inc(s_wT, 1)

            def dve_step(dve, n, c, o, par, has_next, has_cur, has_old):
                cp = 1 - par
                g = m0 + n
                if not has_cur and has_old and turn == 0:
                    first_rows(dve, n_ln[0], st0 + 1, SUPERS)

                def low(c_, p_, k):
                    u = (m0 + c_) * UNITS + k
                    m, _ = rows(k)
                    r = slot(k)
                    dve.wait_ge(s_hhi, u + 1)
                    nc.vector.tensor_tensor(hid_lo[0:m, r, :], hid[0:m, r, :], hid_hi[0:m, r, :],
                                            ALU.subtract).then_inc(s_hlo, 1)

                for k in range(UNITS):
                    if has_cur:
                        u = (m0 + c) * UNITS + k
                        m, e = rows(k)
                        r = slot(k)
                        dve.wait_ge(s_u, u + 1)
                        if k == 0:
                            dve.wait_ge(s_silu, u + 1)
                        else:
                            dve.wait_ge(s_gw, (m0 + c) * PAIRS + k)
                        wait(dve, s_hlo, u - RING + 1)
                        nc.vector.scalar_tensor_tensor(hid[0:m, r, :], PS[0:m, 2 + (cp + k) % 2, :], m_bu[0:m, e:e + 1],
                                                       gate_shared if k == 0 else gw[:, r, :], ALU.add,
                                                       ALU.mult).then_inc(s_hid, 1)
                        if k >= 1:
                            low(c, cp, k - 1)
                    if k == 0 and has_old:
                        low(o, par, UNITS - 1)
                    if k == 1 and has_cur and has_next:
                        wide_low(dve, n, par, m0)
                    if k == LAG + 1 and has_old:
                        dve.wait_ge(s_dT_ps, m0 + o + 2)
                        x4 = X[:, bass.ds(o * TPS, TPS), :]
                        nc.vector.scalar_tensor_tensor(x4, PS[:, 7, :].rearrange("p (t h) -> p t h", t=TPS),
                                                       0.5 / (WS * WS), x4, ALU.mult, ALU.add).then_inc(s_mup, 1)
                    if k == LAG + 2 and has_old and turn == 0:
                        stats(dve, o * TPS, TPS)
                    if k == LAG + 3:
                        if has_next:
                            dve.wait_ge(s_lg_ps, g + 1)
                            nc.vector.tensor_tensor(logits[:], PS[:, 7, 0:TPS * EXPERTS].rearrange("p (t e) -> p t e", t=TPS),
                                                    m_br[:].unsqueeze(1).broadcast_to([P, TPS, EXPERTS]),
                                                    ALU.add).then_inc(s_lg, 1)
                    if has_next and k == LAG + 4:
                        dve.drain()
                        for t in range(TPS):
                            nc.vector.max(best[:, t, :], logits[:, t, :])
                    if has_next and k == LAG + 5:
                        dve.drain()
                        for t in range(TPS):
                            last = nc.vector.match_replace(ranked[:, t, :], best[:, t, :], logits[:, t, :], NEG)
                        last.then_inc(s_rank, 1)
                        dve.wait_ge(s_th, g + 1)
                        nc.vector.tensor_scalar(aff[:], aff[:], 0.5, 0.5, ALU.mult, ALU.add).then_inc(s_aff, 1)
                    if has_next and k == LAG + 6:
                        dve.wait_ge(s_rank, g + 1)
                        dve.wait_ge(s_aff, g + 1)
                        nc.vector.scalar_tensor_tensor(ranked[:], ranked[:], NEG, aff[:], ALU.is_le,
                                                       ALU.mult).then_inc(s_wv, 1)
                    if has_next and k == LAG + 7:
                        dve.wait_ge(s_wv, g + 1)
                        nc.vector.tensor_reduce(wsum[:], ranked[:], AX.X, ALU.add).then_inc(s_ws, 1)
                        dve.wait_ge(s_ws, 3 * g + 1)
                        nc.vector.tensor_scalar(wsum[:], wsum[:], 1e-9, None, ALU.add).then_inc(s_ws, 1)
                    if has_next and k == LAG + 8:
                        dve.wait_ge(s_ws, 3 * g + 2)
                        nc.vector.reciprocal(wsum[:], wsum[:]).then_inc(s_ws, 1)
                        dve.wait_ge(s_ws, 3 * g + 3)
                        wait(dve, s_wT_ps, g)
                        nc.vector.tensor_tensor(w_tok[:], ranked[:], wsum[:].unsqueeze(2).broadcast_to([P, TPS, EXPERTS]),
                                                ALU.mult).then_inc(s_w, 1)
                    if has_next and k == UNITS - 3 and not (isinstance(n, int) and n + 1 >= SUPERS):
                        apply_wide(dve, n + 1, cp, m0)

            def pool_step(pool, n, c, o, par, has_next, has_cur, has_old):
                cp = 1 - par
                for k in range(1, UNITS):
                    if has_cur:
                        u = (m0 + c) * UNITS + k
                        pool.wait_ge(s_silu, u + 1)
                        if (k - 1) % 4 == 0:
                            pool.wait_ge(s_wide[cp][(k - 1) // 4], (turn * SUPERS + (c - cp) + 2) * 16)
                        wait(pool, s_hid, u - RING + 1)
                        nc.gpsimd.tensor_tensor(gw[:, slot(k), :], gate[:, slot(k), :], w_wide[:, cp, k - 1, :],
                                                ALU.mult).then_inc(s_gw, 1)
                    if k == LAG + 3 and has_old and turn == 0:
                        rstds(pool, o * TPS, TPS, st0 + o, par)

            def sp_step(sp, n, par):
                sp.wait_ge(s_wT, m0 + n + 1)
                done = (turn * SUPERS + (n - par) + 2) * 8
                sp.dma_start(w_dram[bass.ds(n, 1), :, :].rearrange("a e t -> (a e) t"), wT[0:EXPERTS, par, :])\
                    .then_inc(s_wst[par], 16)
                sp.wait_ge(s_wst[par], done)
                rows_of = w_dram[bass.ds(n, 1), :, :].rearrange("a (k e) t -> e (a k) t", e=2)
                for q in range(4):
                    wait(sp, s_gw, (m0 + n - 2) * PAIRS + 4 * q + 4)
                    for e in range(2):
                        sp.dma_start(w_wide[64 * e:64 * e + 64, par, 4 * q:4 * q + 4, :],
                                     rows_of[e, 4 * q:4 * q + 4, :].partition_broadcast(INTER))\
                            .then_inc(s_wide[par][q], 16)

            def store(sp, o):
                sp.wait_ge(s_mup, m0 + o + 1)
                sp.dma_start(out_dram[:, bass.ds(o * TPS, TPS), :], X[:, bass.ds(o * TPS, TPS), :]).then_inc(s_out, 16)

            def run(step, engine):
                step(0, -1, -2, 0, True, False, False)
                step(1, 0, -1, 1, True, True, False)
                with engine.Fori(1, SUPERS // 2 - 1) as two:
                    for par in range(2):
                        step(two * 2 + par, two * 2 + (par - 1), two * 2 + (par - 2), par, True, True, True)
                for n in range(SUPERS - 2, SUPERS):
                    step(n, n - 1, n - 2, n % 2, True, True, True)
                step(SUPERS, SUPERS - 1, SUPERS - 2, 0, False, True, True)
                step(SUPERS + 1, SUPERS, SUPERS - 1, 1, False, False, True)

            with nc.Block() as block:
                @block.tensor
                def _(pe):
                    run(lambda *a: pe_step(pe, *a), pe)

                @block.scalar
                def _(act):
                    run(lambda *a: act_step(act, *a), act)

                @block.vector
                def _(dve):
                    dve.wait_ge(s_rstd, st0)
                    run(lambda *a: dve_step(dve, *a), dve)

                @block.gpsimd
                def _(pool):
                    run(lambda *a: pool_step(pool, *a), pool)

                @block.sync
                def _(sp):
                    for n in range(2):
                        sp_step(sp, n, n)
                    with sp.Fori(1, SUPERS // 2) as two:
                        for par in range(2):
                            sp_step(sp, two * 2 + par, par)
                            if turn == 1:
                                store(sp, two * 2 + (par - 2))
                    if turn == 1:
                        for o in range(SUPERS - 2, SUPERS):
                            store(sp, o)
                        sp.wait_ge(s_out, 16 * SUPERS)
            if turn == 0:
                n_st[0] += SUPERS

        front()
        attention(0)
        ffn0()
        experts(0)
        attention(1)
        experts(1)


def layout(inp):
    import numpy as np
    c = np.ascontiguousarray
    a = {k: np.asarray(v) for k, v in inp.items()}
    f = {}
    f["x"] = c(a["L0_attn_hidden_states"])
    f["ident"] = np.eye(128, dtype=np.float32)
    f["ffn0_wT"] = c(a["L0_ffn_W"].T)
    f["ffn0_vT"] = c(a["L0_ffn_V_r"].T)
    f["ffn0_cT"] = c(a["L0_ffn_C"].T)
    w = a["L0_attn_qkv_w"]
    f["qkv_wT"] = c(w.T)
    f["qk_bias"] = c(a["L0_attn_qkv_b"].reshape(3, 128)[0:2].T)
    f["biases"] = c(np.stack([a["L0_ffn_b"], a["L0_attn_qkv_b"].reshape(3, 128)[2], a["L1_attn_bo"]])[None])
    f["r_w1T"] = c(a["L0_attn_r_w1"].T)
    f["r_b1"] = c(a["L0_attn_r_b1"].reshape(-1, 1))
    f["r_w2T"] = c(a["L0_attn_r_w2"].T)
    f["r_b2"] = c(np.tile(a["L0_attn_r_b2"], 8).reshape(-1, 1))
    f["lora_w"] = c(np.stack([a["L1_attn_W" + k].T for k in "qkvo"], 1))
    f["lora_a"] = c(np.stack([a["L1_attn_A" + k] for k in "qkvo"], 1))
    f["lora_bT"] = c(np.stack([a["L1_attn_B" + k].T for k in "qkvo"], 1))
    sel = np.zeros((128, 4, GROUPS, 128), np.float16)
    drop = np.zeros((HEADS, GROUPS, 128), np.float16)
    lane = np.zeros((128, 2), np.float32)
    for v in range(GROUPS):
        for j in range(LANES):
            drop[v * LANES + j, v, 32 * j + ROW_MASK] = 1
            for d in range(HD):
                src = (v * LANES + j) * HD + d
                for copy, (q, k) in enumerate(((0, 2), (1, 2), (0, 3))):
                    sel[src, q, v, 32 * j + copy * HD + d] = 1
                    sel[src, k, v, 32 * j + copy * HD + d] = 1
    lane[ROW_MASK::32, 0] = MASKED
    lane[ROW_MAX::32, 1] = -1.0
    f["sel"], f["sel_drop"], f["lane_bias"] = sel, drop, lane
    f["ident16"] = np.eye(128, dtype=np.float16)
    def cols(we, ws):
        w = np.zeros((128, UNITS, 128), np.float32)
        w[:, :PAIRS] = we.transpose(1, 0, 2).reshape(128, PAIRS, 128)
        w[:, PAIRS, :INTER] = ws
        return w

    def column(be, bs):
        w = np.zeros((128, UNITS), np.float32)
        w[:, :PAIRS] = be.reshape(PAIRS, 128).T
        w[:INTER, PAIRS] = bs
        return w

    f["wg"] = cols(a["L1_ffn_Wg"], a["L1_ffn_Wg_s"])
    f["wu"] = cols(a["L1_ffn_Wu"], a["L1_ffn_Wu_s"])
    wd = np.zeros((128, UNITS, 128), np.float32)
    wd[:, :PAIRS] = a["L1_ffn_Wd"].reshape(PAIRS, 128, 128).transpose(1, 0, 2)
    wd[:INTER, PAIRS] = a["L1_ffn_Wd_s"]
    f["wd"] = wd
    f["bg"] = column(a["L1_ffn_bg"], a["L1_ffn_bg_s"])
    f["bu"] = column(a["L1_ffn_bu"], a["L1_ffn_bu_s"])
    f["bd"] = np.concatenate([a["L1_ffn_bd"], a["L1_ffn_bd_s"].reshape(1, -1)])
    f["wr"] = c(a["L1_ffn_Wr"])
    f["br"] = c(a["L1_ffn_br"])
    return f


def kernel(**inputs):
    import concourse.bacc as _bacc
    from concourse import mybir as _mybir
    from concourse.bass_utils import run_bass_kernel_spmd as _run

    nc = _bacc.Bacc("TRN2", target_bir_lowering=False, num_devices=1)
    arrays = layout(inputs)
    io = {}
    for name, a in arrays.items():
        io[name] = nc.dram_tensor(name + "_dram", a.shape, _mybir.dt.from_np(a.dtype), kind="ExternalInput").ap()
    io["out"] = nc.dram_tensor("out_dram", (16, 256, 128), F32, kind="ExternalOutput").ap()
    program(nc, io)
    r = _run(nc, [{name + "_dram": a for name, a in arrays.items()}], core_ids=[0])
    return r.results[0]["out_dram"]
```
